# Optimizing a Trainium2 kernel written in Bass

```python
import numpy as np
import jax
import jax.numpy as jnp

def _softmax(x, axis=-1):
    return jax.nn.softmax(x, axis=axis)

def _gelu(x):
    return jax.nn.gelu(x, approximate=True)

def _silu(x):
    return jax.nn.silu(x)

def _sigmoid(x):
    return jax.nn.sigmoid(x)

def _layernorm(x, axis=-1, eps=1e-05):
    m = jnp.mean(x, axis=axis, keepdims=True)
    v = jnp.var(x, axis=axis, keepdims=True)
    return (x - m) / jnp.sqrt(v + eps)

def _scatter_add(tgt, idx, src, axis=0):
    return tgt.at[idx].add(src)

def _segment_sum(src, seg, n):
    return jax.ops.segment_sum(src, seg, n)
kernel_name = 'mk_seq_preln_d2_jaxref_r8_1abd85'

def setup_inputs(seed: int=0):
    np.random.seed(seed)
    _w = jnp.asarray

    def _L0_attn_setup():
        import jax, jax.numpy as jnp
        import numpy as np
        N_HEAD = 16
        D_K = 64
        D_V = 64
        EMBED = 128
        BATCH = 4
        SEQ = 256
        key = jax.random.key(seed)
        ks = jax.random.split(key, 12)
        s = lambda d: 1.0 / np.sqrt(d)
        u = lambda k, shape, d: jax.random.uniform(k, shape, jnp.float32, -s(d), s(d))
        return {'z': jax.random.normal(ks[0], (BATCH, SEQ, EMBED), jnp.float32), 'wq': u(ks[1], (EMBED, D_K), D_K), 'wk': u(ks[2], (EMBED, D_K), D_K), 'wv': u(ks[3], (EMBED, D_V), D_V), 'fcq_w': u(ks[4], (D_K, N_HEAD * D_K), D_K), 'fcq_b': u(ks[5], (N_HEAD * D_K,), N_HEAD * D_K), 'fck_w': u(ks[6], (D_K, N_HEAD * D_K), D_K), 'fck_b': u(ks[7], (N_HEAD * D_K,), N_HEAD * D_K), 'fcv_w': u(ks[8], (D_V, N_HEAD * D_V), D_V), 'fcv_b': u(ks[9], (N_HEAD * D_V,), N_HEAD * D_V), 'fco_w': u(ks[10], (N_HEAD * D_V, EMBED), EMBED), 'fco_b': u(ks[11], (EMBED,), EMBED)}
    _L0_attn_in = _L0_attn_setup()

    def _L0_ffn_setup():
        import jax, jax.numpy as jnp
        import numpy as np
        E = 8
        H = 128
        D = 128
        TOP_K = 2
        key = jax.random.key(seed)
        k0, k1, k2, k3 = jax.random.split(key, 4)
        x = jax.random.normal(k0, (1, 256, H), dtype=jnp.float32)
        router_w = jax.random.normal(k1, (E, H), dtype=jnp.float32) * (1.0 / np.sqrt(H))
        up_proj = jax.random.normal(k2, (E, H, 2 * D), dtype=jnp.float32) * (1.0 / np.sqrt(H))
        down_proj = jax.random.normal(k3, (E, D, H), dtype=jnp.float32) * (1.0 / np.sqrt(D))
        return {'x': x, 'router_w': router_w, 'up_proj': up_proj, 'down_proj': down_proj}
    _L0_ffn_in = _L0_ffn_setup()

    def _L1_attn_setup():
        import jax, jax.numpy as jnp
        import numpy as np
        import math
        D_MODEL, D_C, D_R, NH = (128, 128, 32, 16)
        HD = D_MODEL // NH
        B, T = (2, 256)

        def _rope_tables(T, d_R):
            inv_freq = 1.0 / 10000.0 ** (jnp.arange(0, d_R, 2, dtype=jnp.float32) / d_R)
            t = jnp.arange(T, dtype=jnp.float32)
            freqs = jnp.outer(t, inv_freq)
            return (jnp.cos(freqs), jnp.sin(freqs))

        def _rotary_apply(x, cos, sin):
            d = x.shape[-1]
            x1, x2 = (x[..., :d // 2], x[..., d // 2:])
            return jnp.concatenate([x1 * cos - x2 * sin, x2 * cos + x1 * sin], axis=-1)
        key = jax.random.key(seed)
        ks = jax.random.split(key, 8)
        s = lambda fan_in: 1.0 / math.sqrt(fan_in)
        return {'x': jax.random.normal(ks[0], (B, T, D_MODEL), jnp.float32), 'W_kv_down': jax.random.normal(ks[1], (D_MODEL, D_C), jnp.float32) * s(D_MODEL), 'W_k_up': jax.random.normal(ks[2], (D_C, D_MODEL), jnp.float32) * s(D_C), 'W_v_up': jax.random.normal(ks[3], (D_C, D_MODEL), jnp.float32) * s(D_C), 'W_q': jax.random.normal(ks[4], (D_MODEL, D_MODEL), jnp.float32) * s(D_MODEL), 'W_q_rope': jax.random.normal(ks[5], (D_MODEL, D_R), jnp.float32) * s(D_MODEL), 'W_k_rope': jax.random.normal(ks[6], (D_C, D_R), jnp.float32) * s(D_C), 'W_o': jax.random.normal(ks[7], (D_MODEL, D_MODEL), jnp.float32) * s(D_MODEL)}
    _L1_attn_in = _L1_attn_setup()

    def _L1_ffn_setup():
        import jax, jax.numpy as jnp
        import numpy as np
        B, T, C = (2, 64, 128)
        I = 512
        E = 8
        K = 2
        key = jax.random.key(seed)
        ks = jax.random.split(key, 8)
        s = 0.02
        return {'x': jax.random.normal(ks[0], (B, T, C), jnp.float32), 'Wr1': jax.random.normal(ks[1], (C, C // 4), jnp.float32) * s, 'br1': jnp.zeros((C // 4,), jnp.float32), 'Wr2': jax.random.normal(ks[2], (C // 4, E), jnp.float32) * s, 'br2': jnp.zeros((E,), jnp.float32), 'Ws1': jax.random.normal(ks[3], (C, I), jnp.float32) * s, 'bs1': jnp.zeros((I,), jnp.float32), 'Ws2': jax.random.normal(ks[4], (I, C), jnp.float32) * s, 'bs2': jnp.zeros((C,), jnp.float32), 'We1': jax.random.normal(ks[5], (E, C, I), jnp.float32) * s, 'be1': jnp.zeros((E, I), jnp.float32), 'We2': jax.random.normal(ks[6], (E, I, C), jnp.float32) * s, 'be2': jnp.zeros((E, C), jnp.float32)}
    _L1_ffn_in = _L1_ffn_setup()
    _d = {'L0_attn_z': _L0_attn_in['z'], 'L0_attn_wq': _L0_attn_in['wq'], 'L0_attn_wk': _L0_attn_in['wk'], 'L0_attn_wv': _L0_attn_in['wv'], 'L0_attn_fcq_w': _L0_attn_in['fcq_w'], 'L0_attn_fcq_b': _L0_attn_in['fcq_b'], 'L0_attn_fck_w': _L0_attn_in['fck_w'], 'L0_attn_fck_b': _L0_attn_in['fck_b'], 'L0_attn_fcv_w': _L0_attn_in['fcv_w'], 'L0_attn_fcv_b': _L0_attn_in['fcv_b'], 'L0_attn_fco_w': _L0_attn_in['fco_w'], 'L0_attn_fco_b': _L0_attn_in['fco_b'], 'L0_ffn_router_w': _L0_ffn_in['router_w'], 'L0_ffn_up_proj': _L0_ffn_in['up_proj'], 'L0_ffn_down_proj': _L0_ffn_in['down_proj'], 'L1_attn_W_kv_down': _L1_attn_in['W_kv_down'], 'L1_attn_W_k_up': _L1_attn_in['W_k_up'], 'L1_attn_W_v_up': _L1_attn_in['W_v_up'], 'L1_attn_W_q': _L1_attn_in['W_q'], 'L1_attn_W_q_rope': _L1_attn_in['W_q_rope'], 'L1_attn_W_k_rope': _L1_attn_in['W_k_rope'], 'L1_attn_W_o': _L1_attn_in['W_o'], 'L1_ffn_Wr1': _L1_ffn_in['Wr1'], 'L1_ffn_br1': _L1_ffn_in['br1'], 'L1_ffn_Wr2': _L1_ffn_in['Wr2'], 'L1_ffn_br2': _L1_ffn_in['br2'], 'L1_ffn_Ws1': _L1_ffn_in['Ws1'], 'L1_ffn_bs1': _L1_ffn_in['bs1'], 'L1_ffn_Ws2': _L1_ffn_in['Ws2'], 'L1_ffn_bs2': _L1_ffn_in['bs2'], 'L1_ffn_We1': _L1_ffn_in['We1'], 'L1_ffn_be1': _L1_ffn_in['be1'], 'L1_ffn_We2': _L1_ffn_in['We2'], 'L1_ffn_be2': _L1_ffn_in['be2']}
    _x0 = _d['L0_attn_z']
    _d['L0_attn_z'] = jax.random.normal(jax.random.fold_in(jax.random.key(seed), 1), (2, 1024, 128), dtype=_x0.dtype)
    del _x0
    return _d

def reference(L0_attn_z, L0_attn_wq, L0_attn_wk, L0_attn_wv, L0_attn_fcq_w, L0_attn_fcq_b, L0_attn_fck_w, L0_attn_fck_b, L0_attn_fcv_w, L0_attn_fcv_b, L0_attn_fco_w, L0_attn_fco_b, L0_ffn_router_w, L0_ffn_up_proj, L0_ffn_down_proj, L1_attn_W_kv_down, L1_attn_W_k_up, L1_attn_W_v_up, L1_attn_W_q, L1_attn_W_q_rope, L1_attn_W_k_rope, L1_attn_W_o, L1_ffn_Wr1, L1_ffn_br1, L1_ffn_Wr2, L1_ffn_br2, L1_ffn_Ws1, L1_ffn_bs1, L1_ffn_Ws2, L1_ffn_bs2, L1_ffn_We1, L1_ffn_be1, L1_ffn_We2, L1_ffn_be2):

    def _L0_attn_ref(z, wq, wk, wv, fcq_w, fcq_b, fck_w, fck_b, fcv_w, fcv_b, fco_w, fco_b):
        import jax, jax.numpy as jnp
        import numpy as np
        N_HEAD = 16
        D_K = 64
        D_V = 64
        EMBED = 128
        BATCH = 4
        SEQ = 256
        b, n, _ = z.shape
        scale = jnp.sqrt(jnp.float32(D_K))
        q = z @ wq @ fcq_w + fcq_b
        k = z @ wk @ fck_w + fck_b
        v = z @ wv @ fcv_w + fcv_b
        q = q.reshape(b, n, N_HEAD, D_K)
        k = k.reshape(b, n, N_HEAD, D_K)
        v = v.reshape(b, n, N_HEAD, D_V)
        scores = jnp.einsum('bihd,bjhd->bhij', q, k) / scale
        attn = jax.nn.softmax(scores, axis=-1)
        out = jnp.einsum('bhij,bjhd->bihd', attn, v)
        out = out.reshape(b, n, N_HEAD * D_V)
        return out @ fco_w + fco_b

    def _L0_ffn_ref(x, router_w, up_proj, down_proj):
        import jax, jax.numpy as jnp
        import numpy as np
        E = 8
        H = 128
        D = 128
        TOP_K = 2
        B, T, _ = x.shape
        xt = x.reshape(-1, H)
        N = xt.shape[0]
        logits = jnp.einsum('nh,eh->ne', xt, router_w)
        probs = jax.nn.softmax(logits, axis=-1)
        scores, expert_idx = jax.lax.top_k(probs, TOP_K)
        scores = scores / jnp.sum(scores, axis=-1, keepdims=True)
        gate = jnp.zeros((N, E), dtype=xt.dtype).at[jnp.arange(N)[:, None], expert_idx].add(scores)
        h = jnp.einsum('nh,ehd->end', xt, up_proj)
        hidden = jax.nn.silu(h[..., :D]) * h[..., D:]
        out_e = jnp.einsum('end,edh->enh', hidden, down_proj)
        out = jnp.einsum('ne,enh->nh', gate, out_e)
        return out.reshape(B, T, H)

    def _L1_attn_ref(x, W_kv_down, W_k_up, W_v_up, W_q, W_q_rope, W_k_rope, W_o):
        import jax, jax.numpy as jnp
        import numpy as np
        import math
        D_MODEL, D_C, D_R, NH = (128, 128, 32, 16)
        HD = D_MODEL // NH
        B, T = (2, 256)

        def _rope_tables(T, d_R):
            inv_freq = 1.0 / 10000.0 ** (jnp.arange(0, d_R, 2, dtype=jnp.float32) / d_R)
            t = jnp.arange(T, dtype=jnp.float32)
            freqs = jnp.outer(t, inv_freq)
            return (jnp.cos(freqs), jnp.sin(freqs))

        def _rotary_apply(x, cos, sin):
            d = x.shape[-1]
            x1, x2 = (x[..., :d // 2], x[..., d // 2:])
            return jnp.concatenate([x1 * cos - x2 * sin, x2 * cos + x1 * sin], axis=-1)
        Bb, Tt, _ = x.shape
        cos, sin = _rope_tables(Tt, D_R)
        cos = cos[None]
        sin = sin[None]
        c_kv = x @ W_kv_down
        k_rope = _rotary_apply(c_kv @ W_k_rope, cos, sin)
        k = (c_kv @ W_k_up).reshape(Bb, Tt, NH, HD)
        v = (c_kv @ W_v_up).reshape(Bb, Tt, NH, HD)
        q = (x @ W_q).reshape(Bb, Tt, NH, HD)
        q_rope = _rotary_apply(x @ W_q_rope, cos, sin)
        scale = math.sqrt(HD + D_R)
        scores = jnp.einsum('bqhd,bkhd->bhqk', q, k)
        scores = scores + jnp.einsum('bqr,bkr->bqk', q_rope, k_rope)[:, None]
        scores = scores / scale
        causal = jnp.triu(jnp.ones((Tt, Tt), dtype=bool), k=1)
        scores = jnp.where(causal[None, None], -jnp.inf, scores)
        w = jax.nn.softmax(scores, axis=-1)
        attn = jnp.einsum('bhqk,bkhd->bqhd', w, v).reshape(Bb, Tt, D_MODEL)
        return attn @ W_o

    def _L1_ffn_ref(x, Wr1, br1, Wr2, br2, Ws1, bs1, Ws2, bs2, We1, be1, We2, be2):
        import jax, jax.numpy as jnp
        import numpy as np
        B, T, C = (2, 64, 128)
        I = 512
        E = 8
        K = 2
        Bb, Tt, Cc = x.shape
        xf = x.reshape(-1, Cc)
        logits = jax.nn.relu(xf @ Wr1 + br1) @ Wr2 + br2
        gates = jax.nn.softmax(logits, axis=-1)
        tg, ti = jax.lax.top_k(gates, K)
        tg = jax.nn.softmax(tg / K, axis=-1)
        out = jax.nn.silu(xf @ Ws1 + bs1) @ Ws2 + bs2
        for e in range(E):
            h = jax.nn.silu(xf @ We1[e] + be1[e]) @ We2[e] + be2[e]
            w = jnp.sum(tg * (ti == e), axis=-1)
            out = out + w[:, None] * h
        return out.reshape(Bb, Tt, Cc)
    x = L0_attn_z
    x = x + _L0_attn_ref(_layernorm(x, axis=-1), L0_attn_wq, L0_attn_wk, L0_attn_wv, L0_attn_fcq_w, L0_attn_fcq_b, L0_attn_fck_w, L0_attn_fck_b, L0_attn_fcv_w, L0_attn_fcv_b, L0_attn_fco_w, L0_attn_fco_b)
    x = x + _L0_ffn_ref(_layernorm(x, axis=-1), L0_ffn_router_w, L0_ffn_up_proj, L0_ffn_down_proj)
    x = x + _L1_attn_ref(_layernorm(x, axis=-1), L1_attn_W_kv_down, L1_attn_W_k_up, L1_attn_W_v_up, L1_attn_W_q, L1_attn_W_q_rope, L1_attn_W_k_rope, L1_attn_W_o)
    x = x + _L1_ffn_ref(_layernorm(x, axis=-1), L1_ffn_Wr1, L1_ffn_br1, L1_ffn_Wr2, L1_ffn_br2, L1_ffn_Ws1, L1_ffn_bs1, L1_ffn_Ws2, L1_ffn_bs2, L1_ffn_We1, L1_ffn_be1, L1_ffn_We2, L1_ffn_be2)
    return x

_drawn_inputs = setup_inputs


def setup_inputs(seed=0):
    import zlib

    import numpy as np

    out = dict(_drawn_inputs(seed))
    spreads = {'L1_ffn_br1': (0.0, 0.352),
     'L1_ffn_br2': (0.0, 0.1),
     'L1_ffn_bs1': (0.0, 0.442),
     'L1_ffn_bs2': (0.0, 0.1),
     'L1_ffn_be1': (0.0, 0.572),
     'L1_ffn_be2': (0.0, 0.1)}
    factors = {'L0_attn_fcq_b': 27.567, 'L0_attn_fck_b': 64.0}
    for name, (base, spread) in spreads.items():
        noise = np.random.default_rng([zlib.crc32(name.encode()), seed]).standard_normal(out[name].shape)
        drawn = base * np.exp(spread * noise) if base else spread * noise
        out[name] = jnp.asarray(drawn.astype(out[name].dtype))
    for name, factor in factors.items():
        out[name] = (out[name] * factor).astype(out[name].dtype)
    return out
```

```python
import numpy as np
from contextlib import ExitStack
import concourse.bass as bass
from concourse import mybir

F32 = mybir.dt.float32
F32R = mybir.dt.float32r
U32 = mybir.dt.uint32
ACT = mybir.ActivationFunctionType
ALU = mybir.AluOpType
AX = mybir.AxisListType
ds, ts = bass.ds, bass.ts

P = 128
E = 128
B, T = 2, 1024
N = B * T
NT = N // P
TT = T // P
BLK = 512
NBLK = N // BLK
TPB = BLK // P
EPS = 1e-5

NEXP, TOPK = 8, 2

H0, D0 = 16, 64
PAIRS = H0 // 2
STEPS0 = B * PAIRS

H1, D1, DR = 16, 8, 32
QUADS = H1 // 4
STEPS1 = B * QUADS
SCALE1 = float(D1 + DR) ** -0.5
MASKED = -1e30

HID1 = 512
CH = HID1 // P


class Mem:
    pass


def layernorm_block(nc, v, m, j, x_block, base):
    for t in range(TPB):
        ins = nc.vector.bn_stats(m.stats[:, t, :], x_block(t))
    ins.then_inc(m.ln_step, 1)
    v.wait_ge(m.ln_step, base + 1)
    for t in range(TPB):
        ins = nc.vector.bn_aggr(m.mv[:, t, :], m.stats[:, t, :])
    ins.then_inc(m.ln_step, 1)
    v.wait_ge(m.ln_step, base + 2)
    v.wait_ge(m.std_ready, j + 1)
    nc.vector.reciprocal(m.rstd[:, :], m.std[:, :]).then_inc(m.ln_step, 1)
    v.wait_ge(m.ln_step, base + 3)


def deviation_block(nc, act, m, j):
    act.wait_ge(m.ln_step, 3 * j + 2)
    nc.scalar.activation(m.std[:, :], m.mv[:, :, 1], ACT.Sqrt, bias=m.eps[:, 0:1]).then_inc(m.std_ready, 1)


def normalise_block(nc, m, x_block):
    for t in range(TPB):
        ins = nc.vector.tensor_scalar(m.xn[:, t, :], x_block(t), m.mv[:, t, 0:1], m.rstd[:, t:t + 1],
                                      ALU.subtract, ALU.mult)
    return ins


def l0_prologue(nc, m, d):
    with ExitStack() as ctx:
        def sb(name, shape, dt=F32):
            return ctx.enter_context(nc.sbuf_tensor(name, shape, dt))

        def pb(name, shape):
            return ctx.enter_context(nc.psum_tensor(name, shape, F32))

        wl = sb("wl", [P, 5 * D0])
        fq = sb("fq", [P, H0, D0])
        fk = sb("fk", [P, H0, D0])
        fv_t = sb("fv_t", [D0, H0, D0])
        fo = sb("fo", [D0, H0, E])
        bv = sb("bv", [D0, H0])
        bo = sb("bo", [P, 1])
        m.stats = sb("stats0", [P, TPB, 6])
        m.mv = sb("mv0", [P, TPB, 2])
        m.rstd = sb("rstd0", [P, TPB])
        m.std = sb("std0", [P, TPB])
        m.xn = sb("xn0", [P, TPB, E])
        xt = sb("xt0", [P, BLK])
        tr = pb("tr0", [P, BLK])
        lat = [pb(f"lat{i}", [P, BLK]) for i in range(2)]
        vlat = pb("vlat", [P, TPB, P])
        gp = pb("gp", [P, PAIRS, E])
        cp = pb("cp", [P, 1])

        def sem(name):
            return m.ctx.enter_context(nc.semaphore(name))

        x_in, w_in, const_in = sem("x_in"), sem("w_in"), sem("const_in")
        m.ln_step, m.std_ready = sem("ln_step0"), sem("std_ready0")
        eps_set = sem("eps_set")
        xn_ready, transposed, xt_ready = sem("xn_ready0"), sem("transposed0"), sem("xt_ready0")
        lat_filled, hi_done, lat_read = sem("lat_filled"), sem("lat_hi"), sem("lat_read")
        vlat_filled, vlat_read = sem("vlat_filled"), sem("vlat_read")
        g_filled, w_split = sem("g_filled"), sem("w_split")
        block = ctx.enter_context(nc.Block())

        @block.sync
        def _(sp):
            for j in range(NBLK):
                sp.dma_start(m.x[:, TPB * j:TPB * (j + 1), :],
                             d["x"][BLK * j:BLK * (j + 1), :].rearrange("(t p) e -> p t e", p=P)).then_inc(x_in, 16)
            sp.dma_start(m.ident[:, :], d["ident"]).then_inc(const_in, 16)
            sp.dma_start(wl[:, :], d["wl"]).then_inc(const_in, 16)
            for dst, src in ((fq, d["fq"]), (fk, d["fk"]), (fv_t, d["fv_t"]), (fo, d["fo"])):
                sp.dma_start(dst[:, :, :], src).then_inc(w_in, 16)
            for dst, src in ((bv, d["bv"]), (bo, d["bo"]), (m.qk_bias, d["qk_bias"])):
                sp.dma_start(dst[:, :], src).then_inc(w_in, 16)
            sp.wait_ge(w_in, 16 * 7)

        @block.vector
        def _(v):
            for j in range(NBLK):
                def x_block(t):
                    return m.x[:, TPB * j + t, :]

                v.wait_ge(x_in, 16 * NBLK)
                layernorm_block(nc, v, m, j, x_block, 3 * j)
                if j:
                    v.wait_ge(transposed, j)
                normalise_block(nc, m, x_block).then_inc(xn_ready, 1)
                for n, dst in enumerate((m.aq, m.ak)):
                    v.wait_ge(hi_done, 2 * j + n + 1)
                    nc.vector.tensor_tensor(dst[D0:P, ds(BLK * j, BLK)], lat[n][D0:P, :],
                                            dst[D0:P, ds(BLK * j, BLK)], ALU.subtract).then_inc(lat_read, 1)
            v.wait_ge(w_in, 16 * 7)
            for n, src in enumerate((fq, fk)):
                nc.vector.tensor_copy(m.w_all[:, :, 2 * n, :], src[:, :, :]).then_inc(w_split, 1)
                v.wait_ge(w_split, 2 * n + 1)
                nc.vector.tensor_tensor(m.w_all[:, :, 2 * n + 1, :], src[:, :, :], m.w_all[:, :, 2 * n, :],
                                        ALU.subtract).then_inc(w_split, 1)
            v.wait_ge(g_filled, 1)
            nc.vector.tensor_copy(m.g_all[:, :, :], gp[:, :, :])
            nc.vector.tensor_tensor(m.out_bias[:, :], cp[:, :], bo[:, :], ALU.add)

        @block.gpsimd
        def _(pool):
            nc.gpsimd.memset(m.eps[:, :], EPS).then_inc(eps_set, 1)

        @block.scalar
        def _(act):
            act.wait_ge(eps_set, 1)
            for j in range(NBLK):
                deviation_block(nc, act, m, j)
                act.wait_ge(transposed, j + 1)
                if j:
                    act.wait_ge(vlat_filled, j)
                nc.scalar.copy(xt[:, :], tr[:, :]).then_inc(xt_ready, 1)
                for n, dst in enumerate((m.aq, m.ak)):
                    act.wait_ge(lat_filled, 2 * j + n + 1)
                    nc.scalar.copy(dst[:, ds(BLK * j, BLK)], lat[n][:, :]).then_inc(hi_done, 1)
                act.wait_ge(vlat_filled, j + 1)
                nc.scalar.copy(m.c_all[:, ds(TPB * j, TPB), :], vlat[:, :, 0:D0]).then_inc(vlat_read, 1)

        @block.tensor
        def _(pe):
            pe.wait_ge(const_in, 32)
            for j in range(NBLK):
                pe.wait_ge(xn_ready, j + 1)
                if j:
                    pe.wait_ge(xt_ready, j)
                for t in range(TPB):
                    ins = nc.tensor.transpose(tr[:, ts(t, P)], m.xn[:, t, :], m.ident[:, :])
                ins.then_inc(transposed, 1)
                pe.wait_ge(xt_ready, j + 1)
                for n in range(2):
                    if j:
                        pe.wait_ge(lat_read, 2 * (j - 1) + n + 1)
                    nc.tensor.matmul(lat[n][:, :], wl[:, 2 * D0 * n:2 * D0 * (n + 1)], xt[:, :],
                                     start=True, stop=True).then_inc(lat_filled, 1)
                if j:
                    pe.wait_ge(vlat_read, j)
                for t in range(TPB):
                    ins = nc.tensor.matmul(vlat[:, t, 0:D0], xt[:, ts(t, P)], wl[:, 4 * D0:5 * D0],
                                           start=True, stop=True)
                ins.then_inc(vlat_filled, 1)
            pe.wait_ge(w_in, 16 * 7)
            for h in range(H0):
                lo = D0 * (h % 2)
                nc.tensor.matmul(gp[lo:lo + D0, h // 2, :], fv_t[:, h, :], fo[:, h, :], start=True, stop=True)
            for h in range(H0):
                ins = nc.tensor.matmul(cp[:, :], fo[:, h, :], bv[:, h:h + 1], start=(h == 0), stop=(h == H0 - 1))
            ins.then_inc(g_filled, 1)


NEXT_UNITS = ([("q", 0, 0), ("q", 0, 1), ("k", 0, 0), ("k", 0, 1)]
              + [("s", 0, u) for u in range(2 * TT)]
              + [("q", 1, 0), ("q", 1, 1), ("m", 0, 0), ("k", 1, 0), ("k", 1, 1)]
              + [("s", 1, u) for u in range(2 * TT)] + [("m", 1, 0)])
N_NEXT = len(NEXT_UNITS)
L_AT, NORM_AT, G_AT = 8, 30, 31
WITH_FINISH = (NEXT_UNITS[:L_AT] + [("l", 0, 0)] + NEXT_UNITS[L_AT:NORM_AT] + [("n", 0, 0), ("g", 0, 0)]
               + NEXT_UNITS[NORM_AT:NORM_AT + 1] + [("g", 0, 1)] + NEXT_UNITS[NORM_AT + 1:])
FINISH_ONLY = [("l", 0, 0), ("n", 0, 0), ("g", 0, 0), ("g", 0, 1)]
SLOTS = 6
N_STEP = N_NEXT + 3


def script(units):
    left = list(units)
    out, at = [], 0
    for kt in range(TT):
        after = {0: 1, 1: 2, 2: 3}
        parts = [("ST", kt, 0), ("ST", kt, 1)] + ([("PV", kt - 1, 0)] if kt else [])
        for n in range(3):
            if n < len(parts):
                out.append(parts[n])
            for _ in range(after[n]):
                if left:
                    unit = left.pop(0)
                    out.append(("UNIT",) + unit)
                    if unit[0] == "n" and left:
                        out.append(("UNIT",) + left.pop(0))
    out.append(("PV", TT - 1, 0))
    out += [("UNIT",) + u for u in left]
    return out


def units_before(n):
    return N_NEXT if isinstance(n, int) and n == 0 else 2 * N_NEXT + N_STEP * (n - 1)


def l0_attention(nc, m, d):
    with ExitStack() as ctx:
        def sb(name, shape, dt=F32):
            return ctx.enter_context(nc.sbuf_tensor(name, shape, dt))

        def sem(name):
            return m.ctx.enter_context(nc.semaphore(name))

        R2 = range(2)
        kk = [[sb(f"kk{a}{h}", [P, T], F32R) for h in R2] for a in R2]
        k2 = [[sb(f"k2_{a}{h}", [P, T], F32R) for h in R2] for a in R2]
        qq = [[sb(f"qq{a}{h}", [P, T], F32R) for h in R2] for a in R2]
        q2 = [[sb(f"q2_{a}{h}", [P, T], F32R) for h in R2] for a in R2]
        w = [sb(f"w{a}", [P, 2, 4, 2, D0], F32R) for a in R2]
        bias = [sb(f"bias{a}", [P, 4]) for a in R2]
        c = [sb(f"c{a}", [P, TT, D0]) for a in R2]
        g = sb("g", [P, E])
        prob = [sb(f"prob{s}", [P, 2, T]) for s in range(4)]
        psum_k = sb("psum_k", [P, 2, T])
        ut = sb("ut", [P, T])
        rsum = sb("rsum", [P, BLK])
        rb = sb("rb", [P, T])
        on = sb("on", [P, T])
        ones = sb("ones", [P, 32])
        mx = sb("mx", [P, 2, TT, 2])
        mmax = sb("mmax", [P, 2, TT])
        negm = sb("negm", [P, 2, TT])
        mrow = [sb(f"mrow{h}", [TT, P], F32R) for h in R2]
        st = [ctx.enter_context(nc.psum_tensor(f"st{h}", [P, T], F32)) for h in R2]
        pv = ctx.enter_context(nc.psum_tensor("pv", [P, T], F32))
        work = [ctx.enter_context(nc.psum_tensor(f"work{h}", [P, BLK], F32)) for h in R2]

        cleared = sem("cleared")
        w_loaded, c_loaded = [sem(f"w_loaded{a}") for a in R2], [sem(f"c_loaded{a}") for a in R2]
        row_loaded = [sem(f"row_loaded{h}") for h in R2]
        g_loaded, r_stored, r_loaded = sem("g_loaded"), sem("r_stored"), sem("r_loaded")
        filled, read = sem("work_filled"), sem("work_read")
        hi_done, negm_ready, mmax_ready = sem("hi_done"), sem("negm_ready"), sem("mmax_ready")
        st_filled, exp_done, pv_done, ut_ready = sem("st_filled"), sem("exp_done"), sem("pv_done"), sem("ut_ready")
        summed, norm_done = sem("summed"), sem("norm_done")
        block = ctx.enter_context(nc.Block())

        def steps(eng, step):
            step(0, 0, True, False)
            with eng.Fori(0, (STEPS0 - 2) // 2) as i:
                step(2 * i + 1, 1, False, False)
                step(2 * i + 2, 0, False, False)
            step(STEPS0 - 1, 1, False, True)

        def units_of(first, last):
            return NEXT_UNITS if first else FINISH_ONLY if last else WITH_FINISH

        def psum_unit(n, par, first, seen):
            even = 0 if first else (1 + par) % 2
            return units_before(n) + seen, work[(even + seen) % 2]

        def load_pair(sp, k, par):
            for copy in R2:
                sp.dma_start(w[par][:, :, :, copy, :].bitcast(F32),
                             m.w_all[:, ds(2 * (k % PAIRS), 2), :, :].bitcast(F32)).then_inc(w_loaded[par], 16)
            sp.dma_start(bias[par][:, :], m.qk_bias[:, ds(4 * (k % PAIRS), 4)]).then_inc(w_loaded[par], 16)

        def load_values(sp, k, par):
            sp.dma_start(c[par][:, :, :], m.c_all[:, ds(TT * (k // PAIRS), TT), :]).then_inc(c_loaded[par], 16)

        def sp_rows(sp, k, par, hh, u):
            sp.wait_ge(read, u + 1)
            sp.dma_start(q2[par][hh][0:1, :].bitcast(F32), mrow[hh][:, :].bitcast(F32)).then_inc(row_loaded[hh], 16)

        def sp_sums(sp, k, u):
            sp.wait_ge(read, u + 1)
            sp.dma_start(d["sums"], rsum[0:P:32, :]).then_inc(r_stored, 16)
            sp.wait_ge(r_stored, 16 * (k + 1))
            if not (isinstance(k, int) and k == 0):
                sp.wait_ge(norm_done, k)
            for hh in R2:
                sp.dma_start(rb[D0 * hh:D0 * (hh + 1), :],
                             d["sums"][2 * hh:2 * hh + 2, :].rearrange("a n -> (a n)").partition_broadcast(D0)
                             ).then_inc(r_loaded, 16)

        @block.sync
        def _(sp):
            load_pair(sp, 0, 0)
            load_values(sp, 0, 0)
            load_pair(sp, 1, 1)

            def rows_of(k, par, units, base):
                seen = 0
                for kind, hh, j in units:
                    if kind == "m":
                        sp_rows(sp, k, par, hh, base + seen)
                    seen += kind != "n"

            sp.wait_ge(cleared, 2)
            rows_of(0, 0, NEXT_UNITS, 0)

            def step(n, par, first, last):
                base = units_before(n)
                if not last:
                    sp.wait_ge(read, base)
                    load_pair(sp, n + 2, par)
                    if not first:
                        sp.wait_ge(pv_done, TT * n)
                    load_values(sp, n + 1, 1 - par)
                if not first:
                    if last:
                        sp.wait_ge(read, base)
                    sp.dma_start(g[:, :], m.g_all[:, (n - 1) % PAIRS, :]).then_inc(g_loaded, 16)
                    sp_sums(sp, n - 1, base + (0 if last else L_AT))
                if not last:
                    rows_of(n + 1, 1 - par, units_of(first, last), base)

            steps(sp, step)
            sp.wait_ge(read, units_before(STEPS0 - 1) + 3)
            sp.dma_start(g[:, :], m.g_all[:, PAIRS - 1, :]).then_inc(g_loaded, 16)
            sp_sums(sp, STEPS0 - 1, units_before(STEPS0 - 1) + 3)
            for a in R2:
                sp.wait_ge(w_loaded[a], 48 * (STEPS0 // 2) + 48 * (a == 0))
                sp.wait_ge(c_loaded[a], 16 * (STEPS0 // 2))
            sp.wait_ge(r_loaded, 32 * STEPS0)

        @block.gpsimd
        def _(pool):
            for a in R2:
                for h in R2:
                    nc.gpsimd.memset(k2[a][h][0:D0, :].bitcast(F32), 0.0)
                    ins = nc.gpsimd.memset(q2[a][h][0:D0, :].bitcast(F32), 0.0)
            ins.then_inc(cleared, 1)
            pool.wait_ge(cleared, 1)
            for a in R2:
                for h in R2:
                    ins = nc.gpsimd.memset(k2[a][h][0:1, :].bitcast(F32), 1.0)
            nc.gpsimd.memset(ones[:, :], 1.0)
            nc.gpsimd.memset(m.out_t[:, :], 0.0).then_inc(cleared, 1)

            def step(n, par, first, last):
                per = 2 * (TT - 1)
                for kt in range(1, TT):
                    for hh in R2:
                        pool.wait_ge(exp_done, 2 * TT * n + 2 * kt + hh + 1)
                        if kt == 1 and hh == 0 and not first:
                            pool.wait_ge(filled, units_before(n) + (0 if last else L_AT) + 1)
                        if kt == 1:
                            nc.gpsimd.tensor_tensor(psum_k[:, hh, :], prob[0][:, hh, :], prob[1][:, hh, :],
                                                    ALU.add).then_inc(summed, 1)
                        else:
                            pool.wait_ge(summed, per * n + 2 * (kt - 1) + hh - 1)
                            nc.gpsimd.tensor_tensor(psum_k[:, hh, :], psum_k[:, hh, :], prob[kt % 4][:, hh, :],
                                                    ALU.add).then_inc(summed, 1)

            steps(pool, step)

        @block.scalar
        def _(act):
            def proj_evac(kind, j, buf, par, hh):
                b = bias[par][:, 2 * hh + (kind == "k"):2 * hh + (kind == "k") + 1]
                cols = ts(j, BLK)
                if kind == "q":
                    nc.scalar.activation(qq[par][hh][:, cols], buf[:, :], ACT.Identity, bias=b
                                         ).then_inc(hi_done, 1)
                else:
                    nc.scalar.activation(kk[par][hh][0:D0, cols], buf[0:D0, :], ACT.Identity, bias=b[0:D0, :])
                    nc.scalar.activation(k2[par][hh][D0:P, cols], buf[D0:P, :], ACT.Identity, bias=b[D0:P, :]
                                         ).then_inc(hi_done, 1)

            def run(n, par, first, last, todo, base, even):
                seen = 0
                for what, kind, hh, *j in [t + (0,) * (4 - len(t)) for t in todo]:
                    if what == "UNIT":
                        if kind in "qk":
                            act.wait_ge(filled, base + seen + 1)
                            proj_evac(kind, j[0], work[(even + seen) % 2], 1 - par, hh)
                        seen += kind != "n"
                    elif what == "ST":
                        kt = kind
                        at = 2 * TT * n + 2 * kt + hh
                        act.wait_ge(st_filled, at + 1)
                        if not (first and kt < 4):
                            act.wait_ge(pv_done, TT * n + kt - 3)
                            if kt >= 4:
                                act.wait_ge(summed, 14 * n + 2 * max(kt - 4, 1) )
                            else:
                                act.wait_ge(summed, 14 * (n - 1) + 2 * (kt + 4))
                        nc.scalar.activation(prob[kt % 4][:, hh, :], st[hh][:, :], ACT.Exp, scale=D0 ** -0.5
                                             ).then_inc(exp_done, 1)

            act.wait_ge(w_loaded[0], 48)
            run(-1, 1, True, False, [("UNIT",) + u for u in NEXT_UNITS], 0, 0)

            def step(n, par, first, last):
                if not last:
                    act.wait_ge(w_loaded[1 - par], 48 * ((n + 1) // 2 + 1))
                run(n, par, first, last, script(units_of(first, last)), units_before(n),
                    0 if first else (1 + par) % 2)
                act.wait_ge(pv_done, TT * (n + 1))
                if not first:
                    act.wait_ge(norm_done, n)
                nc.scalar.copy(ut[:, :], pv[:, :]).then_inc(ut_ready, 1)

            steps(act, step)

        @block.vector
        def _(v):
            def unit(kind, hh, j, u, buf, par, k):
                cols = ts(j, BLK)
                if kind in "qk":
                    dst, hi = (q2, qq) if kind == "q" else (kk, k2)
                    b = bias[par][D0:P, 2 * hh + (kind == "k"):2 * hh + (kind == "k") + 1]
                    v.wait_ge(hi_done, 8 * k + 4 * hh + 2 * (kind == "k") + j + 1)
                    nc.vector.scalar_tensor_tensor(dst[par][hh][D0:P, cols], buf[D0:P, :], b,
                                                   hi[par][hh][D0:P, cols], ALU.add, ALU.subtract
                                                   ).then_inc(read, 1)
                elif kind == "s":
                    v.wait_ge(filled, u + 1)
                    nc.vector.reduce_max(mx[:, hh, j // 2, j % 2:j % 2 + 1], buf[:, :], AX.X).then_inc(read, 1)
                elif kind == "m":
                    if not (isinstance(k, int) and k == 0):
                        v.wait_ge(row_loaded[hh], 16 * k)
                    v.wait_ge(filled, u + 1)
                    nc.vector.tensor_copy(mrow[hh][:, :], buf[0:TT, 0:P]).then_inc(read, 1)
                elif kind == "l":
                    if not (isinstance(k, int) and k == 0):
                        v.wait_ge(r_stored, 16 * k)
                    v.wait_ge(filled, u + 1)
                    nc.vector.reciprocal(rsum[:, :], buf[:, :]).then_inc(read, 1)
                elif kind == "g":
                    v.wait_ge(filled, u + 1)
                    out = m.out_t[:, ds(T * (k // PAIRS) + BLK * j, BLK)]
                    nc.vector.tensor_tensor(out, buf[:, :], out, ALU.add).then_inc(read, 1)

            def combine(hh, k, u_last):
                v.wait_ge(read, u_last + 1)
                nc.vector.tensor_tensor(mmax[:, hh, :], mx[:, hh, :, 0], mx[:, hh, :, 1], ALU.max
                                        ).then_inc(mmax_ready, 1)
                v.wait_ge(mmax_ready, 2 * k + hh + 1)
                nc.vector.tensor_scalar(negm[:, hh, :], mmax[:, hh, :], -1.0, None, ALU.mult
                                        ).then_inc(negm_ready, 1)

            def normalise(k):
                v.wait_ge(r_loaded, 32 * (k + 1))
                v.wait_ge(ut_ready, k + 1)
                nc.vector.tensor_tensor(on[:, :], ut[:, :], rb[:, :], ALU.mult).then_inc(norm_done, 1)

            def run(n, par, units, base, even):
                seen = 0
                for kind, hh, j in units:
                    k = n - 1 if kind in "lng" else n + 1
                    if kind == "n":
                        normalise(k)
                        continue
                    unit(kind, hh, j, base + seen, work[(even + seen) % 2], 1 - par, k)
                    if kind == "s" and j == 2 * TT - 1:
                        combine(hh, k, base + seen)
                    seen += 1

            v.wait_ge(cleared, 2)
            run(-1, 1, NEXT_UNITS, 0, 0)

            def step(n, par, first, last):
                run(n, par, units_of(first, last), units_before(n), 0 if first else (1 + par) % 2)

            steps(v, step)
            run(STEPS0, 0, FINISH_ONLY, units_before(STEPS0 - 1) + 3, 1)

        @block.tensor
        def _(pe):
            def unit(kind, hh, j, u, seen, buf, par, k, ready):
                if not (isinstance(u, int) and u < 2):
                    pe.wait_ge(read, u - 1)
                if kind in "qk":
                    src, part = (m.aq, 0) if kind == "q" else (m.ak, 2)
                    cols = ds(T * (k // PAIRS) + BLK * j, BLK)
                    nc.tensor.matmul(buf[:, :], w[par][:, hh, part, :, :].rearrange("p a d -> p (a d)"), src[:, cols],
                                     start=True, stop=False)
                    ins = nc.tensor.matmul(buf[:, :], w[par][:, hh, part + 1, :, :].rearrange("p a d -> p (a d)"), src[:, cols],
                                           start=False, stop=True)
                elif kind == "s":
                    if j == 0:
                        pe.wait_ge(read, u)
                    ins = nc.tensor.matmul(buf[:, :], qq[par][hh][:, ts(j // 2, P)], kk[par][hh][:, ts(j % 2, BLK)],
                                           start=True, stop=True)
                elif kind == "m":
                    pe.wait_ge(negm_ready, 2 * k + hh + 1)
                    ins = nc.tensor.matmul(buf[0:TT, 0:P], negm[:, hh, :], m.ident[:, :], start=True, stop=True)
                elif kind == "l":
                    pe.wait_ge(summed, 14 * (k + 1))
                    for q in range(4):
                        ins = nc.tensor.matmul(buf[32 * q:32 * (q + 1), :], ones[:, :],
                                               psum_k[:, q // 2, ts(q % 2, BLK)], start=True, stop=True)
                elif kind == "g":
                    pe.wait_ge(norm_done, k + 1)
                    pe.wait_ge(g_loaded, 16 * (k + 1))
                    ins = nc.tensor.matmul(buf[:, :], g[:, :], on[:, ts(j, BLK)], start=True, stop=True)
                ins.then_inc(filled, 1)

            def run(n, par, todo, base, even, first):
                seen = 0
                for what, *rest in todo:
                    if what == "UNIT":
                        kind, hh, j = rest
                        if kind != "n":
                            unit(kind, hh, j, base + seen, seen, work[(even + seen) % 2], 1 - par,
                                 n - 1 if kind in "lg" else n + 1, None)
                            seen += 1
                    elif what == "ST":
                        kt, hh = rest
                        at = 2 * TT * n + 2 * kt + hh
                        if not (first and kt == 0):
                            pe.wait_ge(exp_done, at - 1)
                        if kt == 0:
                            pe.wait_ge(row_loaded[hh], 16 * (n + 1))
                        for part, (ka, qa) in enumerate(((kk, qq), (k2, q2))):
                            for j in range(2):
                                ins = nc.tensor.matmul(st[hh][:, ts(j, BLK)], ka[par][hh][:, ts(kt, P)],
                                                       qa[par][hh][:, ts(j, BLK)],
                                                       start=(part == 0), stop=(part == 1))
                        ins.then_inc(st_filled, 1)
                    else:
                        kt = rest[0]
                        pe.wait_ge(exp_done, 2 * TT * n + 2 * kt + 2)
                        if kt == 0:
                            pe.wait_ge(c_loaded[par], 16 * (n // 2 + 1))
                            if not first:
                                pe.wait_ge(ut_ready, n)
                        for j in range(2):
                            for hh in R2:
                                ins = nc.tensor.matmul(pv[D0 * hh:D0 * (hh + 1), ts(j, BLK)], c[par][:, kt, :],
                                                       prob[kt % 4][:, hh, ts(j, BLK)],
                                                       start=(kt == 0), stop=(kt == TT - 1))
                        ins.then_inc(pv_done, 1)

            pe.wait_ge(w_loaded[0], 48)
            pe.wait_ge(cleared, 2)
            run(-1, 1, [("UNIT",) + u for u in NEXT_UNITS], 0, 0, True)

            def step(n, par, first, last):
                if not last:
                    pe.wait_ge(w_loaded[1 - par], 48 * ((n + 1) // 2 + 1))
                run(n, par, script(units_of(first, last)), units_before(n), 0 if first else (1 + par) % 2, first)

            steps(pe, step)
            run(STEPS0, 0, [("UNIT",) + u for u in FINISH_ONLY], units_before(STEPS0 - 1) + 3, 1, False)


def residual_out(nc, m, d):
    with ExitStack() as ctx:
        ob = ctx.enter_context(nc.sbuf_tensor("ob", [P, BLK], F32))
        tr = ctx.enter_context(nc.psum_tensor("trr", [P, TPB, P], F32))

        def sem(name):
            return m.ctx.enter_context(nc.semaphore(name))
        ob_ready, transposed, added = sem("ob_ready"), sem("tr_r"), sem("added_r")
        block = ctx.enter_context(nc.Block())

        @block.scalar
        def _(act):
            for j in range(NBLK):
                if j:
                    act.wait_ge(transposed, j)
                nc.scalar.activation(ob[:, :], m.out_t[:, ts(j, BLK)], ACT.Identity, bias=m.out_bias[:, 0:1]
                                     ).then_inc(ob_ready, 1)

        @block.tensor
        def _(pe):
            for j in range(NBLK):
                pe.wait_ge(ob_ready, j + 1)
                if j:
                    pe.wait_ge(added, j)
                for t in range(TPB):
                    ins = nc.tensor.transpose(tr[:, t, :], ob[:, ts(t, P)], m.ident[:, :])
                ins.then_inc(transposed, 1)

        @block.vector
        def _(v):
            for j in range(NBLK):
                v.wait_ge(transposed, j + 1)
                xs = m.x[:, TPB * j:TPB * (j + 1), :]
                nc.vector.tensor_tensor(xs, tr[:, :, :], xs, ALU.add).then_inc(added, 1)


def router(nc, m, d, layer, w_dram, w1_dram, b1_dram, b2_dram):
    L = str(layer)
    with ExitStack() as ctx:
        def sb(name, shape, dt=F32):
            return ctx.enter_context(nc.sbuf_tensor(name + "_r" + L, shape, dt))

        def sem(name):
            return m.ctx.enter_context(nc.semaphore(name + "_r" + L))

        wr = sb("wr", [P if layer == 0 else HR, NEXP])
        if layer == 1:
            wr1 = sb("wr1", [P, HR])
            br1 = sb("br1", [HR, 1])
            br2 = sb("br2", [P, NEXP])
            hr = sb("hr", [HR, N])
        iota = sb("iota", [P, NEXP])
        m.stats = sb("stats", [P, TPB, 6])
        m.mv = sb("mv", [P, TPB, 2])
        m.rstd = sb("rstd", [P, TPB])
        m.std = sb("std", [P, TPB])
        m.xn = sb("xn", [P, TPB, E])
        shape = [P, NT, NEXP]
        lg, ex, probs, top, oh, gate = (sb(n, shape) for n in ("lg", "ex", "probs", "top", "oh", "gate"))
        idx = sb("idx", shape, U32)
        idxf = sb("idxf", [P, NT, TOPK])
        col = sb("col", [P, 8, NT])
        tr = ctx.enter_context(nc.psum_tensor("tr_r" + L, [P, BLK], F32))
        hp = ctx.enter_context(nc.psum_tensor("hp_r" + L, [P, BLK], F32))
        lp = ctx.enter_context(nc.psum_tensor("lp_r" + L, [P, NT, NEXP], F32))
        gp = ctx.enter_context(nc.psum_tensor("gp_r" + L, [P, N], F32))
        loaded, m.ln_step, m.std_ready = sem("loaded"), sem("ln_step"), sem("std_ready")
        xn_ready, transposed, xt_ready = sem("xn_ready"), sem("transposed"), sem("xt_ready")
        hid_filled, hid_ready, logits_done = sem("hid_filled"), sem("hid_ready"), sem("logits_done")
        step, shifted, exp_done, gate_ready = sem("step"), sem("shifted"), sem("exp_done"), sem("gate_ready")
        rows_filled, rows_ready, stored, spread = sem("rows_filled"), sem("rows_ready"), sem("stored"), sem("spread")
        block = ctx.enter_context(nc.Block())
        n_loads = 2 if layer == 0 else 5

        @block.sync
        def _(sp):
            sp.dma_start(wr[:, :], w_dram).then_inc(loaded, 16)
            sp.dma_start(iota[:, :], d["iota"]).then_inc(loaded, 16)
            if layer == 1:
                for dst, src in ((wr1, w1_dram), (br1, b1_dram), (br2, b2_dram)):
                    sp.dma_start(dst[:, :], src).then_inc(loaded, 16)
            m.load_experts(sp)
            sp.wait_ge(rows_ready, 2)
            gates = d["gates0"] if layer == 0 else d["gates1"]
            sp.dma_start(gates, m.gate_t[0:NEXP, :]).then_inc(stored, 16)
            sp.wait_ge(stored, 16)
            for e in range(NEXP):
                sp.dma_start(m.gb[:, e, :], gates[e:e + 1, :].rearrange("a n -> (a n)").partition_broadcast(P)
                             ).then_inc(spread, 16)
            sp.wait_ge(spread, 16 * NEXP)
            m.await_experts(sp)

        @block.gpsimd
        def _(pool):
            nc.gpsimd.memset(m.gate_t[:, :], 1.0).then_inc(rows_ready, 1)

        @block.vector
        def _(v):
            count = [0]

            def link(ins):
                count[0] += 1
                ins.then_inc(step, 1)
                v.wait_ge(step, count[0])

            for j in range(NBLK):
                def x_block(t):
                    return m.x[:, TPB * j + t, :]

                layernorm_block(nc, v, m, j, x_block, 3 * j)
                if j:
                    v.wait_ge(transposed, j)
                normalise_block(nc, m, x_block).then_inc(xn_ready, 1)
            v.wait_ge(loaded, 16 * n_loads)
            v.wait_ge(logits_done, 1)
            if layer == 0:
                link(nc.vector.tensor_copy(lg[:, :, :], lp[:, :, :]))
            else:
                link(nc.vector.tensor_tensor(lg[:, :, :], lp[:, :, :],
                                             br2[:, :].unsqueeze(1).to_broadcast(shape), ALU.add))
            link(nc.vector.reduce_max(col[:, 0, :], lg[:, :, :], AX.X))
            nc.vector.tensor_tensor(lg[:, :, :], lg[:, :, :], col[:, 0, :].unsqueeze(2).to_broadcast(shape),
                                    ALU.subtract).then_inc(shifted, 1)
            v.wait_ge(exp_done, 1)
            link(nc.vector.reduce_sum(col[:, 1, :], ex[:, :, :], AX.X))
            link(nc.vector.reciprocal(col[:, 2, :], col[:, 1, :]))
            link(nc.vector.tensor_tensor(probs[:, :, :], ex[:, :, :],
                                         col[:, 2, :].unsqueeze(2).to_broadcast(shape), ALU.mult))
            for t in range(NT):
                ins = nc.vector.max(top[:, t, :], probs[:, t, :])
            link(ins)
            for t in range(NT):
                ins = nc.vector.max_index(idx[:, t, :], top[:, t, :], probs[:, t, :])
            link(ins)
            link(nc.vector.tensor_copy(idxf[:, :, :], idx[:, :, 0:TOPK]))
            if layer == 0:
                link(nc.vector.tensor_tensor(col[:, 3, :], top[:, :, 0], top[:, :, 1], ALU.add))
                link(nc.vector.reciprocal(col[:, 4, :], col[:, 3, :]))
                nc.vector.tensor_tensor(col[:, 5, :], top[:, :, 0], col[:, 4, :], ALU.mult)
                link(nc.vector.tensor_tensor(col[:, 6, :], top[:, :, 1], col[:, 4, :], ALU.mult))
            else:
                nc.vector.tensor_tensor(col[:, 3, :], top[:, :, 1], top[:, :, 0], ALU.subtract).then_inc(shifted, 1)
                v.wait_ge(exp_done, 2)
                link(nc.vector.tensor_scalar(col[:, 4, :], col[:, 7, :], 1.0, None, ALU.add))
                link(nc.vector.reciprocal(col[:, 5, :], col[:, 4, :]))
                link(nc.vector.tensor_tensor(col[:, 6, :], col[:, 7, :], col[:, 5, :], ALU.mult))
            iota_b = iota[:, :].unsqueeze(1).to_broadcast(shape)
            link(nc.vector.tensor_tensor(oh[:, :, :], iota_b, idxf[:, :, 0:1].to_broadcast(shape), ALU.is_equal))
            link(nc.vector.tensor_tensor(gate[:, :, :], oh[:, :, :], col[:, 5, :].unsqueeze(2).to_broadcast(shape),
                                         ALU.mult))
            link(nc.vector.tensor_tensor(oh[:, :, :], iota_b, idxf[:, :, 1:2].to_broadcast(shape), ALU.is_equal))
            link(nc.vector.tensor_tensor(oh[:, :, :], oh[:, :, :], col[:, 6, :].unsqueeze(2).to_broadcast(shape),
                                         ALU.mult))
            nc.vector.tensor_tensor(gate[:, :, :], gate[:, :, :], oh[:, :, :], ALU.add).then_inc(gate_ready, 1)
            v.wait_ge(rows_ready, 1)
            v.wait_ge(rows_filled, 1)
            nc.vector.tensor_copy(m.gate_t[0:NEXP, :], gp[0:NEXP, :]).then_inc(rows_ready, 1)

        @block.scalar
        def _(act):
            if layer == 1:
                act.wait_ge(loaded, 16 * n_loads)
            for j in range(NBLK):
                deviation_block(nc, act, m, j)
                act.wait_ge(transposed, j + 1)
                nc.scalar.copy(m.xt_all[:, ts(j, BLK)], tr[:, :]).then_inc(xt_ready, 1)
                if layer == 1:
                    act.wait_ge(hid_filled, j + 1)
                    nc.scalar.activation(hr[:, ts(j, BLK)], hp[0:HR, :], ACT.Relu, bias=br1[:, 0:1]
                                         ).then_inc(hid_ready, 1)
            act.wait_ge(shifted, 1)
            nc.scalar.activation(ex[:, :, :], lg[:, :, :], ACT.Exp).then_inc(exp_done, 1)
            if layer == 1:
                act.wait_ge(shifted, 2)
                nc.scalar.activation(col[:, 7, :], col[:, 3, :], ACT.Exp, scale=1.0 / TOPK).then_inc(exp_done, 1)

        @block.tensor
        def _(pe):
            pe.wait_ge(loaded, 16 * n_loads)
            for j in range(NBLK):
                pe.wait_ge(xn_ready, j + 1)
                if j:
                    pe.wait_ge(xt_ready, j)
                for t in range(TPB):
                    ins = nc.tensor.transpose(tr[:, ts(t, P)], m.xn[:, t, :], m.ident[:, :])
                ins.then_inc(transposed, 1)
                pe.wait_ge(xt_ready, j + 1)
                if layer == 1:
                    if j:
                        pe.wait_ge(hid_ready, j)
                    nc.tensor.matmul(hp[0:HR, :], wr1[:, :], m.xt_all[:, ts(j, BLK)], start=True, stop=True
                                     ).then_inc(hid_filled, 1)
                    pe.wait_ge(hid_ready, j + 1)
                src = m.xt_all if layer == 0 else hr
                for t in range(TPB * j, TPB * (j + 1)):
                    ins = nc.tensor.matmul(lp[:, t, :], src[:, ts(t, P)], wr[:, :], start=True, stop=True)
            ins.then_inc(logits_done, 1)
            pe.wait_ge(gate_ready, 1)
            for t in range(NT):
                ins = nc.tensor.matmul(gp[0:NEXP, ts(t, P)], gate[:, t, :], m.ident[:, :], start=True, stop=True)
            ins.then_inc(rows_filled, 1)


HR = E // 4


def experts0(nc, m, d):
    with ExitStack() as ctx:
        def sb(name, shape, dt=F32):
            return ctx.enter_context(nc.sbuf_tensor(name, shape, dt))

        def pb(name, shape):
            return ctx.enter_context(nc.psum_tensor(name, shape, F32))

        def sem(name):
            return m.ctx.enter_context(nc.semaphore(name))

        s = [sb(f"silu0_{i}", [P, BLK]) for i in range(2)]
        hid = [sb(f"hid0_{i}", [P, BLK]) for i in range(2)]
        ob = sb("ob0", [P, BLK])
        h1 = [pb(f"h1_{i}", [P, BLK]) for i in range(2)]
        h2 = [pb(f"h2_{i}", [P, BLK]) for i in range(2)]
        out = pb("out0", [P, BLK])
        tr = pb("tr_e0", [P, TPB, P])
        up_done, silu_done, gated, hid_done = sem("up_done0"), sem("silu_done0"), sem("gated0"), sem("hid_done0")
        down_done, ob_ready, transposed, added = sem("down_done0"), sem("ob_ready0"), sem("tr_done0"), sem("added0")
        block = ctx.enter_context(nc.Block())

        @block.tensor
        def _(pe):
            with pe.Fori(0, NBLK) as j:
                cols = ds(BLK * j, BLK)

                def down(e):
                    pe.wait_ge(hid_done, NEXP * j + e + 1)
                    nc.tensor.matmul(out[:, :], m.down[:, e, :], hid[e % 2][:, :], start=(e == 0),
                                     stop=(e == NEXP - 1)).then_inc(down_done, 1)

                for e in range(NEXP):
                    if e >= 2:
                        pe.wait_ge(hid_done, NEXP * j + e - 1)
                    nc.tensor.matmul(h1[e % 2][:, :], m.up[:, e, 0:P], m.xt_all[:, cols], start=True, stop=True)
                    nc.tensor.matmul(h2[e % 2][:, :], m.up[:, e, P:2 * P], m.xt_all[:, cols], start=True, stop=True
                                     ).then_inc(up_done, 1)
                    if e:
                        down(e - 1)
                down(NEXP - 1)
                pe.wait_ge(ob_ready, j + 1)
                for t in range(TPB):
                    ins = nc.tensor.transpose(tr[:, t, :], ob[:, ts(t, P)], m.ident[:, :])
                ins.then_inc(transposed, 1)

        @block.scalar
        def _(act):
            with act.Fori(0, NBLK) as j:
                for e in range(NEXP):
                    act.wait_ge(up_done, NEXP * j + e + 1)
                    if e >= 2:
                        act.wait_ge(hid_done, NEXP * j + e - 1)
                    nc.scalar.activation(s[e % 2][:, :], h1[e % 2][:, :], ACT.Silu).then_inc(silu_done, 1)
                act.wait_ge(down_done, NEXP * (j + 1))
                nc.scalar.copy(ob[:, :], out[:, :]).then_inc(ob_ready, 1)

        @block.vector
        def _(v):
            with v.Fori(0, NBLK) as j:
                for e in range(NEXP):
                    at = NEXP * j + e
                    v.wait_ge(up_done, at + 1)
                    if e >= 2:
                        v.wait_ge(down_done, at - 1)
                    nc.vector.tensor_tensor(hid[e % 2][:, :], h2[e % 2][:, :], m.gb[:, e, ds(BLK * j, BLK)], ALU.mult
                                            ).then_inc(gated, 1)
                    v.wait_ge(gated, at + 1)
                    v.wait_ge(silu_done, at + 1)
                    nc.vector.tensor_tensor(hid[e % 2][:, :], hid[e % 2][:, :], s[e % 2][:, :], ALU.mult
                                            ).then_inc(hid_done, 1)
                v.wait_ge(transposed, j + 1)
                xs = m.x[:, ds(TPB * j, TPB), :]
                nc.vector.tensor_tensor(xs, tr[:, :, :], xs, ALU.add).then_inc(added, 1)


def l1_prologue(nc, m, d):
    with ExitStack() as ctx:
        def sb(name, shape, dt=F32):
            return ctx.enter_context(nc.sbuf_tensor(name, shape, dt))

        def pb(name, shape):
            return ctx.enter_context(nc.psum_tensor(name, shape, F32))

        def sem(name):
            return m.ctx.enter_context(nc.semaphore(name))

        wkv = sb("wkv", [P, E])
        wv = sb("wv1", [P, E])
        wrope = sb("wrope", [P, 4, P])
        cs = sb("cs", [P, 2, T])
        masks = sb("masks", [P, 2, P])
        m.stats = sb("stats1", [P, TPB, 6])
        m.mv = sb("mv1", [P, TPB, 2])
        m.rstd = sb("rstd1", [P, TPB])
        m.std = sb("std1", [P, TPB])
        m.xn = sb("xn1", [P, TPB, E])
        ca, cb, rot, low = (sb(n, [P, BLK]) for n in ("ca", "cb", "rot", "low"))
        hi = sb("hi1", [P, BLK], F32R)
        tr = pb("tr1", [P, BLK])
        ckp = pb("ckp", [P, BLK])
        vp = pb("vp", [P, TPB, E])
        rp = [pb(f"rp{i}", [P, BLK]) for i in range(2)]
        loaded, m.ln_step, m.std_ready = sem("loaded1"), sem("ln_step1"), sem("std_ready1")
        xn_ready, transposed, xt_ready = sem("xn_ready1"), sem("transposed1"), sem("xt_ready1")
        ck_filled, ck_ready, v_filled, v_read = sem("ck_filled"), sem("ck_ready"), sem("v_filled"), sem("v_read")
        r_filled, r_read, rot_step, hi_ready, packed = (sem("r_filled"), sem("r_read"), sem("rot_step"),
                                                        sem("hi_ready"), sem("packed"))
        cleared, m_ready = sem("v_cleared"), sem("m_ready")
        block = ctx.enter_context(nc.Block())

        @block.sync
        def _(sp):
            for dst, src in ((wkv, d["wkv"]), (wv, d["wv1"]), (m.coef, d["coef"])):
                sp.dma_start(dst[:, :], src).then_inc(loaded, 16)
            for dst, src in ((wrope, d["wrope"]), (cs, d["cs"]), (masks, d["masks"]), (m.wk_all, d["wk1"]), (m.wq_all, d["wq1"])):
                sp.dma_start(dst[:, :, :], src).then_inc(loaded, 16)
            sp.wait_ge(loaded, 16 * 8)

        v_rows = m.v_all[:, :, :, :, :, :].rearrange("p b q t g d -> p (b q t g) d")

        @block.gpsimd
        def _(pool):
            nc.gpsimd.memset(v_rows, 0.0).then_inc(cleared, 1)
            pool.wait_ge(cleared, 1)
            nc.gpsimd.memset(v_rows[:, :, D1:D1 + 1], 1.0).then_inc(cleared, 1)

        @block.vector
        def _(v):
            v.wait_ge(loaded, 16 * 8)
            v.wait_ge(cleared, 2)
            nc.vector.tensor_copy(m.identr[:, :], m.ident[:, :])
            nc.vector.tensor_copy(m.maskr[:, :, :], masks[:, :, :]).then_inc(m_ready, 1)
            for j in range(NBLK):
                def x_block(t):
                    return m.x[:, TPB * j + t, :]

                layernorm_block(nc, v, m, j, x_block, 3 * j)
                if j:
                    v.wait_ge(transposed, j)
                normalise_block(nc, m, x_block).then_inc(xn_ready, 1)
                v.wait_ge(v_filled, j + 1)
                for t in range(TPB):
                    ins = nc.vector.tensor_copy(m.v_all[:, j // 2, :, TPB * (j % 2) + t, :, 0:D1],
                                                vp[:, t, :].rearrange("p (q g d) -> p q g d", q=QUADS, d=D1))
                ins.then_inc(v_read, 1)
                for n, dst in enumerate((m.kr, m.qr)):
                    u = 2 * j + n
                    pos = ds(BLK * (j % 2), BLK)
                    v.wait_ge(r_filled, u + 1)
                    if u:
                        v.wait_ge(hi_ready, u)
                    nc.vector.tensor_tensor(ca[:, :], rp[0][:, :], cs[:, 0, pos], ALU.mult)
                    nc.vector.tensor_tensor(cb[:, :], rp[1][:, :], cs[:, 1, pos], ALU.mult).then_inc(r_read, 1)
                    v.wait_ge(r_read, u + 1)
                    nc.vector.tensor_tensor(rot[:, :], ca[:, :], cb[:, :], ALU.add).then_inc(rot_step, 1)
                    v.wait_ge(hi_ready, u + 1)
                    c = 2 + 2 * n
                    nc.vector.scalar_tensor_tensor(dst[:, ts(j, BLK)], hi[:, :].bitcast(F32), m.coef[:, c + 1:c + 2],
                                                   low[:, :], ALU.mult, ALU.add).then_inc(packed, 1)

        @block.scalar
        def _(act):
            act.wait_ge(loaded, 16 * 8)
            for j in range(NBLK):
                deviation_block(nc, act, m, j)
                act.wait_ge(transposed, j + 1)
                nc.scalar.copy(m.xt_all[:, ts(j, BLK)], tr[:, :]).then_inc(xt_ready, 1)
                act.wait_ge(ck_filled, j + 1)
                nc.scalar.copy(m.ck_all[:, ts(j, BLK)], ckp[:, :]).then_inc(ck_ready, 1)
                for n in range(2):
                    u = 2 * j + n
                    act.wait_ge(rot_step, u + 1)
                    if u:
                        act.wait_ge(packed, u)
                    c = 2 + 2 * n
                    nc.scalar.activation(low[:, :], rot[:, :], ACT.Copy, scale=m.coef[:, c:c + 1])
                    nc.scalar.copy(hi[:, :], rot[:, :]).then_inc(hi_ready, 1)

        @block.tensor
        def _(pe):
            pe.wait_ge(loaded, 16 * 8)
            for j in range(NBLK):
                cols = ts(j, BLK)
                pe.wait_ge(xn_ready, j + 1)
                if j:
                    pe.wait_ge(xt_ready, j)
                for t in range(TPB):
                    ins = nc.tensor.transpose(tr[:, ts(t, P)], m.xn[:, t, :], m.ident[:, :])
                ins.then_inc(transposed, 1)
                pe.wait_ge(xt_ready, j + 1)
                if j:
                    pe.wait_ge(ck_ready, j)
                nc.tensor.matmul(ckp[:, :], wkv[:, :], m.xt_all[:, cols], start=True, stop=True).then_inc(ck_filled, 1)
                pe.wait_ge(ck_ready, j + 1)
                if j:
                    pe.wait_ge(v_read, j)
                for t in range(TPB):
                    ins = nc.tensor.matmul(vp[:, t, :], m.ck_all[:, ts(TPB * j + t, P)], wv[:, :],
                                           start=True, stop=True)
                ins.then_inc(v_filled, 1)
                for n, src in enumerate((m.ck_all, m.xt_all)):
                    if 2 * j + n:
                        pe.wait_ge(r_read, 2 * j + n)
                    for s in range(2):
                        ins = nc.tensor.matmul(rp[s][:, :], wrope[:, 2 * n + s, :], src[:, cols],
                                               start=True, stop=True)
                    ins.then_inc(r_filled, 1)


def s_pieces():
    out = []
    for t in range(TT):
        width = (t + 1) * P
        if width <= BLK:
            out.append((t, 0, width, True))
        else:
            out += [(t, 0, BLK, False), (t, BLK, width - BLK, True)]
    return out


PIECES = s_pieces()
NEXT1 = ([("k", 0, 0), ("k", 0, 1), ("q", 0, 0), ("q", 0, 1)]
         + [("s", 0, u) for u in range(len(PIECES))]
         + [("s", 1, u) for u in range(2)] + [("m", 0, 0)] + [("s", 1, u) for u in range(2, len(PIECES))]
         + [("s", 2, u) for u in range(2)] + [("m", 1, 0)] + [("s", 2, u) for u in range(2, len(PIECES))]
         + [("s", 3, u) for u in range(2)] + [("m", 2, 0)] + [("s", 3, u) for u in range(2, len(PIECES))]
         + [("m", 3, 0)])
FINISH1 = [("t", 0, 0), ("t", 0, 1)]
FULL1 = NEXT1[:4] + FINISH1 + NEXT1[4:]
N_NEXT1, N_STEP1 = len(NEXT1), len(FULL1)


def script1(units):
    left, out = list(units), []
    for kt in range(TT):
        for g in range(4):
            out.append(("ST", kt, g))
            if left:
                out.append(("UNIT",) + left.pop(0))
        if kt:
            out.append(("PV", kt - 1))
        for _ in range(4):
            if left:
                out.append(("UNIT",) + left.pop(0))
    out.append(("PV", TT - 1))
    return out + [("UNIT",) + u for u in left]


def units_before1(n):
    return N_NEXT1 if isinstance(n, int) and n == 0 else 2 * N_NEXT1 + N_STEP1 * (n - 1)


def q_pieces(kt):
    lo = P * kt
    return [(lo, BLK), (BLK, T)] if lo < BLK else [(lo, T)]


def l1_attention(nc, m, d):
    with ExitStack() as ctx:
        def sb(name, shape, dt=F32):
            return ctx.enter_context(nc.sbuf_tensor(name, shape, dt))

        def sem(name):
            return m.ctx.enter_context(nc.semaphore(name))

        R2, R4 = range(2), range(4)
        HEAD = 3 * DR
        ROW = HEAD + 3 * D1
        kk = [sb(f"l1_kk{a}", [P, 4, T], F32R) for a in R2]
        qq = [sb(f"l1_qq{a}", [P, 4, T], F32R) for a in R2]
        wk = [sb(f"l1_wk{a}", [P, P]) for a in R2]
        wq = [sb(f"l1_wq{a}", [P, P]) for a in R2]
        val = [sb(f"l1_v{a}", [P, TT, 4, 32]) for a in R2]
        prob = [sb(f"l1_prob{s}", [P, 4, T]) for s in R2]
        low = sb("l1_low", [P, BLK])
        hi = sb("l1_hi", [P, BLK], F32R)
        head = [sb(f"l1_head{s}", [P, T], F32R) for s in R2]
        ut = sb("l1_ut", [P, T])
        mx = sb("l1_mx", [P, 4, TT, 2])
        mmax = sb("l1_mmax", [P, 4, TT])
        negm = sb("l1_negm", [P, 4, TT])
        mrow = [sb(f"l1_mrow{g}", [TT, P], F32R) for g in R4]
        rs = sb("l1_rs", [P, 2, TPB, 4])
        st = [ctx.enter_context(nc.psum_tensor(f"l1_st{h}", [P, T], F32)) for h in R2]
        pv = ctx.enter_context(nc.psum_tensor("l1_pv", [P, T], F32))
        work = [ctx.enter_context(nc.psum_tensor(f"l1_work{h}", [P, BLK], F32)) for h in R2]

        cleared = sem("cleared1")
        w_loaded = [sem(f"w_loaded1{a}") for a in R2]
        rope_loaded = [sem(f"rope_loaded{a}") for a in R2]
        k_loaded, q_loaded = [sem(f"k_loaded{a}") for a in R2], [sem(f"q_loaded{a}") for a in R2]
        row_loaded = [sem(f"row_loaded1{g}") for g in R4]
        filled, read, halves = sem("work_filled1"), sem("work_read1"), sem("halves")
        negm_ready, mmax_ready, rs_ready = sem("negm_ready1"), sem("mmax_ready1"), sem("rs_ready")
        st_filled, exp_done, pv_done, ut_ready = sem("st_filled1"), sem("exp_done1"), sem("pv_done1"), sem("ut_ready1")
        block = ctx.enter_context(nc.Block())

        def steps(eng, step):
            step(0, 0, True, False)
            with eng.Fori(0, (STEPS1 - 2) // 2) as i:
                step(2 * i + 1, 1, False, False)
                step(2 * i + 2, 0, False, False)
            step(STEPS1 - 1, 1, False, True)

        def units_of(first, last):
            return NEXT1 if first else FINISH1 if last else FULL1

        def at_unit(first, last, kind, j):
            return [u[0] == kind and u[2] == j for u in units_of(first, last)].index(True)

        def even_of(first, par):
            return 0 if first else (1 + par) * N_STEP1 % 2

        @block.sync
        def _(sp):
            v_steps = m.v_all[:, :, :, :, :, :].rearrange("p b q t g d -> p (b q t g) d")

            def load_weights(k, par):
                sp.dma_start(wk[par][:, :], m.wk_all[:, k % QUADS, :]).then_inc(w_loaded[par], 16)
                sp.dma_start(wq[par][:, :], m.wq_all[:, k % QUADS, :]).then_inc(w_loaded[par], 16)
                sp.dma_start(val[par][:, :, :, 0:2 * D1].rearrange("p t g d -> p (t g) d"),
                             v_steps[:, ds(TT * 4 * k, TT * 4), :]
                             ).then_inc(w_loaded[par], 16)

            def load_rope(k, par):
                cols = ds(T * (k // QUADS), T)
                for dst, src in ((kk, m.kr), (qq, m.qr)):
                    for g in R4:
                        sp.dma_start(dst[par][0:HEAD, g, :].bitcast(F32), src[0:HEAD, cols].bitcast(F32)
                                     ).then_inc(rope_loaded[par], 16)

            def head_rows(k, par, units, base):
                seen = 0
                for kind, g, j in units:
                    if kind in "kq" and j == 1:
                        sp.wait_ge(read, base + seen + 1)
                        dst, src, loaded = ((kk, head[0], k_loaded) if kind == "k" else (qq, head[1], q_loaded))
                        for h in R4:
                            sp.dma_start(dst[par][HEAD:P, h, :].bitcast(F32), src[32 * h:32 * (h + 1), :].bitcast(F32)
                                         ).then_inc(loaded[par], 16)
                    if kind == "m":
                        sp.wait_ge(read, base + seen + 1)
                        sp.dma_start(qq[par][ROW:ROW + 1, g, :].bitcast(F32), mrow[g][:, :].bitcast(F32)
                                     ).then_inc(row_loaded[g], 16)
                    seen += 1

            sp.wait_ge(cleared, 1)
            load_weights(0, 0)
            load_rope(0, 0)
            head_rows(0, 0, NEXT1, 0)

            def step(n, par, first, last):
                if not last:
                    if not first:
                        sp.wait_ge(pv_done, TT * n)
                    load_weights(n + 1, 1 - par)
                    load_rope(n + 1, 1 - par)
                    head_rows(n + 1, 1 - par, units_of(first, last), units_before1(n))

            steps(sp, step)

        @block.scalar
        def _(act):
            def run(n, par, todo, base, even, first):
                seen = 0
                for what, kind, *rest in todo:
                    if what == "UNIT":
                        j = rest[1]
                        if kind in "kq":
                            act.wait_ge(filled, base + seen + 1)
                            if not (isinstance(base, int) and base + seen == 0):
                                act.wait_ge(read, base + seen)
                            buf = work[(even + seen) % 2]
                            c = 6 + 2 * (kind == "q")
                            one = m.coef[:, 10:11] if kind == "k" else m.coef[:, 11:12]
                            nc.scalar.activation(low[:, :], buf[:, :], ACT.Identity, scale=m.coef[:, c:c + 1], bias=one)
                            nc.scalar.copy(hi[:, :], buf[:, :]).then_inc(halves, 1)
                        seen += 1
                    elif what == "ST":
                        kt, g = kind, rest[0]
                        act.wait_ge(st_filled, 4 * (TT * n + kt) + g + 1)
                        if not (first and kt < 2):
                            act.wait_ge(pv_done, TT * n + kt - 1)
                        nc.scalar.activation(prob[kt % 2][:, g, P * kt:T], st[g % 2][:, P * kt:T], ACT.Exp,
                                             scale=SCALE1).then_inc(exp_done, 1)

            run(-1, 1, [("UNIT",) + u for u in NEXT1], 0, 0, True)

            def step(n, par, first, last):
                run(n, par, script1(units_of(first, last)), units_before1(n), even_of(first, par), first)
                act.wait_ge(pv_done, TT * (n + 1))
                if not first:
                    act.wait_ge(read, units_before1(n) + at_unit(first, last, "t", 1) + 1)
                nc.scalar.copy(ut[:, :], pv[:, :]).then_inc(ut_ready, 1)

            steps(act, step)

        @block.gpsimd
        def _(pool):
            for a in R2:
                nc.gpsimd.memset(val[a][:, :, :, 2 * D1:], 0.0)
            nc.gpsimd.memset(mx[:, :, :, :], -3e38).then_inc(cleared, 1)

        @block.vector
        def _(v):
            def combine(g, k, u_last):
                v.wait_ge(read, u_last + 1)
                nc.vector.tensor_tensor(mmax[:, g, :], mx[:, g, :, 0], mx[:, g, :, 1], ALU.max).then_inc(mmax_ready, 1)
                v.wait_ge(mmax_ready, 4 * k + g + 1)
                nc.vector.tensor_scalar(negm[:, g, :], mmax[:, g, :], -1.0, None, ALU.mult).then_inc(negm_ready, 1)

            def run(n, par, units, base, even):
                seen = 0
                for kind, g, j in units:
                    u, buf = base + seen, work[(even + seen) % 2]
                    if kind in "kq":
                        k = n + 1
                        c = 6 + 2 * (kind == "q")
                        v.wait_ge(halves, 4 * k + 2 * (kind == "q") + j + 1)
                        if not (isinstance(k, int) and k == 0):
                            loaded = (k_loaded if kind == "k" else q_loaded)[par]
                            v.wait_ge(loaded, 64 * ((k - 1) // 2 + 1))
                        nc.vector.scalar_tensor_tensor(head[kind == "q"][:, ts(j, BLK)], hi[:, :].bitcast(F32),
                                                       m.coef[:, c + 1:c + 2], low[:, :], ALU.mult, ALU.add
                                                       ).then_inc(read, 1)
                    elif kind == "s":
                        t, key, width, diagonal = PIECES[j]
                        v.wait_ge(filled, u + 1)
                        nc.vector.reduce_max(mx[:, g, t, (key > 0):(key > 0) + 1], buf[:, 0:width], AX.X
                                             ).then_inc(read, 1)
                        if j == len(PIECES) - 1:
                            combine(g, n + 1, u)
                    elif kind == "m":
                        k = n + 1
                        if not (isinstance(k, int) and k == 0):
                            v.wait_ge(row_loaded[g], 16 * k)
                        v.wait_ge(filled, u + 1)
                        nc.vector.tensor_copy(mrow[g][:, :], buf[0:TT, 0:P]).then_inc(read, 1)
                    else:
                        k = n - 1
                        v.wait_ge(filled, u + 1)
                        parts = buf[:, :].rearrange("p (t g c) -> p t g c", t=TPB, g=4)
                        nc.vector.reciprocal(rs[:, j, :, :], parts[:, :, :, D1]).then_inc(rs_ready, 1)
                        v.wait_ge(rs_ready, 2 * k + j + 1)
                        nc.vector.tensor_tensor(m.attn[:, ds(TT * (k // QUADS) + TPB * j, TPB), k % QUADS, :, :],
                                                parts[:, :, :, 0:D1],
                                                rs[:, j, :, :].unsqueeze(3).to_broadcast([P, TPB, 4, D1]),
                                                ALU.mult).then_inc(read, 1)
                    seen += 1

            v.wait_ge(cleared, 1)
            run(-1, 1, NEXT1, 0, 0)

            def step(n, par, first, last):
                run(n, par, units_of(first, last), units_before1(n), even_of(first, par))

            steps(v, step)
            run(STEPS1, 0, FINISH1, units_before1(STEPS1 - 1) + 2, 0)

        @block.tensor
        def _(pe):
            def unit(kind, g, j, u, buf, par, k):
                if not (isinstance(u, int) and u < 2):
                    pe.wait_ge(read, u - 1)
                if kind in "kq":
                    w, src = (wk, m.ck_all) if kind == "k" else (wq, m.xt_all)
                    ins = nc.tensor.matmul(buf[:, :], w[par][:, :], src[:, ds(T * (k // QUADS) + BLK * j, BLK)],
                                           start=True, stop=True)
                elif kind == "s":
                    if g == 0 and j == 0:
                        pe.wait_ge(rope_loaded[par], 128 * (k // 2 + 1))
                        pe.wait_ge(k_loaded[par], 64 * (k // 2 + 1))
                        pe.wait_ge(q_loaded[par], 64 * (k // 2 + 1))
                    t, key, width, diagonal = PIECES[j]
                    ins = nc.tensor.matmul(buf[:, 0:width], qq[par][:, g, ts(t, P)], kk[par][:, g, key:key + width],
                                           start=True, stop=not diagonal)
                    if diagonal:
                        ins = nc.tensor.matmul(buf[:, width - P:width], m.identr[:, :], m.maskr[:, 0, :],
                                               start=False, stop=True)
                elif kind == "m":
                    pe.wait_ge(negm_ready, 4 * k + g + 1)
                    ins = nc.tensor.matmul(buf[0:TT, 0:P], negm[:, g, :], m.ident[:, :], start=True, stop=True)
                else:
                    pe.wait_ge(ut_ready, k + 1)
                    for t in range(TPB):
                        ins = nc.tensor.transpose(buf[:, ts(t, P)], ut[:, ts(TPB * j + t, P)], m.ident[:, :])
                ins.then_inc(filled, 1)

            def run(n, par, todo, base, even, first):
                seen = 0
                for what, *rest in todo:
                    if what == "UNIT":
                        kind, g, j = rest
                        unit(kind, g, j, base + seen, work[(even + seen) % 2], 1 - par, n - 1 if kind == "t" else n + 1)
                        seen += 1
                    elif what == "ST":
                        kt, g = rest
                        at = 4 * (TT * n + kt) + g
                        if not (first and kt == 0 and g < 2):
                            pe.wait_ge(exp_done, at - 1)
                        if kt == 0:
                            pe.wait_ge(row_loaded[g], 16 * (n + 1))
                        buf = st[g % 2]
                        pieces = q_pieces(kt)
                        for n_piece, (lo, hi_) in enumerate(pieces):
                            ins = nc.tensor.matmul(buf[:, lo:hi_], kk[par][:, g, ts(kt, P)], qq[par][:, g, lo:hi_],
                                                   start=True, stop=(n_piece > 0))
                            if n_piece == 0:
                                ins = nc.tensor.matmul(buf[:, lo:lo + P], m.identr[:, :], m.maskr[:, 1, :],
                                                       start=False, stop=True)
                        ins.then_inc(st_filled, 1)
                    else:
                        kt = rest[0]
                        pe.wait_ge(exp_done, 4 * (TT * n + kt + 1))
                        if kt == 0 and not first:
                            pe.wait_ge(ut_ready, n)
                        for lo, hi_ in q_pieces(kt):
                            for g in R4:
                                ins = nc.tensor.matmul(pv[32 * g:32 * (g + 1), lo:hi_], val[par][:, kt, g, :],
                                                       prob[kt % 2][:, g, lo:hi_], start=(kt == 0),
                                                       stop=(kt == TT - 1 or (kt == 3 and lo < BLK)))
                        ins.then_inc(pv_done, 1)

            pe.wait_ge(w_loaded[0], 48)
            run(-1, 1, [("UNIT",) + u for u in NEXT1], 0, 0, True)

            def step(n, par, first, last):
                if not last:
                    pe.wait_ge(w_loaded[1 - par], 48 * ((n + 1) // 2 + 1))
                run(n, par, script1(units_of(first, last)), units_before1(n), even_of(first, par), first)

            steps(pe, step)
            run(STEPS1, 0, [("UNIT",) + u for u in FINISH1], units_before1(STEPS1 - 1) + 2, 0, False)


def l1_output(nc, m, d):
    with ExitStack() as ctx:
        wo = ctx.enter_context(nc.sbuf_tensor("wo", [P, E], F32))
        at = [ctx.enter_context(nc.sbuf_tensor(f"at{i}", [P, BLK], F32)) for i in range(2)]
        tr = [ctx.enter_context(nc.psum_tensor(f"tr_o{i}", [P, BLK], F32)) for i in range(2)]
        out = [ctx.enter_context(nc.psum_tensor(f"out_o{i}", [P, TPB, E], F32)) for i in range(2)]

        def sem(name):
            return m.ctx.enter_context(nc.semaphore(name))
        loaded, transposed, at_ready, out_filled, added = (sem("wo_loaded"), sem("tr_o"), sem("at_ready"),
                                                           sem("out_filled"), sem("added_o"))
        block = ctx.enter_context(nc.Block())

        @block.sync
        def _(sp):
            sp.dma_start(wo[:, :], d["wo"]).then_inc(loaded, 16)

        @block.tensor
        def _(pe):
            pe.wait_ge(loaded, 16)
            for j in range(NBLK):
                if j >= 2:
                    pe.wait_ge(at_ready, j - 1)
                for t in range(TPB):
                    src = m.attn[:, TPB * j + t, :, :, :].rearrange("p a b c -> p (a b c)")
                    ins = nc.tensor.transpose(tr[j % 2][:, ts(t, P)], src, m.ident[:, :])
                ins.then_inc(transposed, 1)
                pe.wait_ge(at_ready, j + 1)
                if j >= 2:
                    pe.wait_ge(added, j - 1)
                for t in range(TPB):
                    ins = nc.tensor.matmul(out[j % 2][:, t, :], at[j % 2][:, ts(t, P)], wo[:, :], start=True, stop=True)
                ins.then_inc(out_filled, 1)

        @block.scalar
        def _(act):
            for j in range(NBLK):
                act.wait_ge(transposed, j + 1)
                if j >= 2:
                    act.wait_ge(out_filled, j - 1)
                nc.scalar.copy(at[j % 2][:, :], tr[j % 2][:, :]).then_inc(at_ready, 1)

        @block.vector
        def _(v):
            for j in range(NBLK):
                v.wait_ge(out_filled, j + 1)
                xs = m.x[:, TPB * j:TPB * (j + 1), :]
                nc.vector.tensor_tensor(xs, out[j % 2][:, :, :], xs, ALU.add).then_inc(added, 1)


def experts1(nc, m, d):
    with ExitStack() as ctx:
        def sb(name, shape, dt=F32):
            return ctx.enter_context(nc.sbuf_tensor(name, shape, dt))

        def pb(name, shape):
            return ctx.enter_context(nc.psum_tensor(name, shape, F32))

        def sem(name):
            return m.ctx.enter_context(nc.semaphore(name))

        UNITS = (NEXP + 1) * CH
        s = [sb(f"silu1_{i}", [P, BLK]) for i in range(3)]
        ob = sb("ob1", [P, BLK])
        hp = [pb(f"hid1_{i}", [P, BLK]) for i in range(3)]
        out = pb("out1", [P, BLK])
        tr = pb("tr_e1", [P, TPB, P])
        up_done, silu_done, gated, down_done = sem("up_done1"), sem("silu_done1"), sem("gated1"), sem("down_done1")
        ob_ready, transposed, added, stored = sem("ob_ready1"), sem("tr_done1"), sem("added1"), sem("stored")
        block = ctx.enter_context(nc.Block())

        @block.tensor
        def _(pe):
            with pe.Fori(0, NBLK) as j:
                cols = ds(BLK * j, BLK)

                def down(u):
                    if u < NEXP * CH:
                        pe.wait_ge(gated, NEXP * CH * j + u + 1)
                    else:
                        pe.wait_ge(silu_done, UNITS * j + u + 1)
                    nc.tensor.matmul(out[:, :], m.w2[:, u, :], s[u % 3][:, :], start=(u == 0), stop=False
                                     ).then_inc(down_done, 1)

                for u in range(UNITS):
                    if u >= 3:
                        pe.wait_ge(silu_done, UNITS * j + u - 2)
                    nc.tensor.matmul(hp[u % 3][:, :], m.w1[:, u, :], m.xt_all[:, cols], start=True, stop=True
                                     ).then_inc(up_done, 1)
                    if u >= 2:
                        down(u - 2)
                down(UNITS - 2)
                down(UNITS - 1)
                nc.tensor.matmul(out[:, :], m.b2[0:NEXP + 1, :], m.gate_t[0:NEXP + 1, cols], start=False, stop=True
                                 ).then_inc(down_done, 1)
                pe.wait_ge(ob_ready, j + 1)
                for t in range(TPB):
                    ins = nc.tensor.transpose(tr[:, t, :], ob[:, ts(t, P)], m.ident[:, :])
                ins.then_inc(transposed, 1)

        @block.scalar
        def _(act):
            with act.Fori(0, NBLK) as j:
                for u in range(UNITS):
                    act.wait_ge(up_done, UNITS * j + u + 1)
                    if u >= 3:
                        act.wait_ge(down_done, (UNITS + 1) * j + u - 2)
                    nc.scalar.activation(s[u % 3][:, :], hp[u % 3][:, :], ACT.Silu, bias=m.b1[:, u:u + 1]
                                         ).then_inc(silu_done, 1)
                act.wait_ge(down_done, (UNITS + 1) * (j + 1))
                nc.scalar.copy(ob[:, :], out[:, :]).then_inc(ob_ready, 1)

        @block.vector
        def _(v):
            with v.Fori(0, NBLK) as j:
                for u in range(NEXP * CH):
                    v.wait_ge(silu_done, UNITS * j + u + 1)
                    nc.vector.tensor_tensor(s[u % 3][:, :], s[u % 3][:, :], m.gb[:, u // CH, ds(BLK * j, BLK)],
                                            ALU.mult).then_inc(gated, 1)
                v.wait_ge(transposed, j + 1)
                xs = m.x[:, ds(TPB * j, TPB), :]
                nc.vector.tensor_tensor(xs, tr[:, :, :], xs, ALU.add).then_inc(added, 1)

        @block.sync
        def _(sp):
            with sp.Fori(0, NBLK) as j:
                sp.wait_ge(added, j + 1)
                sp.dma_start(d["out"][ds(BLK * j, BLK), :].rearrange("(t p) e -> p t e", p=P),
                             m.x[:, ds(TPB * j, TPB), :]).then_inc(stored, 16)
            sp.wait_ge(stored, 16 * NBLK)


def build(nc, d):
    with ExitStack() as ctx:
        m = Mem()
        m.ctx = ctx

        def sb(name, shape, dt=F32):
            return ctx.enter_context(nc.sbuf_tensor(name, shape, dt))

        m.x = sb("x", [P, NT, E])
        m.ident = sb("ident", [P, P])
        m.eps = sb("eps", [P, 1])

        with ExitStack() as layer:
            def sl(name, shape, dt=F32):
                return layer.enter_context(nc.sbuf_tensor(name, shape, dt))

            m.aq = sl("aq", [P, N], F32R)
            m.ak = sl("ak", [P, N], F32R)
            m.w_all = sl("w_all", [P, H0, 4, D0], F32R)
            m.c_all = sl("c_all", [P, NT, D0])
            m.g_all = sl("g_all", [P, PAIRS, E])
            m.out_bias = sl("out_bias", [P, 1])
            m.out_t = sl("out_t", [P, N])
            m.qk_bias = sl("qk_bias", [P, 4 * PAIRS])
            l0_prologue(nc, m, d)
            l0_attention(nc, m, d)
            residual_out(nc, m, d)

        with ExitStack() as layer:
            def sl(name, shape, dt=F32):
                return layer.enter_context(nc.sbuf_tensor(name, shape, dt))

            m.xt_all = sl("xt_all0", [P, N])
            m.gb = sl("gb0", [P, NEXP, N])
            m.gate_t = sl("gate_t0", [P, N])
            m.up = sl("up", [P, NEXP, 2 * P])
            m.down = sl("down", [P, NEXP, E])
            loaded = ctx.enter_context(nc.semaphore("experts0_loaded"))

            def load_experts(sp):
                sp.dma_start(m.up[:, :, :], d["up"]).then_inc(loaded, 16)
                sp.dma_start(m.down[:, :, :], d["down"]).then_inc(loaded, 16)

            def await_experts(sp):
                sp.wait_ge(loaded, 32)

            m.load_experts, m.await_experts = load_experts, await_experts
            router(nc, m, d, 0, d["router"], None, None, None)
            experts0(nc, m, d)

        with ExitStack() as layer:
            def sl(name, shape, dt=F32):
                return layer.enter_context(nc.sbuf_tensor(name, shape, dt))

            m.xt_all = sl("xt_all1", [P, N])
            m.ck_all = sl("ck_all", [P, N])
            m.v_all = sl("v_all", [P, B, QUADS, TT, 4, 2 * D1])
            m.kr = sl("kr", [P, N], F32R)
            m.qr = sl("qr", [P, N], F32R)
            m.attn = sl("attn", [P, NT, QUADS, 4, D1])
            m.identr = sl("identr", [P, P], F32R)
            m.maskr = sl("maskr", [P, 2, P], F32R)
            m.coef = sl("coef", [P, 12])
            m.wk_all = sl("wk_all", [P, QUADS, P])
            m.wq_all = sl("wq_all", [P, QUADS, P])
            l1_prologue(nc, m, d)
            l1_attention(nc, m, d)
            l1_output(nc, m, d)

        with ExitStack() as layer:
            def sl(name, shape, dt=F32):
                return layer.enter_context(nc.sbuf_tensor(name, shape, dt))

            m.xt_all = sl("xt_all2", [P, N])
            m.gb = sl("gb1", [P, NEXP, N])
            m.gate_t = sl("gate_t1", [P, N])
            m.w1 = sl("up1", [P, (NEXP + 1) * CH, P])
            m.w2 = sl("down1", [P, (NEXP + 1) * CH, E])
            m.b1 = sl("bias_up1", [P, (NEXP + 1) * CH])
            m.b2 = sl("bias_down1", [NEXP + 1, E])
            loaded = ctx.enter_context(nc.semaphore("experts1_loaded"))

            def load_experts(sp):
                for dst, src in ((m.w1, d["w1"]), (m.w2, d["w2"])):
                    sp.dma_start(dst[:, :, :], src).then_inc(loaded, 16)
                for dst, src in ((m.b1, d["b1"]), (m.b2, d["b2"])):
                    sp.dma_start(dst[:, :], src).then_inc(loaded, 16)

            def await_experts(sp):
                sp.wait_ge(loaded, 64)

            m.load_experts, m.await_experts = load_experts, await_experts
            router(nc, m, d, 1, d["wr2"], d["wr1"], d["br1"], d["br2"])
            experts1(nc, m, d)


def kernel(**inputs):
    import numpy as _np
    import concourse.bacc as _bacc
    from concourse import mybir as _mybir
    from concourse.bass_utils import run_bass_kernel_spmd as _run

    i = {k: _np.asarray(v) for k, v in inputs.items()}
    h, dk = 16, 64

    def twice(a):
        return _np.concatenate([a, a], axis=0)

    def qk_columns():
        q = i["L0_attn_fcq_b"].reshape(h, dk)
        k = i["L0_attn_fck_b"].reshape(h, dk)
        return twice(_np.stack([q, k], axis=1).reshape(2 * h, dk).T)

    def head_columns(w):
        w = w.reshape(128, 16, 8)
        return _np.concatenate([w, w, w, _np.zeros_like(w)], axis=2).reshape(128, 4, 128)

    def rotary_columns(w):
        swapped = _np.concatenate([w[:, 16:], w[:, :16]], axis=1)
        return [_np.tile(w, (1, 4)), _np.tile(swapped, (1, 4))]

    def rotary_tables():
        inv = (1.0 / _np.power(_np.float32(10000.0), _np.arange(0, 32, 2, dtype=_np.float32) / _np.float32(32))
               ).astype(_np.float32)
        angle = _np.outer(_np.arange(1024, dtype=_np.float32), inv).astype(_np.float32).T
        cos, sin = _np.cos(angle), _np.sin(angle)
        return _np.stack([_np.tile(_np.concatenate([cos, cos]), (4, 1)),
                          _np.tile(_np.concatenate([-sin, sin]), (4, 1))], axis=1).astype(_np.float32)

    def part_columns():
        c = _np.zeros((128, 12), _np.float32)
        row = _np.arange(128)
        for at, rest in ((2, row // 32 == 1), (4, row // 32 == 2),
                         (6, row % 32 // 8 == 1), (8, row % 32 // 8 == 2)):
            c[:, at] = rest
            c[:, at + 1] = _np.where(rest, -1.0, 1.0)
        c[:, 10] = row % 32 == 24
        return c

    def masks():
        later = _np.triu(_np.ones((128, 128), _np.float32), 1)
        return _np.stack([later, later.T], axis=1) * _np.float32(MASKED)

    wq, wk, wv = i["L0_attn_wq"], i["L0_attn_wk"], i["L0_attn_wv"]
    w1 = _np.concatenate([i["L1_ffn_We1"], i["L1_ffn_Ws1"][None]])
    w2 = _np.concatenate([i["L1_ffn_We2"], i["L1_ffn_Ws2"][None]])
    b1 = _np.concatenate([i["L1_ffn_be1"], i["L1_ffn_bs1"][None]])
    arrays = {
        "x": i["L0_attn_z"].reshape(2048, 128),
        "ident": _np.eye(128, dtype=_np.float32),
        "wl": _np.concatenate([wq, wq, wk, wk, wv], axis=1),
        "fq": twice(i["L0_attn_fcq_w"]).reshape(128, h, dk),
        "fk": twice(i["L0_attn_fck_w"]).reshape(128, h, dk),
        "fv_t": i["L0_attn_fcv_w"].reshape(dk, h, dk).transpose(2, 1, 0),
        "fo": i["L0_attn_fco_w"].reshape(h, dk, 128).transpose(1, 0, 2),
        "bv": i["L0_attn_fcv_b"].reshape(h, dk).T,
        "bo": i["L0_attn_fco_b"].reshape(128, 1),
        "qk_bias": qk_columns(),
        "router": i["L0_ffn_router_w"].T,
        "iota": _np.tile(_np.arange(8, dtype=_np.float32), (128, 1)),
        "up": i["L0_ffn_up_proj"].transpose(1, 0, 2),
        "down": i["L0_ffn_down_proj"].transpose(1, 0, 2),
        "wkv": i["L1_attn_W_kv_down"],
        "wv1": i["L1_attn_W_v_up"],
        "wrope": _np.stack(rotary_columns(i["L1_attn_W_k_rope"]) + rotary_columns(i["L1_attn_W_q_rope"]), axis=1),
        "cs": rotary_tables(),
        "masks": masks(),
        "coef": part_columns(),
        "wk1": head_columns(i["L1_attn_W_k_up"]),
        "wq1": head_columns(i["L1_attn_W_q"]),
        "wo": i["L1_attn_W_o"],
        "wr1": i["L1_ffn_Wr1"],
        "br1": i["L1_ffn_br1"].reshape(32, 1),
        "wr2": i["L1_ffn_Wr2"],
        "br2": _np.tile(i["L1_ffn_br2"], (128, 1)),
        "w1": w1.transpose(1, 0, 2).reshape(128, 36, 128),
        "w2": w2.reshape(36, 128, 128).transpose(1, 0, 2),
        "b1": b1.reshape(36, 128).T,
        "b2": _np.concatenate([i["L1_ffn_be2"], i["L1_ffn_bs2"][None]]),
    }
    nc = _bacc.Bacc("TRN2", target_bir_lowering=False, num_devices=1)
    ins, feed = {}, {}
    for name, a in arrays.items():
        a = _np.ascontiguousarray(a)
        feed["in_" + name] = a
        ins[name] = nc.dram_tensor("in_" + name, a.shape, _mybir.dt.float32, kind="ExternalInput").ap()
    ins["sums"] = nc.dram_tensor("scratch_sums", (4, 512), _mybir.dt.float32, kind="Internal").ap()
    for n in range(2):
        ins[f"gates{n}"] = nc.dram_tensor(f"scratch_gates{n}", (8, 2048), _mybir.dt.float32, kind="Internal").ap()
    ins["out"] = nc.dram_tensor("out_x", (2048, 128), _mybir.dt.float32, kind="ExternalOutput").ap()
    build(nc, ins)
    r = _run(nc, [feed], core_ids=[0])
    return r.results[0]["out_x"].reshape(2, 1024, 128)
```

```python
import numpy as np
from contextlib import ExitStack
import concourse.bass as bass
from concourse import mybir

F32 = mybir.dt.float32
F32R = mybir.dt.float32r
U32 = mybir.dt.uint32
ACT = mybir.ActivationFunctionType
ALU = mybir.AluOpType
AX = mybir.AxisListType
ds, ts = bass.ds, bass.ts

P = 128
E = 128
B, T = 2, 1024
N = B * T
NT = N // P
TT = T // P
BLK = 512
NBLK = N // BLK
TPB = BLK // P
EPS = 1e-5

NEXP, TOPK = 8, 2

H0, D0 = 16, 64
PAIRS = H0 // 2
STEPS0 = B * PAIRS

H1, D1, DR = 16, 8, 32
QUADS = H1 // 4
STEPS1 = B * QUADS
SCALE1 = float(D1 + DR) ** -0.5
MASKED = -1e30

HID1 = 512
CH = HID1 // P


class Mem:
    pass


def layernorm_block(nc, v, m, j, x_block, base):
    for t in range(TPB):
        ins = nc.vector.bn_stats(m.stats[:, t, :], x_block(t))
    ins.then_inc(m.ln_step, 1)
    v.wait_ge(m.ln_step, base + 1)
    for t in range(TPB):
        ins = nc.vector.bn_aggr(m.mv[:, t, :], m.stats[:, t, :])
    ins.then_inc(m.ln_step, 1)
    v.wait_ge(m.ln_step, base + 2)
    v.wait_ge(m.std_ready, j + 1)
    nc.vector.reciprocal(m.rstd[:, :], m.std[:, :]).then_inc(m.ln_step, 1)
    v.wait_ge(m.ln_step, base + 3)


def deviation_block(nc, act, m, j):
    act.wait_ge(m.ln_step, 3 * j + 2)
    nc.scalar.activation(m.std[:, :], m.mv[:, :, 1], ACT.Sqrt, bias=m.eps[:, 0:1]).then_inc(m.std_ready, 1)


def normalise_block(nc, m, x_block):
    for t in range(TPB):
        ins = nc.vector.tensor_scalar(m.xn[:, t, :], x_block(t), m.mv[:, t, 0:1], m.rstd[:, t:t + 1],
                                      ALU.subtract, ALU.mult)
    return ins


def l0_prologue(nc, m, d):
    with ExitStack() as ctx:
        def sb(name, shape, dt=F32):
            return ctx.enter_context(nc.sbuf_tensor(name, shape, dt))

        def pb(name, shape):
            return ctx.enter_context(nc.psum_tensor(name, shape, F32))

        wl = sb("wl", [P, 5 * D0])
        fq = sb("fq", [P, H0, D0])
        fk = sb("fk", [P, H0, D0])
        fv_t = sb("fv_t", [D0, H0, D0])
        fo = sb("fo", [D0, H0, E])
        bv = sb("bv", [D0, H0])
        bo = sb("bo", [P, 1])
        m.stats = sb("stats0", [P, TPB, 6])
        m.mv = sb("mv0", [P, TPB, 2])
        m.rstd = sb("rstd0", [P, TPB])
        m.std = sb("std0", [P, TPB])
        m.xn = sb("xn0", [P, TPB, E])
        xt = sb("xt0", [P, BLK])
        tr = pb("tr0", [P, BLK])
        lat = [pb(f"lat{i}", [P, BLK]) for i in range(2)]
        vlat = pb("vlat", [P, TPB, P])
        gp = pb("gp", [P, PAIRS, E])
        cp = pb("cp", [P, 1])

        def sem(name):
            return m.ctx.enter_context(nc.semaphore(name))

        x_in, w_in, const_in = sem("x_in"), sem("w_in"), sem("const_in")
        m.ln_step, m.std_ready = sem("ln_step0"), sem("std_ready0")
        eps_set = sem("eps_set")
        xn_ready, transposed, xt_ready = sem("xn_ready0"), sem("transposed0"), sem("xt_ready0")
        lat_filled, hi_done, lat_read = sem("lat_filled"), sem("lat_hi"), sem("lat_read")
        vlat_filled, vlat_read = sem("vlat_filled"), sem("vlat_read")
        g_filled, w_split = sem("g_filled"), sem("w_split")
        block = ctx.enter_context(nc.Block())

        @block.sync
        def _(sp):
            for j in range(NBLK):
                sp.dma_start(m.x[:, TPB * j:TPB * (j + 1), :],
                             d["x"][BLK * j:BLK * (j + 1), :].rearrange("(t p) e -> p t e", p=P)).then_inc(x_in, 16)
            sp.dma_start(m.ident[:, :], d["ident"]).then_inc(const_in, 16)
            sp.dma_start(wl[:, :], d["wl"]).then_inc(const_in, 16)
            for dst, src in ((fq, d["fq"]), (fk, d["fk"]), (fv_t, d["fv_t"]), (fo, d["fo"])):
                sp.dma_start(dst[:, :, :], src).then_inc(w_in, 16)
            for dst, src in ((bv, d["bv"]), (bo, d["bo"]), (m.qk_bias, d["qk_bias"])):
                sp.dma_start(dst[:, :], src).then_inc(w_in, 16)
            sp.wait_ge(w_in, 16 * 7)

        @block.vector
        def _(v):
            for j in range(NBLK):
                def x_block(t):
                    return m.x[:, TPB * j + t, :]

                v.wait_ge(x_in, 16 * NBLK)
                layernorm_block(nc, v, m, j, x_block, 3 * j)
                if j:
                    v.wait_ge(transposed, j)
                normalise_block(nc, m, x_block).then_inc(xn_ready, 1)
                for n, dst in enumerate((m.aq, m.ak)):
                    v.wait_ge(hi_done, 2 * j + n + 1)
                    nc.vector.tensor_tensor(dst[D0:P, ds(BLK * j, BLK)], lat[n][D0:P, :],
                                            dst[D0:P, ds(BLK * j, BLK)], ALU.subtract).then_inc(lat_read, 1)
            v.wait_ge(w_in, 16 * 7)
            for n, src in enumerate((fq, fk)):
                nc.vector.tensor_copy(m.w_all[:, :, 2 * n, :], src[:, :, :]).then_inc(w_split, 1)
                v.wait_ge(w_split, 2 * n + 1)
                nc.vector.tensor_tensor(m.w_all[:, :, 2 * n + 1, :], src[:, :, :], m.w_all[:, :, 2 * n, :],
                                        ALU.subtract).then_inc(w_split, 1)
            v.wait_ge(g_filled, 1)
            nc.vector.tensor_copy(m.g_all[:, :, :], gp[:, :, :])
            nc.vector.tensor_tensor(m.out_bias[:, :], cp[:, :], bo[:, :], ALU.add)

        @block.gpsimd
        def _(pool):
            nc.gpsimd.memset(m.eps[:, :], EPS).then_inc(eps_set, 1)

        @block.scalar
        def _(act):
            act.wait_ge(eps_set, 1)
            for j in range(NBLK):
                deviation_block(nc, act, m, j)
                act.wait_ge(transposed, j + 1)
                if j:
                    act.wait_ge(vlat_filled, j)
                nc.scalar.copy(xt[:, :], tr[:, :]).then_inc(xt_ready, 1)
                for n, dst in enumerate((m.aq, m.ak)):
                    act.wait_ge(lat_filled, 2 * j + n + 1)
                    nc.scalar.copy(dst[:, ds(BLK * j, BLK)], lat[n][:, :]).then_inc(hi_done, 1)
                act.wait_ge(vlat_filled, j + 1)
                nc.scalar.copy(m.c_all[:, ds(TPB * j, TPB), :], vlat[:, :, 0:D0]).then_inc(vlat_read, 1)

        @block.tensor
        def _(pe):
            pe.wait_ge(const_in, 32)
            for j in range(NBLK):
                pe.wait_ge(xn_ready, j + 1)
                if j:
                    pe.wait_ge(xt_ready, j)
                for t in range(TPB):
                    ins = nc.tensor.transpose(tr[:, ts(t, P)], m.xn[:, t, :], m.ident[:, :])
                ins.then_inc(transposed, 1)
                pe.wait_ge(xt_ready, j + 1)
                for n in range(2):
                    if j:
                        pe.wait_ge(lat_read, 2 * (j - 1) + n + 1)
                    nc.tensor.matmul(lat[n][:, :], wl[:, 2 * D0 * n:2 * D0 * (n + 1)], xt[:, :],
                                     start=True, stop=True).then_inc(lat_filled, 1)
                if j:
                    pe.wait_ge(vlat_read, j)
                for t in range(TPB):
                    ins = nc.tensor.matmul(vlat[:, t, 0:D0], xt[:, ts(t, P)], wl[:, 4 * D0:5 * D0],
                                           start=True, stop=True)
                ins.then_inc(vlat_filled, 1)
            pe.wait_ge(w_in, 16 * 7)
            for h in range(H0):
                lo = D0 * (h % 2)
                nc.tensor.matmul(gp[lo:lo + D0, h // 2, :], fv_t[:, h, :], fo[:, h, :], start=True, stop=True)
            for h in range(H0):
                ins = nc.tensor.matmul(cp[:, :], fo[:, h, :], bv[:, h:h + 1], start=(h == 0), stop=(h == H0 - 1))
            ins.then_inc(g_filled, 1)


def s_units(hh, first, last):
    return [("s", hh, u) for u in range(first, last)]


WITH_FINISH = ([("q", 0, 0), ("q", 0, 1), ("k", 0, 0), ("k", 0, 1), ("q", 1, 0), ("q", 1, 1)]
               + s_units(0, 0, 3) + [("k", 1, 0)] + s_units(0, 3, 4) + [("k", 1, 1), ("l", 0, 0)]
               + s_units(0, 4, 11) + [("r", 0, 0)] + s_units(0, 11, 16) + s_units(1, 0, 1) + [("m", 0, 0)]
               + s_units(1, 1, 4) + [("n", 0, 0)] + s_units(1, 4, 6) + [("g", 0, 0)] + s_units(1, 6, 8)
               + [("g", 0, 1)] + s_units(1, 8, 16) + [("m", 1, 0)])
NEXT_UNITS = [u for u in WITH_FINISH if u[0] in "qksm"]
FINISH_ONLY = [u for u in WITH_FINISH if u[0] in "lrng"]


def psum_units(units):
    return [u for u in units if u[0] not in "rn"]


def position(units, kind, hh, j):
    return psum_units(units).index((kind, hh, j))


N_NEXT, N_STEP = len(psum_units(NEXT_UNITS)), len(psum_units(WITH_FINISH))


def script(units, first):
    left = list(units)
    out = []

    def units_after(n):
        while n and left:
            unit = left.pop(0)
            out.append(("UNIT",) + unit)
            n -= unit[0] not in "rn"

    for kt in range(TT):
        for part in (("ST", kt, 0, 0), ("ST", kt, 0, 1), ("ST", kt, 1, 0), ("ST", kt, 1, 1),
                     ("PV", kt - 1, 0), ("PV", kt - 1, 1)):
            if part[0] == "ST" or kt or not first:
                out.append(part)
                if len(units) > len(FINISH_ONLY):
                    units_after(2 if part[0] == "PV" and part[2] and kt % 2 else 1)
                elif kt % 2 and part[:1] + part[2:] == ("ST", 0, 0):
                    units_after(1)
    units_after(len(left))
    return out


def units_before(n):
    return N_NEXT if isinstance(n, int) and n == 0 else 2 * N_NEXT + N_STEP * (n - 1)


def l0_attention(nc, m, d):
    with ExitStack() as ctx:
        def sb(name, shape, dt=F32):
            return ctx.enter_context(nc.sbuf_tensor(name, shape, dt))

        def sem(name):
            return m.ctx.enter_context(nc.semaphore(name))

        R2 = range(2)
        kk = [[sb(f"kk{a}{h}", [P, T], F32R) for h in R2] for a in R2]
        k2 = [[sb(f"k2_{a}{h}", [P, T], F32R) for h in R2] for a in R2]
        qq = [[sb(f"qq{a}{h}", [P, T], F32R) for h in R2] for a in R2]
        q2 = [[sb(f"q2_{a}{h}", [P, T], F32R) for h in R2] for a in R2]
        w = [sb(f"w{a}", [P, 2, 4, 2, D0], F32R) for a in R2]
        bias = [sb(f"bias{a}", [P, 4]) for a in R2]
        c = [sb(f"c{a}", [P, TT, D0]) for a in R2]
        g = sb("g", [P, E])
        prob = [sb(f"prob{s}", [P, 2, T]) for s in range(4)]
        psum_k = sb("psum_k", [P, 2, T])
        ut = sb("ut", [P, T])
        rsum = sb("rsum", [P, BLK])
        sums_c = sb("sums_c", [P, 2 * T // P])
        inv_c = sb("inv_c", [P, 2 * T // P])
        rb = sb("rb", [P, T])
        on = sb("on", [P, T])
        ones = sb("ones", [P, 32])
        mx = sb("mx", [P, 2, TT, 2])
        mmax = sb("mmax", [P, 2, TT])
        negm = sb("negm", [P, 2, TT])
        mrow = [sb(f"mrow{h}", [TT, P], F32R) for h in R2]
        st = [ctx.enter_context(nc.psum_tensor(f"st{h}", [P, T], F32)) for h in R2]
        pv = ctx.enter_context(nc.psum_tensor("pv", [P, T], F32))
        work = [ctx.enter_context(nc.psum_tensor(f"work{h}", [P, BLK], F32)) for h in R2]

        cleared = sem("cleared")
        w_loaded, c_loaded = [sem(f"w_loaded{a}") for a in R2], [sem(f"c_loaded{a}") for a in R2]
        row_loaded = [sem(f"row_loaded{h}") for h in R2]
        g_loaded, r_stored, r_loaded = sem("g_loaded"), sem("r_stored"), sem("r_loaded")
        sums_spread, inv_ready = sem("sums_spread"), sem("inv_ready")
        filled, read = sem("work_filled"), sem("work_read")
        hi_done, negm_ready, mmax_ready = sem("hi_done"), sem("negm_ready"), sem("mmax_ready")
        st_filled, exp_done, pv_done, ut_ready = sem("st_filled"), sem("exp_done"), sem("pv_done"), sem("ut_ready")
        summed, norm_done = sem("summed"), sem("norm_done")
        block = ctx.enter_context(nc.Block())

        def steps(eng, step):
            step(0, 0, True, False)
            with eng.Fori(0, (STEPS0 - 2) // 2) as i:
                step(2 * i + 1, 1, False, False)
                step(2 * i + 2, 0, False, False)
            step(STEPS0 - 1, 1, False, True)

        def units_of(first, last):
            return NEXT_UNITS if first else FINISH_ONLY if last else WITH_FINISH

        def psum_unit(n, par, first, seen):
            even = 0 if first else (1 + par) % 2
            return units_before(n) + seen, work[(even + seen) % 2]

        def load_pair(sp, k, par):
            for copy in R2:
                sp.dma_start(w[par][:, :, :, copy, :].bitcast(F32),
                             m.w_all[:, ds(2 * (k % PAIRS), 2), :, :].bitcast(F32)).then_inc(w_loaded[par], 16)
            sp.dma_start(bias[par][:, :], m.qk_bias[:, ds(4 * (k % PAIRS), 4)]).then_inc(w_loaded[par], 16)

        def load_values(sp, k, par):
            sp.dma_start(c[par][:, :, :], m.c_all[:, ds(TT * (k // PAIRS), TT), :]).then_inc(c_loaded[par], 16)

        def sp_rows(sp, k, par, hh, u):
            sp.wait_ge(read, u + 1)
            sp.dma_start(q2[par][hh][0:1, :].bitcast(F32), mrow[hh][:, :].bitcast(F32)).then_inc(row_loaded[hh], 16)

        def sp_sums(sp, k, u):
            sp.wait_ge(read, u + 1)
            sp.dma_start(sums_c[:, :], rsum[0:P:32, :]).then_inc(sums_spread, 16)
            sp.wait_ge(inv_ready, k + 1)
            sp.dma_start(d["sums"].rearrange("a (p f) -> (a p) f", f=2 * T // P), inv_c[:, :]).then_inc(r_stored, 16)
            sp.wait_ge(r_stored, 16 * (k + 1))
            for hh in R2:
                sp.dma_start(rb[D0 * hh:D0 * (hh + 1), :],
                             d["sums"][2 * hh:2 * hh + 2, :].rearrange("a n -> (a n)").partition_broadcast(D0)
                             ).then_inc(r_loaded, 16)

        @block.sync
        def _(sp):
            load_pair(sp, 0, 0)
            load_values(sp, 0, 0)
            load_pair(sp, 1, 1)

            def rows_of(k, par, units, base):
                seen = 0
                for kind, hh, j in units:
                    if kind == "m":
                        sp_rows(sp, k, par, hh, base + seen)
                    seen += kind not in "rn"

            sp.wait_ge(cleared, 2)
            rows_of(0, 0, NEXT_UNITS, 0)

            def step(n, par, first, last):
                base = units_before(n)
                if not last:
                    sp.wait_ge(read, base)
                    load_pair(sp, n + 2, par)
                    if not first:
                        sp.wait_ge(pv_done, TT * n)
                    load_values(sp, n + 1, 1 - par)
                if not first:
                    if last:
                        sp.wait_ge(read, base)
                    sp.dma_start(g[:, :], m.g_all[:, (n - 1) % PAIRS, :]).then_inc(g_loaded, 16)
                    sp_sums(sp, n - 1, base + position(units_of(first, last), "l", 0, 0))
                if not last:
                    rows_of(n + 1, 1 - par, units_of(first, last), base)

            steps(sp, step)
            sp.wait_ge(read, units_before(STEPS0 - 1) + 3)
            sp.dma_start(g[:, :], m.g_all[:, PAIRS - 1, :]).then_inc(g_loaded, 16)
            sp_sums(sp, STEPS0 - 1, units_before(STEPS0 - 1) + 3)
            for a in R2:
                sp.wait_ge(w_loaded[a], 48 * (STEPS0 // 2) + 48 * (a == 0))
                sp.wait_ge(c_loaded[a], 16 * (STEPS0 // 2))
            sp.wait_ge(r_loaded, 32 * STEPS0)

        @block.gpsimd
        def _(pool):
            for a in R2:
                for h in R2:
                    nc.gpsimd.memset(k2[a][h][0:D0, :].bitcast(F32), 0.0)
                    ins = nc.gpsimd.memset(q2[a][h][0:D0, :].bitcast(F32), 0.0)
            ins.then_inc(cleared, 1)
            pool.wait_ge(cleared, 1)
            for a in R2:
                for h in R2:
                    ins = nc.gpsimd.memset(k2[a][h][0:1, :].bitcast(F32), 1.0)
            nc.gpsimd.memset(ones[:, :], 1.0)
            nc.gpsimd.memset(m.out_t[:, :], 0.0).then_inc(cleared, 1)

            def step(n, par, first, last):
                per = 2 * (TT - 1)
                for kt in range(1, TT):
                    for hh in R2:
                        pool.wait_ge(exp_done, 2 * TT * n + 2 * kt + hh + 1)
                        if kt == 1 and hh == 0 and not first:
                            pool.wait_ge(filled, units_before(n) + position(units_of(first, last), "l", 0, 0) + 1)
                        if kt == 1:
                            nc.gpsimd.tensor_tensor(psum_k[:, hh, :], prob[0][:, hh, :], prob[1][:, hh, :],
                                                    ALU.add).then_inc(summed, 1)
                        else:
                            pool.wait_ge(summed, per * n + 2 * (kt - 1) + hh - 1)
                            nc.gpsimd.tensor_tensor(psum_k[:, hh, :], psum_k[:, hh, :], prob[kt % 4][:, hh, :],
                                                    ALU.add).then_inc(summed, 1)

            steps(pool, step)

        @block.scalar
        def _(act):
            def proj_evac(kind, j, buf, par, hh):
                b = bias[par][:, 2 * hh + (kind == "k"):2 * hh + (kind == "k") + 1]
                cols = ts(j, BLK)
                if kind == "q":
                    nc.scalar.activation(qq[par][hh][:, cols], buf[:, :], ACT.Identity, bias=b
                                         ).then_inc(hi_done, 1)
                else:
                    nc.scalar.activation(k2[par][hh][D0:P, cols], buf[D0:P, :], ACT.Identity, bias=b[D0:P, :]
                                         ).then_inc(hi_done, 1)

            def run(n, par, first, last, todo, base, even):
                seen = 0
                for what, kind, hh, *j in [t + (0,) * (4 - len(t)) for t in todo]:
                    if what == "UNIT":
                        if kind in "qk":
                            act.wait_ge(filled, base + seen + 1)
                            proj_evac(kind, j[0], work[(even + seen) % 2], 1 - par, hh)
                        seen += kind not in "rn"
                    elif what == "PV" and kind < 0 and hh:
                        act.wait_ge(pv_done, TT * n)
                        act.wait_ge(read, base)
                        nc.scalar.copy(ut[:, :], pv[:, :]).then_inc(ut_ready, 1)
                    elif what == "ST" and j[0]:
                        kt = kind
                        at = 2 * TT * n + 2 * kt + hh
                        act.wait_ge(st_filled, at + 1)
                        if not (first and kt < 4):
                            act.wait_ge(pv_done, TT * n + kt - 3)
                            if kt >= 4:
                                act.wait_ge(summed, 14 * n + 2 * max(kt - 4, 1) )
                            else:
                                act.wait_ge(summed, 14 * (n - 1) + 2 * (kt + 4))
                        nc.scalar.activation(prob[kt % 4][:, hh, :], st[hh][:, :], ACT.Exp, scale=D0 ** -0.5
                                             ).then_inc(exp_done, 1)

            act.wait_ge(w_loaded[0], 48)
            run(-1, 1, True, False, [("UNIT",) + u for u in NEXT_UNITS], 0, 0)

            def step(n, par, first, last):
                if not last:
                    act.wait_ge(w_loaded[1 - par], 48 * ((n + 1) // 2 + 1))
                run(n, par, first, last, script(units_of(first, last), first), units_before(n),
                    0 if first else (1 + par) % 2)

            steps(act, step)
            act.wait_ge(pv_done, TT * STEPS0)
            act.wait_ge(norm_done, STEPS0 - 1)
            nc.scalar.copy(ut[:, :], pv[:, :]).then_inc(ut_ready, 1)

        @block.vector
        def _(v):
            def unit(kind, hh, j, u, buf, par, k):
                cols = ts(j, BLK)
                if kind in "qk":
                    dst, hi = (q2, qq) if kind == "q" else (kk, k2)
                    b = bias[par][D0:P, 2 * hh + (kind == "k"):2 * hh + (kind == "k") + 1]
                    v.wait_ge(hi_done, 8 * k + 4 * hh + 2 * (kind == "k") + j + 1)
                    if kind == "k":
                        nc.vector.tensor_copy(kk[par][hh][0:D0, cols],
                                              k2[par][hh][D0:P, cols].bitcast(F32))
                    nc.vector.scalar_tensor_tensor(dst[par][hh][D0:P, cols], buf[D0:P, :], b,
                                                   hi[par][hh][D0:P, cols], ALU.add, ALU.subtract
                                                   ).then_inc(read, 1)
                elif kind == "s":
                    v.wait_ge(filled, u + 1)
                    nc.vector.reduce_max(mx[:, hh, j // 2, j % 2:j % 2 + 1], buf[:, :], AX.X).then_inc(read, 1)
                elif kind == "m":
                    if not (isinstance(k, int) and k == 0):
                        v.wait_ge(row_loaded[hh], 16 * k)
                    v.wait_ge(filled, u + 1)
                    nc.vector.tensor_copy(mrow[hh][:, :], buf[0:TT, 0:P]).then_inc(read, 1)
                elif kind == "l":
                    v.wait_ge(filled, u + 1)
                    nc.vector.tensor_copy(rsum[:, :], buf[:, :]).then_inc(read, 1)
                elif kind == "g":
                    v.wait_ge(filled, u + 1)
                    out = m.out_t[:, ds(T * (k // PAIRS) + BLK * j, BLK)]
                    nc.vector.tensor_tensor(out, buf[:, :], out, ALU.add).then_inc(read, 1)

            def combine(hh, k, u_last):
                v.wait_ge(read, u_last + 1)
                nc.vector.tensor_tensor(mmax[:, hh, :], mx[:, hh, :, 0], mx[:, hh, :, 1], ALU.max
                                        ).then_inc(mmax_ready, 1)
                v.wait_ge(mmax_ready, 2 * k + hh + 1)
                nc.vector.tensor_scalar(negm[:, hh, :], mmax[:, hh, :], -1.0, None, ALU.mult
                                        ).then_inc(negm_ready, 1)

            def normalise(k):
                v.wait_ge(r_loaded, 32 * (k + 1))
                v.wait_ge(ut_ready, k + 1)
                nc.vector.tensor_tensor(on[:, :], ut[:, :], rb[:, :], ALU.mult).then_inc(norm_done, 1)

            def run(n, par, units, base, even):
                seen = 0
                for kind, hh, j in units:
                    k = n - 1 if kind in "lrng" else n + 1
                    if kind == "r":
                        v.wait_ge(sums_spread, 16 * (k + 1))
                        nc.vector.reciprocal(inv_c[:, :], sums_c[:, :]).then_inc(inv_ready, 1)
                        continue
                    if kind == "n":
                        normalise(k)
                        continue
                    unit(kind, hh, j, base + seen, work[(even + seen) % 2], 1 - par, k)
                    if kind == "s" and j == 2 * TT - 1:
                        combine(hh, k, base + seen)
                    seen += 1

            v.wait_ge(cleared, 2)
            run(-1, 1, NEXT_UNITS, 0, 0)

            def step(n, par, first, last):
                run(n, par, units_of(first, last), units_before(n), 0 if first else (1 + par) % 2)

            steps(v, step)
            run(STEPS0, 0, FINISH_ONLY, units_before(STEPS0 - 1) + 3, 1)

        @block.tensor
        def _(pe):
            def unit(kind, hh, j, u, buf, par, k, proj_end):
                if not (isinstance(u, int) and u < 2):
                    pe.wait_ge(read, u - 1)
                if kind in "qk":
                    src, part = (m.aq, 0) if kind == "q" else (m.ak, 2)
                    cols = ds(T * (k // PAIRS) + BLK * j, BLK)
                    nc.tensor.matmul(buf[:, :], w[par][:, hh, part, :, :].rearrange("p a d -> p (a d)"), src[:, cols],
                                     start=True, stop=False)
                    ins = nc.tensor.matmul(buf[:, :], w[par][:, hh, part + 1, :, :].rearrange("p a d -> p (a d)"), src[:, cols],
                                           start=False, stop=True)
                elif kind == "s":
                    if j == 0:
                        pe.wait_ge(read, proj_end)
                    ins = nc.tensor.matmul(buf[:, :], qq[par][hh][:, ts(j // 2, P)], kk[par][hh][:, ts(j % 2, BLK)],
                                           start=True, stop=True)
                elif kind == "m":
                    pe.wait_ge(negm_ready, 2 * k + hh + 1)
                    ins = nc.tensor.matmul(buf[0:TT, 0:P], negm[:, hh, :], m.ident[:, :], start=True, stop=True)
                elif kind == "l":
                    pe.wait_ge(summed, 14 * (k + 1))
                    for q in range(4):
                        ins = nc.tensor.matmul(buf[32 * q:32 * (q + 1), :], ones[:, :],
                                               psum_k[:, q // 2, ts(q % 2, BLK)], start=True, stop=True)
                elif kind == "g":
                    pe.wait_ge(norm_done, k + 1)
                    pe.wait_ge(g_loaded, 16 * (k + 1))
                    ins = nc.tensor.matmul(buf[:, :], g[:, :], on[:, ts(j, BLK)], start=True, stop=True)
                ins.then_inc(filled, 1)

            def run(n, par, todo, base, even, first, units):
                seen = 0
                for what, *rest in todo:
                    if what == "UNIT":
                        kind, hh, j = rest
                        if kind not in "rn":
                            unit(kind, hh, j, base + seen, work[(even + seen) % 2], 1 - par,
                                 n - 1 if kind in "lg" else n + 1,
                                 base + position(units, "k", hh, 1) + 1 if kind == "s" else None)
                            seen += 1
                    elif what == "ST":
                        kt, hh, j = rest
                        at = 2 * TT * n + 2 * kt + hh
                        if j == 0 and not (first and kt == 0):
                            pe.wait_ge(exp_done, at - 1)
                        if kt == 0 and j == 0:
                            pe.wait_ge(row_loaded[hh], 16 * (n + 1))
                        for part, (ka, qa) in enumerate(((kk, qq), (k2, q2))):
                            ins = nc.tensor.matmul(st[hh][:, ts(j, BLK)], ka[par][hh][:, ts(kt, P)],
                                                   qa[par][hh][:, ts(j, BLK)],
                                                   start=(part == 0), stop=(part == 1))
                        if j:
                            ins.then_inc(st_filled, 1)
                    else:
                        kt, j = rest
                        if j == 0:
                            pe.wait_ge(exp_done, 2 * TT * n + 2 * kt + 2)
                        if kt == 0 and j == 0:
                            pe.wait_ge(c_loaded[par], 16 * (n // 2 + 1))
                            if not first:
                                pe.wait_ge(ut_ready, n)
                        product(kt % TT, j, par if kt >= 0 else 1 - par)

            def product(kt, j, par):
                for hh in R2:
                    ins = nc.tensor.matmul(pv[D0 * hh:D0 * (hh + 1), ts(j, BLK)], c[par][:, kt, :],
                                           prob[kt % 4][:, hh, ts(j, BLK)],
                                           start=(kt == 0), stop=(kt == TT - 1))
                if j:
                    ins.then_inc(pv_done, 1)

            pe.wait_ge(w_loaded[0], 48)
            pe.wait_ge(cleared, 2)
            run(-1, 1, [("UNIT",) + u for u in NEXT_UNITS], 0, 0, True, NEXT_UNITS)

            def step(n, par, first, last):
                if not last:
                    pe.wait_ge(w_loaded[1 - par], 48 * ((n + 1) // 2 + 1))
                units = units_of(first, last)
                run(n, par, script(units, first), units_before(n), 0 if first else (1 + par) % 2, first, units)

            steps(pe, step)
            pe.wait_ge(exp_done, 2 * TT * STEPS0)
            for j in range(2):
                product(TT - 1, j, (STEPS0 - 1) % 2)
            run(STEPS0, 0, [("UNIT",) + u for u in FINISH_ONLY], units_before(STEPS0 - 1) + 3, 1, False, FINISH_ONLY)


def residual_out(nc, m, d):
    with ExitStack() as ctx:
        ob = ctx.enter_context(nc.sbuf_tensor("ob", [P, BLK], F32))
        tr = ctx.enter_context(nc.psum_tensor("trr", [P, TPB, P], F32))

        def sem(name):
            return m.ctx.enter_context(nc.semaphore(name))
        ob_ready, transposed, added = sem("ob_ready"), sem("tr_r"), sem("added_r")
        block = ctx.enter_context(nc.Block())

        @block.scalar
        def _(act):
            for j in range(NBLK):
                if j:
                    act.wait_ge(transposed, j)
                nc.scalar.activation(ob[:, :], m.out_t[:, ts(j, BLK)], ACT.Identity, bias=m.out_bias[:, 0:1]
                                     ).then_inc(ob_ready, 1)

        @block.tensor
        def _(pe):
            for j in range(NBLK):
                pe.wait_ge(ob_ready, j + 1)
                if j:
                    pe.wait_ge(added, j)
                for t in range(TPB):
                    ins = nc.tensor.transpose(tr[:, t, :], ob[:, ts(t, P)], m.ident[:, :])
                ins.then_inc(transposed, 1)

        @block.vector
        def _(v):
            for j in range(NBLK):
                v.wait_ge(transposed, j + 1)
                xs = m.x[:, TPB * j:TPB * (j + 1), :]
                nc.vector.tensor_tensor(xs, tr[:, :, :], xs, ALU.add).then_inc(added, 1)


def router(nc, m, d, layer, w_dram, w1_dram, b1_dram, b2_dram):
    L = str(layer)
    with ExitStack() as ctx:
        def sb(name, shape, dt=F32):
            return ctx.enter_context(nc.sbuf_tensor(name + "_r" + L, shape, dt))

        def sem(name):
            return m.ctx.enter_context(nc.semaphore(name + "_r" + L))

        wr = sb("wr", [P if layer == 0 else HR, NEXP])
        if layer == 1:
            wr1 = sb("wr1", [P, HR])
            br1 = sb("br1", [HR, 1])
            br2 = sb("br2", [P, NEXP])
            hr = sb("hr", [HR, N])
        iota = sb("iota", [P, NEXP])
        m.stats = sb("stats", [P, TPB, 6])
        m.mv = sb("mv", [P, TPB, 2])
        m.rstd = sb("rstd", [P, TPB])
        m.std = sb("std", [P, TPB])
        m.xn = sb("xn", [P, TPB, E])
        shape = [P, NT, NEXP]
        lg, ex, probs, top, oh, gate = (sb(n, shape) for n in ("lg", "ex", "probs", "top", "oh", "gate"))
        idx = sb("idx", shape, U32)
        idxf = sb("idxf", [P, NT, TOPK])
        col = sb("col", [P, 8, NT])
        tr = ctx.enter_context(nc.psum_tensor("tr_r" + L, [P, BLK], F32))
        hp = ctx.enter_context(nc.psum_tensor("hp_r" + L, [P, BLK], F32))
        lp = ctx.enter_context(nc.psum_tensor("lp_r" + L, [P, NT, NEXP], F32))
        gp = ctx.enter_context(nc.psum_tensor("gp_r" + L, [P, N], F32))
        loaded, m.ln_step, m.std_ready = sem("loaded"), sem("ln_step"), sem("std_ready")
        xn_ready, transposed, xt_ready = sem("xn_ready"), sem("transposed"), sem("xt_ready")
        hid_filled, hid_ready, logits_done = sem("hid_filled"), sem("hid_ready"), sem("logits_done")
        step, shifted, exp_done, gate_ready = sem("step"), sem("shifted"), sem("exp_done"), sem("gate_ready")
        rows_filled, rows_ready, stored, spread = sem("rows_filled"), sem("rows_ready"), sem("stored"), sem("spread")
        block = ctx.enter_context(nc.Block())
        n_loads = 2 if layer == 0 else 5

        @block.sync
        def _(sp):
            sp.dma_start(wr[:, :], w_dram).then_inc(loaded, 16)
            sp.dma_start(iota[:, :], d["iota"]).then_inc(loaded, 16)
            if layer == 1:
                for dst, src in ((wr1, w1_dram), (br1, b1_dram), (br2, b2_dram)):
                    sp.dma_start(dst[:, :], src).then_inc(loaded, 16)
            m.load_experts(sp)
            sp.wait_ge(rows_ready, 2)
            gates = d["gates0"] if layer == 0 else d["gates1"]
            sp.dma_start(gates, m.gate_t[0:NEXP, :]).then_inc(stored, 16)
            sp.wait_ge(stored, 16)
            for e in range(NEXP):
                sp.dma_start(m.gb[:, e, :], gates[e:e + 1, :].rearrange("a n -> (a n)").partition_broadcast(P)
                             ).then_inc(spread, 16)
            sp.wait_ge(spread, 16 * NEXP)
            m.await_experts(sp)

        @block.gpsimd
        def _(pool):
            nc.gpsimd.memset(m.gate_t[:, :], 1.0).then_inc(rows_ready, 1)

        @block.vector
        def _(v):
            count = [0]

            def link(ins):
                count[0] += 1
                ins.then_inc(step, 1)
                v.wait_ge(step, count[0])

            for j in range(NBLK):
                def x_block(t):
                    return m.x[:, TPB * j + t, :]

                layernorm_block(nc, v, m, j, x_block, 3 * j)
                if j:
                    v.wait_ge(transposed, j)
                normalise_block(nc, m, x_block).then_inc(xn_ready, 1)
            v.wait_ge(loaded, 16 * n_loads)
            v.wait_ge(logits_done, 1)
            if layer == 0:
                link(nc.vector.tensor_copy(lg[:, :, :], lp[:, :, :]))
            else:
                link(nc.vector.tensor_tensor(lg[:, :, :], lp[:, :, :],
                                             br2[:, :].unsqueeze(1).to_broadcast(shape), ALU.add))
            link(nc.vector.reduce_max(col[:, 0, :], lg[:, :, :], AX.X))
            nc.vector.tensor_tensor(lg[:, :, :], lg[:, :, :], col[:, 0, :].unsqueeze(2).to_broadcast(shape),
                                    ALU.subtract).then_inc(shifted, 1)
            v.wait_ge(exp_done, 1)
            link(nc.vector.reduce_sum(col[:, 1, :], ex[:, :, :], AX.X))
            link(nc.vector.reciprocal(col[:, 2, :], col[:, 1, :]))
            link(nc.vector.tensor_tensor(probs[:, :, :], ex[:, :, :],
                                         col[:, 2, :].unsqueeze(2).to_broadcast(shape), ALU.mult))
            for t in range(NT):
                ins = nc.vector.max(top[:, t, :], probs[:, t, :])
            link(ins)
            for t in range(NT):
                ins = nc.vector.max_index(idx[:, t, :], top[:, t, :], probs[:, t, :])
            link(ins)
            link(nc.vector.tensor_copy(idxf[:, :, :], idx[:, :, 0:TOPK]))
            if layer == 0:
                link(nc.vector.tensor_tensor(col[:, 3, :], top[:, :, 0], top[:, :, 1], ALU.add))
                link(nc.vector.reciprocal(col[:, 4, :], col[:, 3, :]))
                nc.vector.tensor_tensor(col[:, 5, :], top[:, :, 0], col[:, 4, :], ALU.mult)
                link(nc.vector.tensor_tensor(col[:, 6, :], top[:, :, 1], col[:, 4, :], ALU.mult))
            else:
                nc.vector.tensor_tensor(col[:, 3, :], top[:, :, 1], top[:, :, 0], ALU.subtract).then_inc(shifted, 1)
                v.wait_ge(exp_done, 2)
                link(nc.vector.tensor_scalar(col[:, 4, :], col[:, 7, :], 1.0, None, ALU.add))
                link(nc.vector.reciprocal(col[:, 5, :], col[:, 4, :]))
                link(nc.vector.tensor_tensor(col[:, 6, :], col[:, 7, :], col[:, 5, :], ALU.mult))
            iota_b = iota[:, :].unsqueeze(1).to_broadcast(shape)
            link(nc.vector.tensor_tensor(oh[:, :, :], iota_b, idxf[:, :, 0:1].to_broadcast(shape), ALU.is_equal))
            link(nc.vector.tensor_tensor(gate[:, :, :], oh[:, :, :], col[:, 5, :].unsqueeze(2).to_broadcast(shape),
                                         ALU.mult))
            link(nc.vector.tensor_tensor(oh[:, :, :], iota_b, idxf[:, :, 1:2].to_broadcast(shape), ALU.is_equal))
            link(nc.vector.tensor_tensor(oh[:, :, :], oh[:, :, :], col[:, 6, :].unsqueeze(2).to_broadcast(shape),
                                         ALU.mult))
            nc.vector.tensor_tensor(gate[:, :, :], gate[:, :, :], oh[:, :, :], ALU.add).then_inc(gate_ready, 1)
            v.wait_ge(rows_ready, 1)
            v.wait_ge(rows_filled, 1)
            nc.vector.tensor_copy(m.gate_t[0:NEXP, :], gp[0:NEXP, :]).then_inc(rows_ready, 1)

        @block.scalar
        def _(act):
            if layer == 1:
                act.wait_ge(loaded, 16 * n_loads)
            for j in range(NBLK):
                deviation_block(nc, act, m, j)
                act.wait_ge(transposed, j + 1)
                nc.scalar.copy(m.xt_all[:, ts(j, BLK)], tr[:, :]).then_inc(xt_ready, 1)
                if layer == 1:
                    act.wait_ge(hid_filled, j + 1)
                    nc.scalar.activation(hr[:, ts(j, BLK)], hp[0:HR, :], ACT.Relu, bias=br1[:, 0:1]
                                         ).then_inc(hid_ready, 1)
            act.wait_ge(shifted, 1)
            nc.scalar.activation(ex[:, :, :], lg[:, :, :], ACT.Exp).then_inc(exp_done, 1)
            if layer == 1:
                act.wait_ge(shifted, 2)
                nc.scalar.activation(col[:, 7, :], col[:, 3, :], ACT.Exp, scale=1.0 / TOPK).then_inc(exp_done, 1)

        @block.tensor
        def _(pe):
            pe.wait_ge(loaded, 16 * n_loads)
            for j in range(NBLK):
                pe.wait_ge(xn_ready, j + 1)
                if j:
                    pe.wait_ge(xt_ready, j)
                for t in range(TPB):
                    ins = nc.tensor.transpose(tr[:, ts(t, P)], m.xn[:, t, :], m.ident[:, :])
                ins.then_inc(transposed, 1)
                pe.wait_ge(xt_ready, j + 1)
                if layer == 1:
                    if j:
                        pe.wait_ge(hid_ready, j)
                    nc.tensor.matmul(hp[0:HR, :], wr1[:, :], m.xt_all[:, ts(j, BLK)], start=True, stop=True
                                     ).then_inc(hid_filled, 1)
                    pe.wait_ge(hid_ready, j + 1)
                src = m.xt_all if layer == 0 else hr
                for t in range(TPB * j, TPB * (j + 1)):
                    ins = nc.tensor.matmul(lp[:, t, :], src[:, ts(t, P)], wr[:, :], start=True, stop=True)
            ins.then_inc(logits_done, 1)
            pe.wait_ge(gate_ready, 1)
            for t in range(NT):
                ins = nc.tensor.matmul(gp[0:NEXP, ts(t, P)], gate[:, t, :], m.ident[:, :], start=True, stop=True)
            ins.then_inc(rows_filled, 1)


HR = E // 4


def experts0(nc, m, d):
    with ExitStack() as ctx:
        def sb(name, shape, dt=F32):
            return ctx.enter_context(nc.sbuf_tensor(name, shape, dt))

        def pb(name, shape):
            return ctx.enter_context(nc.psum_tensor(name, shape, F32))

        def sem(name):
            return m.ctx.enter_context(nc.semaphore(name))

        s = [sb(f"silu0_{i}", [P, BLK]) for i in range(2)]
        hid = [sb(f"hid0_{i}", [P, BLK]) for i in range(2)]
        ob = sb("ob0", [P, BLK])
        h1 = [pb(f"h1_{i}", [P, BLK]) for i in range(2)]
        h2 = [pb(f"h2_{i}", [P, BLK]) for i in range(2)]
        out = pb("out0", [P, BLK])
        tr = pb("tr_e0", [P, TPB, P])
        up_done, silu_done, gated, hid_done = sem("up_done0"), sem("silu_done0"), sem("gated0"), sem("hid_done0")
        down_done, ob_ready, transposed, added = sem("down_done0"), sem("ob_ready0"), sem("tr_done0"), sem("added0")
        block = ctx.enter_context(nc.Block())

        @block.tensor
        def _(pe):
            with pe.Fori(0, NBLK) as j:
                cols = ds(BLK * j, BLK)

                def down(e):
                    pe.wait_ge(hid_done, NEXP * j + e + 1)
                    nc.tensor.matmul(out[:, :], m.down[:, e, :], hid[e % 2][:, :], start=(e == 0),
                                     stop=(e == NEXP - 1)).then_inc(down_done, 1)

                for e in range(NEXP):
                    if e >= 2:
                        pe.wait_ge(hid_done, NEXP * j + e - 1)
                    nc.tensor.matmul(h1[e % 2][:, :], m.up[:, e, 0:P], m.xt_all[:, cols], start=True, stop=True)
                    nc.tensor.matmul(h2[e % 2][:, :], m.up[:, e, P:2 * P], m.xt_all[:, cols], start=True, stop=True
                                     ).then_inc(up_done, 1)
                    if e:
                        down(e - 1)
                down(NEXP - 1)
                pe.wait_ge(ob_ready, j + 1)
                for t in range(TPB):
                    ins = nc.tensor.transpose(tr[:, t, :], ob[:, ts(t, P)], m.ident[:, :])
                ins.then_inc(transposed, 1)

        @block.scalar
        def _(act):
            with act.Fori(0, NBLK) as j:
                for e in range(NEXP):
                    act.wait_ge(up_done, NEXP * j + e + 1)
                    if e >= 2:
                        act.wait_ge(hid_done, NEXP * j + e - 1)
                    nc.scalar.activation(s[e % 2][:, :], h1[e % 2][:, :], ACT.Silu).then_inc(silu_done, 1)
                act.wait_ge(down_done, NEXP * (j + 1))
                nc.scalar.copy(ob[:, :], out[:, :]).then_inc(ob_ready, 1)

        @block.vector
        def _(v):
            with v.Fori(0, NBLK) as j:
                for e in range(NEXP):
                    at = NEXP * j + e
                    v.wait_ge(up_done, at + 1)
                    if e >= 2:
                        v.wait_ge(down_done, at - 1)
                    nc.vector.tensor_tensor(hid[e % 2][:, :], h2[e % 2][:, :], m.gb[:, e, ds(BLK * j, BLK)], ALU.mult
                                            ).then_inc(gated, 1)
                    v.wait_ge(gated, at + 1)
                    v.wait_ge(silu_done, at + 1)
                    nc.vector.tensor_tensor(hid[e % 2][:, :], hid[e % 2][:, :], s[e % 2][:, :], ALU.mult
                                            ).then_inc(hid_done, 1)
                v.wait_ge(transposed, j + 1)
                xs = m.x[:, ds(TPB * j, TPB), :]
                nc.vector.tensor_tensor(xs, tr[:, :, :], xs, ALU.add).then_inc(added, 1)


def l1_prologue(nc, m, d):
    with ExitStack() as ctx:
        def sb(name, shape, dt=F32):
            return ctx.enter_context(nc.sbuf_tensor(name, shape, dt))

        def pb(name, shape):
            return ctx.enter_context(nc.psum_tensor(name, shape, F32))

        def sem(name):
            return m.ctx.enter_context(nc.semaphore(name))

        wkv = sb("wkv", [P, E])
        wv = sb("wv1", [P, E])
        wrope = sb("wrope", [P, 4, P])
        cs = sb("cs", [P, 2, T])
        masks = sb("masks", [P, 2, P])
        m.stats = sb("stats1", [P, TPB, 6])
        m.mv = sb("mv1", [P, TPB, 2])
        m.rstd = sb("rstd1", [P, TPB])
        m.std = sb("std1", [P, TPB])
        m.xn = sb("xn1", [P, TPB, E])
        ca, cb, rot, low = (sb(n, [P, BLK]) for n in ("ca", "cb", "rot", "low"))
        hi = sb("hi1", [P, BLK], F32R)
        tr = pb("tr1", [P, BLK])
        ckp = pb("ckp", [P, BLK])
        vp = pb("vp", [P, TPB, E])
        rp = [pb(f"rp{i}", [P, BLK]) for i in range(2)]
        loaded, m.ln_step, m.std_ready = sem("loaded1"), sem("ln_step1"), sem("std_ready1")
        xn_ready, transposed, xt_ready = sem("xn_ready1"), sem("transposed1"), sem("xt_ready1")
        ck_filled, ck_ready, v_filled, v_read = sem("ck_filled"), sem("ck_ready"), sem("v_filled"), sem("v_read")
        r_filled, r_read, rot_step, hi_ready, packed = (sem("r_filled"), sem("r_read"), sem("rot_step"),
                                                        sem("hi_ready"), sem("packed"))
        cleared, m_ready = sem("v_cleared"), sem("m_ready")
        block = ctx.enter_context(nc.Block())

        @block.sync
        def _(sp):
            for dst, src in ((wkv, d["wkv"]), (wv, d["wv1"]), (m.coef, d["coef"])):
                sp.dma_start(dst[:, :], src).then_inc(loaded, 16)
            for dst, src in ((wrope, d["wrope"]), (cs, d["cs"]), (masks, d["masks"]), (m.wk_all, d["wk1"]), (m.wq_all, d["wq1"])):
                sp.dma_start(dst[:, :, :], src).then_inc(loaded, 16)
            sp.wait_ge(loaded, 16 * 8)

        v_rows = m.v_all[:, :, :, :, :, :].rearrange("p b q t g d -> p (b q t g) d")

        @block.gpsimd
        def _(pool):
            nc.gpsimd.memset(v_rows, 0.0).then_inc(cleared, 1)
            pool.wait_ge(cleared, 1)
            nc.gpsimd.memset(v_rows[:, :, D1:D1 + 1], 1.0).then_inc(cleared, 1)

        @block.vector
        def _(v):
            v.wait_ge(loaded, 16 * 8)
            v.wait_ge(cleared, 2)
            nc.vector.tensor_copy(m.identr[:, :], m.ident[:, :])
            nc.vector.tensor_copy(m.maskr[:, :, :], masks[:, :, :]).then_inc(m_ready, 1)
            for j in range(NBLK):
                def x_block(t):
                    return m.x[:, TPB * j + t, :]

                layernorm_block(nc, v, m, j, x_block, 3 * j)
                if j:
                    v.wait_ge(transposed, j)
                normalise_block(nc, m, x_block).then_inc(xn_ready, 1)
                v.wait_ge(v_filled, j + 1)
                for t in range(TPB):
                    ins = nc.vector.tensor_copy(m.v_all[:, j // 2, :, TPB * (j % 2) + t, :, 0:D1],
                                                vp[:, t, :].rearrange("p (q g d) -> p q g d", q=QUADS, d=D1))
                ins.then_inc(v_read, 1)
                for n, dst in enumerate((m.kr, m.qr)):
                    u = 2 * j + n
                    pos = ds(BLK * (j % 2), BLK)
                    v.wait_ge(r_filled, u + 1)
                    if u:
                        v.wait_ge(hi_ready, u)
                    nc.vector.tensor_tensor(ca[:, :], rp[0][:, :], cs[:, 0, pos], ALU.mult)
                    nc.vector.tensor_tensor(cb[:, :], rp[1][:, :], cs[:, 1, pos], ALU.mult).then_inc(r_read, 1)
                    v.wait_ge(r_read, u + 1)
                    nc.vector.tensor_tensor(rot[:, :], ca[:, :], cb[:, :], ALU.add).then_inc(rot_step, 1)
                    v.wait_ge(hi_ready, u + 1)
                    c = 2 + 2 * n
                    nc.vector.scalar_tensor_tensor(dst[:, ts(j, BLK)], hi[:, :].bitcast(F32), m.coef[:, c + 1:c + 2],
                                                   low[:, :], ALU.mult, ALU.add).then_inc(packed, 1)

        @block.scalar
        def _(act):
            act.wait_ge(loaded, 16 * 8)
            for j in range(NBLK):
                deviation_block(nc, act, m, j)
                act.wait_ge(transposed, j + 1)
                nc.scalar.copy(m.xt_all[:, ts(j, BLK)], tr[:, :]).then_inc(xt_ready, 1)
                act.wait_ge(ck_filled, j + 1)
                nc.scalar.copy(m.ck_all[:, ts(j, BLK)], ckp[:, :]).then_inc(ck_ready, 1)
                for n in range(2):
                    u = 2 * j + n
                    act.wait_ge(rot_step, u + 1)
                    if u:
                        act.wait_ge(packed, u)
                    c = 2 + 2 * n
                    nc.scalar.activation(low[:, :], rot[:, :], ACT.Copy, scale=m.coef[:, c:c + 1])
                    nc.scalar.copy(hi[:, :], rot[:, :]).then_inc(hi_ready, 1)

        @block.tensor
        def _(pe):
            pe.wait_ge(loaded, 16 * 8)
            for j in range(NBLK):
                cols = ts(j, BLK)
                pe.wait_ge(xn_ready, j + 1)
                if j:
                    pe.wait_ge(xt_ready, j)
                for t in range(TPB):
                    ins = nc.tensor.transpose(tr[:, ts(t, P)], m.xn[:, t, :], m.ident[:, :])
                ins.then_inc(transposed, 1)
                pe.wait_ge(xt_ready, j + 1)
                if j:
                    pe.wait_ge(ck_ready, j)
                nc.tensor.matmul(ckp[:, :], wkv[:, :], m.xt_all[:, cols], start=True, stop=True).then_inc(ck_filled, 1)
                pe.wait_ge(ck_ready, j + 1)
                if j:
                    pe.wait_ge(v_read, j)
                for t in range(TPB):
                    ins = nc.tensor.matmul(vp[:, t, :], m.ck_all[:, ts(TPB * j + t, P)], wv[:, :],
                                           start=True, stop=True)
                ins.then_inc(v_filled, 1)
                for n, src in enumerate((m.ck_all, m.xt_all)):
                    if 2 * j + n:
                        pe.wait_ge(r_read, 2 * j + n)
                    for s in range(2):
                        ins = nc.tensor.matmul(rp[s][:, :], wrope[:, 2 * n + s, :], src[:, cols],
                                               start=True, stop=True)
                    ins.then_inc(r_filled, 1)


def s_pieces():
    out = []
    for t in range(TT):
        width = (t + 1) * P
        if width <= BLK:
            out.append((t, 0, width, True))
        else:
            out += [(t, 0, BLK, False), (t, BLK, width - BLK, True)]
    return out


PIECES = s_pieces()
EARLY = [u for u in range(len(PIECES)) if PIECES[u][0] < TPB]
LATE = [u for u in range(len(PIECES)) if PIECES[u][0] >= TPB]


def s_early(first, last):
    return [("s", g, u) for g in range(4) for u in EARLY][first:last]


def s_late():
    out = [("s", g, u) for g in range(4) for u in LATE]
    for g in range(3):
        out.insert(len(LATE) * (g + 1) + 2 + g, ("m", g, 0))
    return out + [("m", 3, 0)]


PROJ1 = [("k", 0, 0), ("q", 0, 0), ("k", 0, 1), ("q", 0, 1)]
START1 = PROJ1 + s_early(0, None) + PROJ1 + s_late()
NEXT1 = (PROJ1[:1] + s_early(0, 2) + PROJ1[1:2] + s_early(2, 8) + PROJ1[2:3] + s_early(8, 10) + PROJ1[3:]
         + s_early(10, None) + s_late())
FINISH1 = [("t", 0, 0), ("t", 0, 1)]
FULL1 = FINISH1 + NEXT1
AT_TILE = [8, 8, 8, 8, 7, 7, 6, 5]


def before_last_projection(units, seen):
    same = [i for i in range(seen) if units[i][0] == units[seen][0]]
    return same[-1] if same else None


def quads_ahead(units, seen):
    kind = units[seen][0]
    return 1 + (kind in "kq" and not (units is START1 and seen < len(PROJ1)))


def script1(units):
    left, out = list(units), []
    for kt in range(TT):
        parts = [("ST", kt, g) for g in range(4)]
        if kt:
            parts += [("PV", kt - 1, n) for n in range(len(q_pieces(kt - 1)))]
        for n, part in enumerate(parts):
            out.append(part)
            for _ in range(AT_TILE[kt] * (n + 1) // len(parts) - AT_TILE[kt] * n // len(parts)):
                if left:
                    out.append(("UNIT",) + left.pop(0))
    out.append(("PV", TT - 1, 0))
    return out + [("UNIT",) + u for u in left]


def units_before1(n):
    at_0 = len(START1)
    return at_0 if isinstance(n, int) and n == 0 else at_0 + len(NEXT1) + len(FULL1) * (n - 1)


def q_pieces(kt):
    lo = P * kt
    return [(lo, BLK), (BLK, T)] if lo < BLK else [(lo, T)]


def l1_attention(nc, m, d):
    with ExitStack() as ctx:
        def sb(name, shape, dt=F32):
            return ctx.enter_context(nc.sbuf_tensor(name, shape, dt))

        def sem(name):
            return m.ctx.enter_context(nc.semaphore(name))

        R2, R4 = range(2), range(4)
        HEAD = 3 * DR
        ROW = HEAD + 3 * D1
        kk = [sb(f"l1_kk{a}", [P, 4, T], F32R) for a in R2]
        qq = [sb(f"l1_qq{a}", [P, 4, T], F32R) for a in R2]
        wk, wq = sb("l1_wk", [P, P]), sb("l1_wq", [P, P])
        val = [sb(f"l1_v{a}", [P, TT, 4, 32]) for a in R2]
        prob = [sb(f"l1_prob{s}", [P, 4, T]) for s in R2]
        low = [sb(f"l1_low{i}", [P, BLK]) for i in R2]
        hi = [sb(f"l1_hi{i}", [P, BLK], F32R) for i in R2]
        head = [sb(f"l1_head{s}", [P, T], F32R) for s in R2]
        ut = sb("l1_ut", [P, T])
        mx = sb("l1_mx", [P, 4, TT, 2])
        mmax = sb("l1_mmax", [P, 4, TT])
        negm = sb("l1_negm", [P, 4, TT])
        mrow = [sb(f"l1_mrow{g}", [TT, P], F32R) for g in R4]
        rs = sb("l1_rs", [P, 2, TPB, 4])
        st = [ctx.enter_context(nc.psum_tensor(f"l1_st{h}", [P, T], F32)) for h in R2]
        pv = ctx.enter_context(nc.psum_tensor("l1_pv", [P, T], F32))
        work = [ctx.enter_context(nc.psum_tensor(f"l1_work{h}", [P, BLK], F32)) for h in R2]

        cleared = sem("cleared1")
        w_loaded = sem("l1_w_loaded")
        val_loaded, rope_copied = [sem(f"val_loaded{a}") for a in R2], sem("rope_copied")
        rope_loaded, k_loaded, q_loaded = ([[sem(f"{name}_loaded{a}{j}") for j in R2] for a in R2]
                                           for name in ("rope", "k", "q"))
        row_loaded = [sem(f"row_loaded1{g}") for g in R4]
        filled, read, halves = sem("work_filled1"), sem("work_read1"), sem("halves")
        negm_ready, mmax_ready, rs_ready = sem("negm_ready1"), sem("mmax_ready1"), sem("rs_ready")
        st_filled, exp_done, pv_done, ut_ready = sem("st_filled1"), sem("exp_done1"), sem("pv_done1"), sem("ut_ready1")
        block = ctx.enter_context(nc.Block())

        def steps(eng, step):
            step(0, 0, True, False)
            with eng.Fori(0, (STEPS1 - 2) // 2) as i:
                step(2 * i + 1, 1, False, False)
                step(2 * i + 2, 0, False, False)
            step(STEPS1 - 1, 1, False, True)

        def units_of(first, last):
            return NEXT1 if first else FINISH1 if last else FULL1

        def at_unit(first, last, kind, j):
            return [u[0] == kind and u[2] == j for u in units_of(first, last)].index(True)

        def even_of(first, par):
            return (len(START1) + (0 if first else len(NEXT1) + (1 + par) * len(FULL1))) % 2

        @block.sync
        def _(sp):
            v_steps = m.v_all[:, :, :, :, :, :].rearrange("p b q t g d -> p (b q t g) d")

            def load_weights(k):
                sp.dma_start(wk[:, :], m.wk_all[:, k % QUADS, :]).then_inc(w_loaded, 16)
                sp.dma_start(wq[:, :], m.wq_all[:, k % QUADS, :]).then_inc(w_loaded, 16)

            def load_values(k, par):
                sp.dma_start(val[par][:, :, :, 0:2 * D1].rearrange("p t g d -> p (t g) d"),
                             v_steps[:, ds(TT * 4 * k, TT * 4), :]
                             ).then_inc(val_loaded[par], 16)

            def load_rows(k, par, j):
                half = ts(j, BLK)
                for dst, src, loaded in ((kk, head[0], k_loaded), (qq, head[1], q_loaded)):
                    for h in R4:
                        sp.dma_start(dst[par][HEAD:P, h, half].bitcast(F32),
                                     src[32 * h:32 * (h + 1), half].bitcast(F32)).then_inc(loaded[par][j], 16)
                sp.dma_start(qq[par][0:HEAD, :, half].bitcast(F32),
                             m.qr[0:HEAD, ds(T * (k // QUADS % B) + BLK * j, BLK)].unsqueeze(1)
                             .to_broadcast([HEAD, 4, BLK]).bitcast(F32)).then_inc(rope_loaded[par][j], 16)

            def max_rows(par, units, base):
                seen = 0
                for kind, g, j in units:
                    if kind == "m":
                        sp.wait_ge(read, base + seen + 1)
                        sp.dma_start(qq[par][ROW:ROW + 1, g, :].bitcast(F32), mrow[g][:, :].bitcast(F32)
                                     ).then_inc(row_loaded[g], 16)
                    seen += 1

            sp.wait_ge(cleared, 1)
            load_weights(0)
            load_values(0, 0)
            sp.wait_ge(read, len(PROJ1))
            load_weights(1)
            load_rows(0, 0, 0)
            load_rows(0, 0, 1)
            sp.wait_ge(read, START1.index(("m", 0, 0)) - len(LATE) - 2)
            load_weights(2)
            load_rows(1, 1, 0)
            max_rows(0, START1, 0)

            def step(n, par, first, last):
                if not last:
                    base, units = units_before1(n), units_of(first, last)
                    if not first:
                        sp.wait_ge(pv_done, TT * n)
                    load_rows(n + 1, 1 - par, 1)
                    load_values(n + 1, 1 - par)
                    sp.wait_ge(read, base + units.index(("q", 0, 1)) + 1)
                    sp.wait_ge(st_filled, 4 * (TT * n + TPB))
                    load_rows(n + 2, par, 0)
                    load_weights(n + 3)
                    max_rows(1 - par, units, base)

            steps(sp, step)
            sp.wait_ge(w_loaded, 32 * (STEPS1 + 2))
            sp.wait_ge(rope_loaded[0][0], 16 * (STEPS1 // 2 + 1))
            sp.wait_ge(k_loaded[0][0], 64 * (STEPS1 // 2 + 1))
            sp.wait_ge(q_loaded[0][0], 64 * (STEPS1 // 2 + 1))

        @block.scalar
        def _(act):
            def run(n, par, todo, base, even, first, units):
                seen = 0
                for what, kind, *rest in todo:
                    if what == "UNIT":
                        j = rest[1]
                        if kind in "kq":
                            act.wait_ge(filled, base + seen + 1)
                            back = before_last_projection(units, seen)
                            if back is not None:
                                act.wait_ge(read, base + back + 1)
                            elif not (isinstance(base, int) and base == 0):
                                act.wait_ge(read, base)
                            b = kind == "q"
                            buf = work[(even + seen) % 2]
                            c = 6 + 2 * (kind == "q")
                            one = m.coef[:, 10:11] if kind == "k" else m.coef[:, 11:12]
                            nc.scalar.activation(low[b][:, :], buf[:, :], ACT.Identity, scale=m.coef[:, c:c + 1], bias=one)
                            nc.scalar.copy(hi[b][:, :], buf[:, :]).then_inc(halves, 1)
                        seen += 1
                    elif what == "ST":
                        kt, g = kind, rest[0]
                        act.wait_ge(st_filled, 4 * (TT * n + kt) + g + 1)
                        if not (first and kt < 2):
                            act.wait_ge(pv_done, TT * n + kt - 1)
                        nc.scalar.activation(prob[kt % 2][:, g, P * kt:T], st[g % 2][:, P * kt:T], ACT.Exp,
                                             scale=SCALE1).then_inc(exp_done, 1)

            for g in R4:
                nc.scalar.copy(kk[0][0:HEAD, g, 0:BLK], m.kr[0:HEAD, 0:BLK].bitcast(F32)).then_inc(rope_copied, 1)
            run(-1, 1, [("UNIT",) + u for u in START1], 0, 0, True, START1)

            def step(n, par, first, last):
                units = units_of(first, last)
                run(n, par, script1(units), units_before1(n), even_of(first, par), first, units)
                act.wait_ge(pv_done, TT * (n + 1))
                if not first:
                    act.wait_ge(read, units_before1(n) + at_unit(first, last, "t", 1) + 1)
                nc.scalar.copy(ut[:, :], pv[:, :]).then_inc(ut_ready, 1)

            steps(act, step)

        @block.gpsimd
        def _(pool):
            for a in R2:
                nc.gpsimd.memset(val[a][:, :, :, 2 * D1:], 0.0)
            nc.gpsimd.memset(mx[:, :, :, :], -3e38).then_inc(cleared, 1)

            pool.wait_ge(rope_copied, 4)

            def copy_rope(k, par, j):
                for g in R4:
                    nc.gpsimd.tensor_copy(kk[par][0:HEAD, g, ts(j, BLK)],
                                          m.kr[0:HEAD, ds(T * (k // QUADS % B) + BLK * j, BLK)].bitcast(F32)
                                          ).then_inc(rope_copied, 1)

            copy_rope(0, 0, 1)
            copy_rope(1, 1, 0)

            def step(n, par, first, last):
                if not last:
                    if not first:
                        pool.wait_ge(st_filled, 4 * TT * n)
                    copy_rope(n + 1, 1 - par, 1)
                    pool.wait_ge(st_filled, 4 * (TT * n + TPB))
                    copy_rope(n + 2, par, 0)

            steps(pool, step)

        @block.vector
        def _(v):
            def combine(g, k, u_last):
                v.wait_ge(read, u_last + 1)
                nc.vector.tensor_tensor(mmax[:, g, :], mx[:, g, :, 0], mx[:, g, :, 1], ALU.max).then_inc(mmax_ready, 1)
                v.wait_ge(mmax_ready, 4 * k + g + 1)
                nc.vector.tensor_scalar(negm[:, g, :], mmax[:, g, :], -1.0, None, ALU.mult).then_inc(negm_ready, 1)

            def run(n, par, units, base, even):
                seen = 0
                for kind, g, j in units:
                    u, buf = base + seen, work[(even + seen) % 2]
                    if kind in "kq":
                        k = n + quads_ahead(units, seen)
                        c, b = 6 + 2 * (kind == "q"), kind == "q"
                        v.wait_ge(halves, 4 * k + 2 * j + (kind == "q") + 1)
                        if not (isinstance(k, int) and k == 0):
                            loaded = (k_loaded if kind == "k" else q_loaded)[1 - par]
                            v.wait_ge(loaded[j], 64 * ((k - 1) // 2 + 1))
                        nc.vector.scalar_tensor_tensor(head[kind == "q"][:, ts(j, BLK)], hi[b][:, :].bitcast(F32),
                                                       m.coef[:, c + 1:c + 2], low[b][:, :], ALU.mult, ALU.add
                                                       ).then_inc(read, 1)
                    elif kind == "s":
                        t, key, width, diagonal = PIECES[j]
                        v.wait_ge(filled, u + 1)
                        nc.vector.reduce_max(mx[:, g, t, (key > 0):(key > 0) + 1], buf[:, 0:width], AX.X
                                             ).then_inc(read, 1)
                        if j == len(PIECES) - 1:
                            combine(g, n + 1, u)
                    elif kind == "m":
                        k = n + 1
                        if not (isinstance(k, int) and k == 0):
                            v.wait_ge(row_loaded[g], 16 * k)
                        v.wait_ge(filled, u + 1)
                        nc.vector.tensor_copy(mrow[g][:, :], buf[0:TT, 0:P]).then_inc(read, 1)
                    else:
                        k = n - 1
                        v.wait_ge(filled, u + 1)
                        parts = buf[:, :].rearrange("p (t g c) -> p t g c", t=TPB, g=4)
                        nc.vector.reciprocal(rs[:, j, :, :], parts[:, :, :, D1]).then_inc(rs_ready, 1)
                        v.wait_ge(rs_ready, 2 * k + j + 1)
                        nc.vector.tensor_tensor(m.attn[:, ds(TT * (k // QUADS) + TPB * j, TPB), k % QUADS, :, :],
                                                parts[:, :, :, 0:D1],
                                                rs[:, j, :, :].unsqueeze(3).to_broadcast([P, TPB, 4, D1]),
                                                ALU.mult).then_inc(read, 1)
                    seen += 1

            v.wait_ge(cleared, 1)
            run(-1, 1, START1, 0, 0)

            def step(n, par, first, last):
                run(n, par, units_of(first, last), units_before1(n), even_of(first, par))

            steps(v, step)
            run(STEPS1, 0, FINISH1, units_before1(STEPS1 - 1) + 2, even_of(False, 1))

        @block.tensor
        def _(pe):
            def unit(kind, g, j, u, buf, par, k):
                if not (isinstance(u, int) and u < 2):
                    pe.wait_ge(read, u - 1)
                if kind in "kq":
                    w, src = (wk, m.ck_all) if kind == "k" else (wq, m.xt_all)
                    if kind == "k" and j == 0:
                        pe.wait_ge(w_loaded, 32 * (k + 1))
                    ins = nc.tensor.matmul(buf[:, :], w[:, :], src[:, ds(T * (k // QUADS % B) + BLK * j, BLK)],
                                           start=True, stop=True)
                elif kind == "s":
                    half = PIECES[j][0] >= TPB
                    if j in (EARLY[0], LATE[0]):
                        pe.wait_ge(rope_copied, 8 * k + 4 * half + g + 1)
                        if g == 0:
                            pe.wait_ge(rope_loaded[par][half], 16 * (k // 2 + 1))
                            pe.wait_ge(k_loaded[par][half], 64 * (k // 2 + 1))
                            pe.wait_ge(q_loaded[par][half], 64 * (k // 2 + 1))
                    t, key, width, diagonal = PIECES[j]
                    ins = nc.tensor.matmul(buf[:, 0:width], qq[par][:, g, ts(t, P)], kk[par][:, g, key:key + width],
                                           start=True, stop=not diagonal)
                    if diagonal:
                        ins = nc.tensor.matmul(buf[:, width - P:width], m.identr[:, :], m.maskr[:, 0, :],
                                               start=False, stop=True)
                elif kind == "m":
                    pe.wait_ge(negm_ready, 4 * k + g + 1)
                    ins = nc.tensor.matmul(buf[0:TT, 0:P], negm[:, g, :], m.ident[:, :], start=True, stop=True)
                else:
                    pe.wait_ge(ut_ready, k + 1)
                    for t in range(TPB):
                        ins = nc.tensor.transpose(buf[:, ts(t, P)], ut[:, ts(TPB * j + t, P)], m.ident[:, :])
                ins.then_inc(filled, 1)

            def run(n, par, todo, base, even, first, units):
                seen = 0
                for what, *rest in todo:
                    if what == "UNIT":
                        kind, g, j = rest
                        k = n - 1 if kind == "t" else n + quads_ahead(units, seen)
                        unit(kind, g, j, base + seen, work[(even + seen) % 2], 1 - par, k)
                        seen += 1
                    elif what == "ST":
                        kt, g = rest
                        at = 4 * (TT * n + kt) + g
                        if not (first and kt == 0 and g < 2):
                            pe.wait_ge(exp_done, at - 1)
                        if kt == 0:
                            pe.wait_ge(row_loaded[g], 16 * (n + 1))
                        buf = st[g % 2]
                        pieces = q_pieces(kt)
                        for n_piece, (lo, hi_) in enumerate(pieces):
                            ins = nc.tensor.matmul(buf[:, lo:hi_], kk[par][:, g, ts(kt, P)], qq[par][:, g, lo:hi_],
                                                   start=True, stop=(n_piece > 0))
                            if n_piece == 0:
                                ins = nc.tensor.matmul(buf[:, lo:lo + P], m.identr[:, :], m.maskr[:, 1, :],
                                                       start=False, stop=True)
                        ins.then_inc(st_filled, 1)
                    else:
                        kt, piece = rest
                        if piece == 0:
                            pe.wait_ge(exp_done, 4 * (TT * n + kt + 1))
                        if kt == 0 and piece == 0:
                            pe.wait_ge(val_loaded[par], 16 * (n // 2 + 1))
                            if not first:
                                pe.wait_ge(ut_ready, n)
                        lo, hi_ = q_pieces(kt)[piece]
                        for g in R4:
                            ins = nc.tensor.matmul(pv[32 * g:32 * (g + 1), lo:hi_], val[par][:, kt, g, :],
                                                   prob[kt % 2][:, g, lo:hi_], start=(kt == 0),
                                                   stop=(kt == TT - 1 or (kt == 3 and lo < BLK)))
                        if piece == len(q_pieces(kt)) - 1:
                            ins.then_inc(pv_done, 1)

            run(-1, 1, [("UNIT",) + u for u in START1], 0, 0, True, START1)

            def step(n, par, first, last):
                units = units_of(first, last)
                run(n, par, script1(units), units_before1(n), even_of(first, par), first, units)

            steps(pe, step)
            run(STEPS1, 0, [("UNIT",) + u for u in FINISH1], units_before1(STEPS1 - 1) + 2, even_of(False, 1), False,
                FINISH1)


def l1_output(nc, m, d):
    with ExitStack() as ctx:
        wo = ctx.enter_context(nc.sbuf_tensor("wo", [P, E], F32))
        at = [ctx.enter_context(nc.sbuf_tensor(f"at{i}", [P, BLK], F32)) for i in range(2)]
        tr = [ctx.enter_context(nc.psum_tensor(f"tr_o{i}", [P, BLK], F32)) for i in range(2)]
        out = [ctx.enter_context(nc.psum_tensor(f"out_o{i}", [P, TPB, E], F32)) for i in range(2)]

        def sem(name):
            return m.ctx.enter_context(nc.semaphore(name))
        loaded, transposed, at_ready, out_filled, added = (sem("wo_loaded"), sem("tr_o"), sem("at_ready"),
                                                           sem("out_filled"), sem("added_o"))
        block = ctx.enter_context(nc.Block())

        @block.sync
        def _(sp):
            sp.dma_start(wo[:, :], d["wo"]).then_inc(loaded, 16)

        @block.tensor
        def _(pe):
            pe.wait_ge(loaded, 16)
            for j in range(NBLK):
                if j >= 2:
                    pe.wait_ge(at_ready, j - 1)
                for t in range(TPB):
                    src = m.attn[:, TPB * j + t, :, :, :].rearrange("p a b c -> p (a b c)")
                    ins = nc.tensor.transpose(tr[j % 2][:, ts(t, P)], src, m.ident[:, :])
                ins.then_inc(transposed, 1)
                pe.wait_ge(at_ready, j + 1)
                if j >= 2:
                    pe.wait_ge(added, j - 1)
                for t in range(TPB):
                    ins = nc.tensor.matmul(out[j % 2][:, t, :], at[j % 2][:, ts(t, P)], wo[:, :], start=True, stop=True)
                ins.then_inc(out_filled, 1)

        @block.scalar
        def _(act):
            for j in range(NBLK):
                act.wait_ge(transposed, j + 1)
                if j >= 2:
                    act.wait_ge(out_filled, j - 1)
                nc.scalar.copy(at[j % 2][:, :], tr[j % 2][:, :]).then_inc(at_ready, 1)

        @block.vector
        def _(v):
            for j in range(NBLK):
                v.wait_ge(out_filled, j + 1)
                xs = m.x[:, TPB * j:TPB * (j + 1), :]
                nc.vector.tensor_tensor(xs, out[j % 2][:, :, :], xs, ALU.add).then_inc(added, 1)


def experts1(nc, m, d):
    with ExitStack() as ctx:
        def sb(name, shape, dt=F32):
            return ctx.enter_context(nc.sbuf_tensor(name, shape, dt))

        def pb(name, shape):
            return ctx.enter_context(nc.psum_tensor(name, shape, F32))

        def sem(name):
            return m.ctx.enter_context(nc.semaphore(name))

        UNITS = (NEXP + 1) * CH
        s = [sb(f"silu1_{i}", [P, BLK]) for i in range(3)]
        ob = sb("ob1", [P, BLK])
        hp = [pb(f"hid1_{i}", [P, BLK]) for i in range(3)]
        out = pb("out1", [P, BLK])
        tr = pb("tr_e1", [P, TPB, P])
        up_done, silu_done, gated, down_done = sem("up_done1"), sem("silu_done1"), sem("gated1"), sem("down_done1")
        ob_ready, transposed, added, stored = sem("ob_ready1"), sem("tr_done1"), sem("added1"), sem("stored")
        block = ctx.enter_context(nc.Block())

        @block.tensor
        def _(pe):
            with pe.Fori(0, NBLK) as j:
                cols = ds(BLK * j, BLK)

                def down(u):
                    if u < NEXP * CH:
                        pe.wait_ge(gated, NEXP * CH * j + u + 1)
                    else:
                        pe.wait_ge(silu_done, UNITS * j + u + 1)
                    nc.tensor.matmul(out[:, :], m.w2[:, u, :], s[u % 3][:, :], start=(u == 0), stop=False
                                     ).then_inc(down_done, 1)

                for u in range(UNITS):
                    if u >= 3:
                        pe.wait_ge(silu_done, UNITS * j + u - 2)
                    nc.tensor.matmul(hp[u % 3][:, :], m.w1[:, u, :], m.xt_all[:, cols], start=True, stop=True
                                     ).then_inc(up_done, 1)
                    if u >= 2:
                        down(u - 2)
                down(UNITS - 2)
                down(UNITS - 1)
                nc.tensor.matmul(out[:, :], m.b2[0:NEXP + 1, :], m.gate_t[0:NEXP + 1, cols], start=False, stop=True
                                 ).then_inc(down_done, 1)
                pe.wait_ge(ob_ready, j + 1)
                for t in range(TPB):
                    ins = nc.tensor.transpose(tr[:, t, :], ob[:, ts(t, P)], m.ident[:, :])
                ins.then_inc(transposed, 1)

        @block.scalar
        def _(act):
            with act.Fori(0, NBLK) as j:
                for u in range(UNITS):
                    act.wait_ge(up_done, UNITS * j + u + 1)
                    if u >= 3:
                        act.wait_ge(down_done, (UNITS + 1) * j + u - 2)
                    nc.scalar.activation(s[u % 3][:, :], hp[u % 3][:, :], ACT.Silu, bias=m.b1[:, u:u + 1]
                                         ).then_inc(silu_done, 1)
                act.wait_ge(down_done, (UNITS + 1) * (j + 1))
                nc.scalar.copy(ob[:, :], out[:, :]).then_inc(ob_ready, 1)

        @block.vector
        def _(v):
            with v.Fori(0, NBLK) as j:
                for u in range(NEXP * CH):
                    v.wait_ge(silu_done, UNITS * j + u + 1)
                    nc.vector.tensor_tensor(s[u % 3][:, :], s[u % 3][:, :], m.gb[:, u // CH, ds(BLK * j, BLK)],
                                            ALU.mult).then_inc(gated, 1)
                v.wait_ge(transposed, j + 1)
                xs = m.x[:, ds(TPB * j, TPB), :]
                nc.vector.tensor_tensor(xs, tr[:, :, :], xs, ALU.add).then_inc(added, 1)

        @block.sync
        def _(sp):
            with sp.Fori(0, NBLK) as j:
                sp.wait_ge(added, j + 1)
                sp.dma_start(d["out"][ds(BLK * j, BLK), :].rearrange("(t p) e -> p t e", p=P),
                             m.x[:, ds(TPB * j, TPB), :]).then_inc(stored, 16)
            sp.wait_ge(stored, 16 * NBLK)


def build(nc, d):
    with ExitStack() as ctx:
        m = Mem()
        m.ctx = ctx

        def sb(name, shape, dt=F32):
            return ctx.enter_context(nc.sbuf_tensor(name, shape, dt))

        m.x = sb("x", [P, NT, E])
        m.ident = sb("ident", [P, P])
        m.eps = sb("eps", [P, 1])

        with ExitStack() as layer:
            def sl(name, shape, dt=F32):
                return layer.enter_context(nc.sbuf_tensor(name, shape, dt))

            m.aq = sl("aq", [P, N], F32R)
            m.ak = sl("ak", [P, N], F32R)
            m.w_all = sl("w_all", [P, H0, 4, D0], F32R)
            m.c_all = sl("c_all", [P, NT, D0])
            m.g_all = sl("g_all", [P, PAIRS, E])
            m.out_bias = sl("out_bias", [P, 1])
            m.out_t = sl("out_t", [P, N])
            m.qk_bias = sl("qk_bias", [P, 4 * PAIRS])
            l0_prologue(nc, m, d)
            l0_attention(nc, m, d)
            residual_out(nc, m, d)

        with ExitStack() as layer:
            def sl(name, shape, dt=F32):
                return layer.enter_context(nc.sbuf_tensor(name, shape, dt))

            m.xt_all = sl("xt_all0", [P, N])
            m.gb = sl("gb0", [P, NEXP, N])
            m.gate_t = sl("gate_t0", [P, N])
            m.up = sl("up", [P, NEXP, 2 * P])
            m.down = sl("down", [P, NEXP, E])
            loaded = ctx.enter_context(nc.semaphore("experts0_loaded"))

            def load_experts(sp):
                sp.dma_start(m.up[:, :, :], d["up"]).then_inc(loaded, 16)
                sp.dma_start(m.down[:, :, :], d["down"]).then_inc(loaded, 16)

            def await_experts(sp):
                sp.wait_ge(loaded, 32)

            m.load_experts, m.await_experts = load_experts, await_experts
            router(nc, m, d, 0, d["router"], None, None, None)
            experts0(nc, m, d)

        with ExitStack() as layer:
            def sl(name, shape, dt=F32):
                return layer.enter_context(nc.sbuf_tensor(name, shape, dt))

            m.xt_all = sl("xt_all1", [P, N])
            m.ck_all = sl("ck_all", [P, N])
            m.v_all = sl("v_all", [P, B, QUADS, TT, 4, 2 * D1])
            m.kr = sl("kr", [P, N], F32R)
            m.qr = sl("qr", [P, N], F32R)
            m.attn = sl("attn", [P, NT, QUADS, 4, D1])
            m.identr = sl("identr", [P, P], F32R)
            m.maskr = sl("maskr", [P, 2, P], F32R)
            m.coef = sl("coef", [P, 12])
            m.wk_all = sl("wk_all", [P, QUADS, P])
            m.wq_all = sl("wq_all", [P, QUADS, P])
            l1_prologue(nc, m, d)
            l1_attention(nc, m, d)
            l1_output(nc, m, d)

        with ExitStack() as layer:
            def sl(name, shape, dt=F32):
                return layer.enter_context(nc.sbuf_tensor(name, shape, dt))

            m.xt_all = sl("xt_all2", [P, N])
            m.gb = sl("gb1", [P, NEXP, N])
            m.gate_t = sl("gate_t1", [P, N])
            m.w1 = sl("up1", [P, (NEXP + 1) * CH, P])
            m.w2 = sl("down1", [P, (NEXP + 1) * CH, E])
            m.b1 = sl("bias_up1", [P, (NEXP + 1) * CH])
            m.b2 = sl("bias_down1", [NEXP + 1, E])
            loaded = ctx.enter_context(nc.semaphore("experts1_loaded"))

            def load_experts(sp):
                for dst, src in ((m.w1, d["w1"]), (m.w2, d["w2"])):
                    sp.dma_start(dst[:, :, :], src).then_inc(loaded, 16)
                for dst, src in ((m.b1, d["b1"]), (m.b2, d["b2"])):
                    sp.dma_start(dst[:, :], src).then_inc(loaded, 16)

            def await_experts(sp):
                sp.wait_ge(loaded, 64)

            m.load_experts, m.await_experts = load_experts, await_experts
            router(nc, m, d, 1, d["wr2"], d["wr1"], d["br1"], d["br2"])
            experts1(nc, m, d)


def kernel(**inputs):
    import numpy as _np
    import concourse.bacc as _bacc
    from concourse import mybir as _mybir
    from concourse.bass_utils import run_bass_kernel_spmd as _run

    i = {k: _np.asarray(v) for k, v in inputs.items()}
    h, dk = 16, 64

    def twice(a):
        return _np.concatenate([a, a], axis=0)

    def qk_columns():
        q = i["L0_attn_fcq_b"].reshape(h, dk)
        k = i["L0_attn_fck_b"].reshape(h, dk)
        return twice(_np.stack([q, k], axis=1).reshape(2 * h, dk).T)

    def head_columns(w):
        w = w.reshape(128, 16, 8)
        return _np.concatenate([w, w, w, _np.zeros_like(w)], axis=2).reshape(128, 4, 128)

    def rotary_columns(w):
        swapped = _np.concatenate([w[:, 16:], w[:, :16]], axis=1)
        return [_np.tile(w, (1, 4)), _np.tile(swapped, (1, 4))]

    def rotary_tables():
        inv = (1.0 / _np.power(_np.float32(10000.0), _np.arange(0, 32, 2, dtype=_np.float32) / _np.float32(32))
               ).astype(_np.float32)
        angle = _np.outer(_np.arange(1024, dtype=_np.float32), inv).astype(_np.float32).T
        cos, sin = _np.cos(angle), _np.sin(angle)
        return _np.stack([_np.tile(_np.concatenate([cos, cos]), (4, 1)),
                          _np.tile(_np.concatenate([-sin, sin]), (4, 1))], axis=1).astype(_np.float32)

    def part_columns():
        c = _np.zeros((128, 12), _np.float32)
        row = _np.arange(128)
        for at, rest in ((2, row // 32 == 1), (4, row // 32 == 2),
                         (6, row % 32 // 8 == 1), (8, row % 32 // 8 == 2)):
            c[:, at] = rest
            c[:, at + 1] = _np.where(rest, -1.0, 1.0)
        c[:, 10] = row % 32 == 24
        return c

    def masks():
        later = _np.triu(_np.ones((128, 128), _np.float32), 1)
        return _np.stack([later, later.T], axis=1) * _np.float32(MASKED)

    wq, wk, wv = i["L0_attn_wq"], i["L0_attn_wk"], i["L0_attn_wv"]
    w1 = _np.concatenate([i["L1_ffn_We1"], i["L1_ffn_Ws1"][None]])
    w2 = _np.concatenate([i["L1_ffn_We2"], i["L1_ffn_Ws2"][None]])
    b1 = _np.concatenate([i["L1_ffn_be1"], i["L1_ffn_bs1"][None]])
    arrays = {
        "x": i["L0_attn_z"].reshape(2048, 128),
        "ident": _np.eye(128, dtype=_np.float32),
        "wl": _np.concatenate([wq, wq, wk, wk, wv], axis=1),
        "fq": twice(i["L0_attn_fcq_w"]).reshape(128, h, dk),
        "fk": twice(i["L0_attn_fck_w"]).reshape(128, h, dk),
        "fv_t": i["L0_attn_fcv_w"].reshape(dk, h, dk).transpose(2, 1, 0),
        "fo": i["L0_attn_fco_w"].reshape(h, dk, 128).transpose(1, 0, 2),
        "bv": i["L0_attn_fcv_b"].reshape(h, dk).T,
        "bo": i["L0_attn_fco_b"].reshape(128, 1),
        "qk_bias": qk_columns(),
        "router": i["L0_ffn_router_w"].T,
        "iota": _np.tile(_np.arange(8, dtype=_np.float32), (128, 1)),
        "up": i["L0_ffn_up_proj"].transpose(1, 0, 2),
        "down": i["L0_ffn_down_proj"].transpose(1, 0, 2),
        "wkv": i["L1_attn_W_kv_down"],
        "wv1": i["L1_attn_W_v_up"],
        "wrope": _np.stack(rotary_columns(i["L1_attn_W_k_rope"]) + rotary_columns(i["L1_attn_W_q_rope"]), axis=1),
        "cs": rotary_tables(),
        "masks": masks(),
        "coef": part_columns(),
        "wk1": head_columns(i["L1_attn_W_k_up"]),
        "wq1": head_columns(i["L1_attn_W_q"]),
        "wo": i["L1_attn_W_o"],
        "wr1": i["L1_ffn_Wr1"],
        "br1": i["L1_ffn_br1"].reshape(32, 1),
        "wr2": i["L1_ffn_Wr2"],
        "br2": _np.tile(i["L1_ffn_br2"], (128, 1)),
        "w1": w1.transpose(1, 0, 2).reshape(128, 36, 128),
        "w2": w2.reshape(36, 128, 128).transpose(1, 0, 2),
        "b1": b1.reshape(36, 128).T,
        "b2": _np.concatenate([i["L1_ffn_be2"], i["L1_ffn_bs2"][None]]),
    }
    nc = _bacc.Bacc("TRN2", target_bir_lowering=False, num_devices=1)
    ins, feed = {}, {}
    for name, a in arrays.items():
        a = _np.ascontiguousarray(a)
        feed["in_" + name] = a
        ins[name] = nc.dram_tensor("in_" + name, a.shape, _mybir.dt.float32, kind="ExternalInput").ap()
    ins["sums"] = nc.dram_tensor("scratch_sums", (4, 512), _mybir.dt.float32, kind="Internal").ap()
    for n in range(2):
        ins[f"gates{n}"] = nc.dram_tensor(f"scratch_gates{n}", (8, 2048), _mybir.dt.float32, kind="Internal").ap()
    ins["out"] = nc.dram_tensor("out_x", (2048, 128), _mybir.dt.float32, kind="ExternalOutput").ap()
    build(nc, ins)
    r = _run(nc, [feed], core_ids=[0])
    return r.results[0]["out_x"].reshape(2, 1024, 128)
```

```python
import numpy as np
from contextlib import ExitStack
import concourse.bass as bass
from concourse import mybir

F32 = mybir.dt.float32
F32R = mybir.dt.float32r
U32 = mybir.dt.uint32
ACT = mybir.ActivationFunctionType
ALU = mybir.AluOpType
AX = mybir.AxisListType
ds, ts = bass.ds, bass.ts

P = 128
E = 128
B, T = 2, 1024
N = B * T
NT = N // P
TT = T // P
BLK = 512
NBLK = N // BLK
TPB = BLK // P
EPS = 1e-5

NEXP, TOPK = 8, 2

H0, D0 = 16, 64
PAIRS = H0 // 2
STEPS0 = B * PAIRS

H1, D1, DR = 16, 8, 32
QUADS = H1 // 4
STEPS1 = B * QUADS
SCALE1 = float(D1 + DR) ** -0.5
MASKED = -1e30

HID1 = 512
CH = HID1 // P


class Mem:
    pass


def layernorm_statistics(nc, v, m):
    for t in range(NT):
        ins = nc.vector.bn_stats(m.stats[:, t, :], m.x[:, t, :])
    ins.then_inc(m.ln_step, 1)
    v.wait_ge(m.ln_step, 1)
    for t in range(NT):
        ins = nc.vector.bn_aggr(m.mv[:, t, :], m.stats[:, t, :])
    ins.then_inc(m.ln_step, 1)
    v.wait_ge(m.std_ready, 1)
    nc.vector.reciprocal(m.rstd[:, :], m.std[:, :]).then_inc(m.ln_step, 1)
    v.wait_ge(m.ln_step, 3)


def deviation(nc, act, m):
    act.wait_ge(m.ln_step, 2)
    nc.scalar.activation(m.std[:, :], m.mv[:, :, 1], ACT.Sqrt, bias=m.eps[:, 0:1]).then_inc(m.std_ready, 1)


def normalise_block(nc, v, m, j, xn_ready, transposed):
    if j >= 2:
        v.wait_ge(transposed, j - 1)
    for t in range(TPB):
        at = TPB * j + t
        ins = nc.vector.tensor_scalar(m.xn[:, j % 2, t, :], m.x[:, at, :], m.mv[:, at, 0:1], m.rstd[:, at:at + 1],
                                      ALU.subtract, ALU.mult)
    ins.then_inc(xn_ready, 1)


def transpose_block(nc, pe, m, j, tr, xn_ready, xt_ready, transposed):
    pe.wait_ge(xn_ready, j + 1)
    if j >= 2:
        pe.wait_ge(xt_ready, j - 1)
    for t in range(TPB):
        ins = nc.tensor.transpose(tr[j % 2][:, ts(t, P)], m.xn[:, j % 2, t, :], m.ident[:, :])
    ins.then_inc(transposed, 1)


def layernorm_buffers(m, sb):
    m.stats = sb("stats", [P, NT, 6])
    m.mv = sb("mv", [P, NT, 2])
    m.rstd = sb("rstd", [P, NT])
    m.std = sb("std", [P, NT])
    m.xn = sb("xn", [P, 2, TPB, E])


def l0_prologue(nc, m, d):
    with ExitStack() as ctx:
        def sb(name, shape, dt=F32):
            return ctx.enter_context(nc.sbuf_tensor(name, shape, dt))

        def pb(name, shape):
            return ctx.enter_context(nc.psum_tensor(name, shape, F32))

        wl = sb("wl", [P, 5 * D0])
        fq = sb("fq", [P, H0, D0])
        fk = sb("fk", [P, H0, D0])
        fv_t = sb("fv_t", [D0, H0, D0])
        fo = sb("fo", [D0, H0, E])
        bv = sb("bv", [D0, H0])
        bo = sb("bo", [P, 1])
        layernorm_buffers(m, lambda name, shape: sb(name + "0", shape))
        xt = [sb(f"xt0_{i}", [P, BLK]) for i in range(2)]
        tr = [pb(f"tr0_{i}", [P, BLK]) for i in range(2)]
        lat = [pb(f"lat{i}", [P, BLK]) for i in range(2)]
        vlat = pb("vlat", [P, TPB, P])
        gp = pb("gp", [P, PAIRS, E])
        cp = pb("cp", [P, 1])

        def sem(name):
            return m.ctx.enter_context(nc.semaphore(name))

        x_in, w_in, const_in = sem("x_in"), sem("w_in"), sem("const_in")
        m.ln_step, m.std_ready = sem("ln_step0"), sem("std_ready0")
        eps_set = sem("eps_set")
        xn_ready, transposed, xt_ready = sem("xn_ready0"), sem("transposed0"), sem("xt_ready0")
        lat_filled, hi_done, lat_read = sem("lat_filled"), sem("lat_hi"), sem("lat_read")
        vlat_filled, vlat_read = sem("vlat_filled"), sem("vlat_read")
        g_filled, w_split = sem("g_filled"), sem("w_split")
        block = ctx.enter_context(nc.Block())

        @block.sync
        def _(sp):
            for j in range(NBLK):
                sp.dma_start(m.x[:, TPB * j:TPB * (j + 1), :],
                             d["x"][BLK * j:BLK * (j + 1), :].rearrange("(t p) e -> p t e", p=P)).then_inc(x_in, 16)
            sp.dma_start(m.ident[:, :], d["ident"]).then_inc(const_in, 16)
            sp.dma_start(wl[:, :], d["wl"]).then_inc(const_in, 16)
            for dst, src in ((fq, d["fq"]), (fk, d["fk"]), (fv_t, d["fv_t"]), (fo, d["fo"])):
                sp.dma_start(dst[:, :, :], src).then_inc(w_in, 16)
            for dst, src in ((bv, d["bv"]), (bo, d["bo"]), (m.qk_bias, d["qk_bias"])):
                sp.dma_start(dst[:, :], src).then_inc(w_in, 16)
            sp.wait_ge(w_in, 16 * 7)

        @block.vector
        def _(v):
            def rest(j):
                for n, dst in enumerate((m.aq, m.ak)):
                    v.wait_ge(hi_done, 2 * j + n + 1)
                    nc.vector.tensor_tensor(dst[D0:P, ds(BLK * j, BLK)], lat[n][D0:P, :],
                                            dst[D0:P, ds(BLK * j, BLK)], ALU.subtract).then_inc(lat_read, 1)

            v.wait_ge(x_in, 16 * NBLK)
            layernorm_statistics(nc, v, m)
            for j in range(NBLK):
                normalise_block(nc, v, m, j, xn_ready, transposed)
                if j:
                    rest(j - 1)
            rest(NBLK - 1)
            v.wait_ge(w_in, 16 * 7)
            for n, src in enumerate((fq, fk)):
                nc.vector.tensor_copy(m.w_all[:, :, 2 * n, :], src[:, :, :]).then_inc(w_split, 1)
                v.wait_ge(w_split, 2 * n + 1)
                nc.vector.tensor_tensor(m.w_all[:, :, 2 * n + 1, :], src[:, :, :], m.w_all[:, :, 2 * n, :],
                                        ALU.subtract).then_inc(w_split, 1)
            v.wait_ge(g_filled, 1)
            nc.vector.tensor_copy(m.g_all[:, :, :], gp[:, :, :])
            nc.vector.tensor_tensor(m.out_bias[:, :], cp[:, :], bo[:, :], ALU.add)

        @block.gpsimd
        def _(pool):
            nc.gpsimd.memset(m.eps[:, :], EPS).then_inc(eps_set, 1)

        @block.scalar
        def _(act):
            act.wait_ge(eps_set, 1)
            deviation(nc, act, m)

            def copy_xt(j):
                act.wait_ge(transposed, j + 1)
                if j >= 2:
                    act.wait_ge(vlat_filled, j - 1)
                nc.scalar.copy(xt[j % 2][:, :], tr[j % 2][:, :]).then_inc(xt_ready, 1)

            copy_xt(0)
            for j in range(NBLK):
                if j + 1 < NBLK:
                    copy_xt(j + 1)
                for n, dst in enumerate((m.aq, m.ak)):
                    act.wait_ge(lat_filled, 2 * j + n + 1)
                    nc.scalar.copy(dst[:, ds(BLK * j, BLK)], lat[n][:, :]).then_inc(hi_done, 1)
                act.wait_ge(vlat_filled, j + 1)
                nc.scalar.copy(m.c_all[:, ds(TPB * j, TPB), :], vlat[:, :, 0:D0]).then_inc(vlat_read, 1)

        @block.tensor
        def _(pe):
            pe.wait_ge(const_in, 32)
            transpose_block(nc, pe, m, 0, tr, xn_ready, xt_ready, transposed)
            for j in range(NBLK):
                if j + 1 < NBLK:
                    transpose_block(nc, pe, m, j + 1, tr, xn_ready, xt_ready, transposed)
                pe.wait_ge(xt_ready, j + 1)
                for n in range(2):
                    if j:
                        pe.wait_ge(lat_read, 2 * (j - 1) + n + 1)
                    nc.tensor.matmul(lat[n][:, :], wl[:, 2 * D0 * n:2 * D0 * (n + 1)], xt[j % 2][:, :],
                                     start=True, stop=True).then_inc(lat_filled, 1)
                if j:
                    pe.wait_ge(vlat_read, j)
                for t in range(TPB):
                    ins = nc.tensor.matmul(vlat[:, t, 0:D0], xt[j % 2][:, ts(t, P)], wl[:, 4 * D0:5 * D0],
                                           start=True, stop=True)
                ins.then_inc(vlat_filled, 1)
            pe.wait_ge(w_in, 16 * 7)
            for h in range(H0):
                lo = D0 * (h % 2)
                nc.tensor.matmul(gp[lo:lo + D0, h // 2, :], fv_t[:, h, :], fo[:, h, :], start=True, stop=True)
            for h in range(H0):
                ins = nc.tensor.matmul(cp[:, :], fo[:, h, :], bv[:, h:h + 1], start=(h == 0), stop=(h == H0 - 1))
            ins.then_inc(g_filled, 1)


def s_units(hh, first, last):
    return [("s", hh, u) for u in range(first, last)]


WITH_FINISH = ([("q", 0, 0), ("q", 0, 1), ("k", 0, 0), ("k", 0, 1), ("q", 1, 0), ("q", 1, 1)]
               + s_units(0, 0, 4) + [("k", 1, 0)] + s_units(0, 4, 8) + [("k", 1, 1), ("l", 0, 0)]
               + s_units(0, 8, 11) + [("r", 0, 0)] + s_units(0, 11, 16) + s_units(1, 0, 1) + [("m", 0, 0)]
               + s_units(1, 1, 4) + [("n", 0, 0)] + s_units(1, 4, 6) + [("g", 0, 0)] + s_units(1, 6, 8)
               + [("g", 0, 1)] + s_units(1, 8, 16) + [("m", 1, 0)])
NEXT_UNITS = [u for u in WITH_FINISH if u[0] in "qksm"]
FINISH_ONLY = [u for u in WITH_FINISH if u[0] in "lrng"]


def psum_units(units):
    return [u for u in units if u[0] not in "rn"]


def position(units, kind, hh, j):
    return psum_units(units).index((kind, hh, j))


N_NEXT, N_STEP = len(psum_units(NEXT_UNITS)), len(psum_units(WITH_FINISH))


def script(units, first):
    left = list(units)
    out = []

    def units_after(n):
        while n and left:
            unit = left.pop(0)
            out.append(("UNIT",) + unit)
            n -= unit[0] not in "rn"

    for kt in range(TT):
        for part in (("ST", kt, 0, 0), ("ST", kt, 0, 1), ("ST", kt, 1, 0), ("ST", kt, 1, 1),
                     ("PV", kt - 1, 0), ("PV", kt - 1, 1)):
            if part[0] == "ST" or kt or not first:
                out.append(part)
                if len(units) > len(FINISH_ONLY):
                    units_after(2 if part[0] == "PV" and part[2] and kt % 2 else 1)
                elif kt % 2 and part[:1] + part[2:] == ("ST", 0, 0):
                    units_after(1)
    units_after(len(left))
    return out


def units_before(n):
    return N_NEXT if isinstance(n, int) and n == 0 else 2 * N_NEXT + N_STEP * (n - 1)


def l0_attention(nc, m, d):
    with ExitStack() as ctx:
        def sb(name, shape, dt=F32):
            return ctx.enter_context(nc.sbuf_tensor(name, shape, dt))

        def sem(name):
            return m.ctx.enter_context(nc.semaphore(name))

        R2 = range(2)
        kk = [[sb(f"kk{a}{h}", [P, T], F32R) for h in R2] for a in R2]
        k2 = [[sb(f"k2_{a}{h}", [P, T], F32R) for h in R2] for a in R2]
        qq = [[sb(f"qq{a}{h}", [P, T], F32R) for h in R2] for a in R2]
        q2 = [[sb(f"q2_{a}{h}", [P, T], F32R) for h in R2] for a in R2]
        w = [sb(f"w{a}", [P, 2, 4, 2, D0], F32R) for a in R2]
        bias = [sb(f"bias{a}", [P, 4]) for a in R2]
        c = [sb(f"c{a}", [P, TT, D0]) for a in R2]
        g = sb("g", [P, E])
        prob = [sb(f"prob{s}", [P, 2, T]) for s in range(4)]
        psum_k = sb("psum_k", [P, 2, T])
        ut = sb("ut", [P, T])
        rsum = sb("rsum", [P, BLK])
        sums_c = sb("sums_c", [P, 2 * T // P])
        inv_c = sb("inv_c", [P, 2 * T // P])
        rb = sb("rb", [P, T])
        on = sb("on", [P, T])
        ones = sb("ones", [P, 32])
        mx = sb("mx", [P, 2, TT, 2])
        mmax = sb("mmax", [P, 2, TT])
        negm = sb("negm", [P, 2, TT])
        mrow = [sb(f"mrow{h}", [TT, P], F32R) for h in R2]
        st = [ctx.enter_context(nc.psum_tensor(f"st{h}", [P, T], F32)) for h in R2]
        pv = ctx.enter_context(nc.psum_tensor("pv", [P, T], F32))
        work = [ctx.enter_context(nc.psum_tensor(f"work{h}", [P, BLK], F32)) for h in R2]

        start_work = work + [st[h][:, ts(j, BLK)] for h in R2 for j in R2]

        cleared = sem("cleared")
        w_loaded, c_loaded = [sem(f"w_loaded{a}") for a in R2], [sem(f"c_loaded{a}") for a in R2]
        row_loaded = [sem(f"row_loaded{h}") for h in R2]
        g_loaded, r_stored, r_loaded = sem("g_loaded"), sem("r_stored"), sem("r_loaded")
        sums_spread, inv_ready = sem("sums_spread"), sem("inv_ready")
        filled, read = sem("work_filled"), sem("work_read")
        hi_done, negm_ready, mmax_ready = sem("hi_done"), sem("negm_ready"), sem("mmax_ready")
        st_filled, exp_done, pv_done, ut_ready = sem("st_filled"), sem("exp_done"), sem("pv_done"), sem("ut_ready")
        summed, norm_done = sem("summed"), sem("norm_done")
        block = ctx.enter_context(nc.Block())

        def steps(eng, step):
            step(0, 0, True, False)
            with eng.Fori(0, (STEPS0 - 2) // 2) as i:
                step(2 * i + 1, 1, False, False)
                step(2 * i + 2, 0, False, False)
            step(STEPS0 - 1, 1, False, True)

        def units_of(first, last):
            return NEXT_UNITS if first else FINISH_ONLY if last else WITH_FINISH

        def load_pair(sp, k, par):
            for copy in R2:
                sp.dma_start(w[par][:, :, :, copy, :].bitcast(F32),
                             m.w_all[:, ds(2 * (k % PAIRS), 2), :, :].bitcast(F32)).then_inc(w_loaded[par], 16)
            sp.dma_start(bias[par][:, :], m.qk_bias[:, ds(4 * (k % PAIRS), 4)]).then_inc(w_loaded[par], 16)

        def load_values(sp, k, par):
            sp.dma_start(c[par][:, :, :], m.c_all[:, ds(TT * (k // PAIRS), TT), :]).then_inc(c_loaded[par], 16)

        def sp_rows(sp, k, par, hh, u):
            sp.wait_ge(read, u + 1)
            sp.dma_start(q2[par][hh][0:1, :].bitcast(F32), mrow[hh][:, :].bitcast(F32)).then_inc(row_loaded[hh], 16)

        def sp_sums(sp, k, u):
            sp.wait_ge(read, u + 1)
            sp.dma_start(sums_c[:, :], rsum[0:P:32, :]).then_inc(sums_spread, 16)
            sp.wait_ge(inv_ready, k + 1)
            sp.dma_start(d["sums"].rearrange("a (p f) -> (a p) f", f=2 * T // P), inv_c[:, :]).then_inc(r_stored, 16)
            sp.wait_ge(r_stored, 16 * (k + 1))
            for hh in R2:
                sp.dma_start(rb[D0 * hh:D0 * (hh + 1), :],
                             d["sums"][2 * hh:2 * hh + 2, :].rearrange("a n -> (a n)").partition_broadcast(D0)
                             ).then_inc(r_loaded, 16)

        @block.sync
        def _(sp):
            load_pair(sp, 0, 0)
            load_values(sp, 0, 0)
            load_pair(sp, 1, 1)

            def rows_of(k, par, units, base):
                seen = 0
                for kind, hh, j in units:
                    if kind == "m":
                        sp_rows(sp, k, par, hh, base + seen)
                    seen += kind not in "rn"

            sp.wait_ge(cleared, 2)
            rows_of(0, 0, NEXT_UNITS, 0)

            def step(n, par, first, last):
                base = units_before(n)
                if not last:
                    sp.wait_ge(read, base)
                    load_pair(sp, n + 2, par)
                    if not first:
                        sp.wait_ge(pv_done, TT * n)
                    load_values(sp, n + 1, 1 - par)
                if not first:
                    if last:
                        sp.wait_ge(read, base)
                    sp.dma_start(g[:, :], m.g_all[:, (n - 1) % PAIRS, :]).then_inc(g_loaded, 16)
                    sp_sums(sp, n - 1, base + position(units_of(first, last), "l", 0, 0))
                if not last:
                    rows_of(n + 1, 1 - par, units_of(first, last), base)

            steps(sp, step)
            sp.wait_ge(read, units_before(STEPS0 - 1) + 3)
            sp.dma_start(g[:, :], m.g_all[:, PAIRS - 1, :]).then_inc(g_loaded, 16)
            sp_sums(sp, STEPS0 - 1, units_before(STEPS0 - 1) + 3)
            for a in R2:
                sp.wait_ge(w_loaded[a], 48 * (STEPS0 // 2) + 48 * (a == 0))
                sp.wait_ge(c_loaded[a], 16 * (STEPS0 // 2))
            sp.wait_ge(r_loaded, 32 * STEPS0)

        @block.gpsimd
        def _(pool):
            for a in R2:
                for h in R2:
                    nc.gpsimd.memset(k2[a][h][0:D0, :].bitcast(F32), 0.0)
                    ins = nc.gpsimd.memset(q2[a][h][0:D0, :].bitcast(F32), 0.0)
            ins.then_inc(cleared, 1)
            pool.wait_ge(cleared, 1)
            for a in R2:
                for h in R2:
                    ins = nc.gpsimd.memset(k2[a][h][0:1, :].bitcast(F32), 1.0)
            nc.gpsimd.memset(ones[:, :], 1.0)
            nc.gpsimd.memset(m.out_t[:, :], 0.0).then_inc(cleared, 1)

            def step(n, par, first, last):
                per = 2 * (TT - 1)
                for kt in range(1, TT):
                    for hh in R2:
                        pool.wait_ge(exp_done, 2 * TT * n + 2 * kt + hh + 1)
                        if kt == 1 and hh == 0 and not first:
                            pool.wait_ge(filled, units_before(n) + position(units_of(first, last), "l", 0, 0) + 1)
                        if kt == 1:
                            nc.gpsimd.tensor_tensor(psum_k[:, hh, :], prob[0][:, hh, :], prob[1][:, hh, :],
                                                    ALU.add).then_inc(summed, 1)
                        else:
                            pool.wait_ge(summed, per * n + 2 * (kt - 1) + hh - 1)
                            nc.gpsimd.tensor_tensor(psum_k[:, hh, :], psum_k[:, hh, :], prob[kt % 4][:, hh, :],
                                                    ALU.add).then_inc(summed, 1)

            steps(pool, step)

        @block.scalar
        def _(act):
            def proj_evac(kind, j, buf, par, hh):
                b = bias[par][:, 2 * hh + (kind == "k"):2 * hh + (kind == "k") + 1]
                cols = ts(j, BLK)
                if kind == "q":
                    nc.scalar.activation(qq[par][hh][:, cols], buf[:, :], ACT.Identity, bias=b
                                         ).then_inc(hi_done, 1)
                else:
                    nc.scalar.activation(k2[par][hh][D0:P, cols], buf[D0:P, :], ACT.Identity, bias=b[D0:P, :]
                                         ).then_inc(hi_done, 1)

            def run(n, par, first, last, todo, base, even, work=work):
                seen = 0
                for what, kind, hh, *j in [t + (0,) * (4 - len(t)) for t in todo]:
                    if what == "UNIT":
                        if kind in "qk":
                            act.wait_ge(filled, base + seen + 1)
                            proj_evac(kind, j[0], work[(even + seen) % len(work)], 1 - par, hh)
                        seen += kind not in "rn"
                    elif what == "PV" and kind < 0 and hh:
                        act.wait_ge(pv_done, TT * n)
                        act.wait_ge(read, base)
                        nc.scalar.copy(ut[:, :], pv[:, :]).then_inc(ut_ready, 1)
                    elif what == "ST" and j[0]:
                        kt = kind
                        at = 2 * TT * n + 2 * kt + hh
                        act.wait_ge(st_filled, at + 1)
                        if not (first and kt < 4):
                            act.wait_ge(pv_done, TT * n + kt - 3)
                            if kt >= 4:
                                act.wait_ge(summed, 14 * n + 2 * max(kt - 4, 1) )
                            else:
                                act.wait_ge(summed, 14 * (n - 1) + 2 * (kt + 4))
                        nc.scalar.activation(prob[kt % 4][:, hh, :], st[hh][:, :], ACT.Exp, scale=D0 ** -0.5
                                             ).then_inc(exp_done, 1)

            act.wait_ge(w_loaded[0], 48)
            run(-1, 1, True, False, [("UNIT",) + u for u in NEXT_UNITS], 0, 0, start_work)

            def step(n, par, first, last):
                if not last:
                    act.wait_ge(w_loaded[1 - par], 48 * ((n + 1) // 2 + 1))
                run(n, par, first, last, script(units_of(first, last), first), units_before(n),
                    0 if first else (1 + par) % 2)

            steps(act, step)
            act.wait_ge(pv_done, TT * STEPS0)
            act.wait_ge(norm_done, STEPS0 - 1)
            nc.scalar.copy(ut[:, :], pv[:, :]).then_inc(ut_ready, 1)

        @block.vector
        def _(v):
            def unit(kind, hh, j, u, buf, par, k):
                cols = ts(j, BLK)
                if kind in "qk":
                    dst, hi = (q2, qq) if kind == "q" else (kk, k2)
                    b = bias[par][D0:P, 2 * hh + (kind == "k"):2 * hh + (kind == "k") + 1]
                    v.wait_ge(hi_done, 8 * k + 4 * hh + 2 * (kind == "k") + j + 1)
                    if kind == "k":
                        nc.vector.tensor_copy(kk[par][hh][0:D0, cols],
                                              k2[par][hh][D0:P, cols].bitcast(F32))
                    nc.vector.scalar_tensor_tensor(dst[par][hh][D0:P, cols], buf[D0:P, :], b,
                                                   hi[par][hh][D0:P, cols], ALU.add, ALU.subtract
                                                   ).then_inc(read, 1)
                elif kind == "s":
                    v.wait_ge(filled, u + 1)
                    nc.vector.reduce_max(mx[:, hh, j // 2, j % 2:j % 2 + 1], buf[:, :], AX.X).then_inc(read, 1)
                elif kind == "m":
                    if not (isinstance(k, int) and k == 0):
                        v.wait_ge(row_loaded[hh], 16 * k)
                    v.wait_ge(filled, u + 1)
                    nc.vector.tensor_copy(mrow[hh][:, :], buf[0:TT, 0:P]).then_inc(read, 1)
                elif kind == "l":
                    v.wait_ge(filled, u + 1)
                    nc.vector.tensor_copy(rsum[:, :], buf[:, :]).then_inc(read, 1)
                elif kind == "g":
                    v.wait_ge(filled, u + 1)
                    out = m.out_t[:, ds(T * (k // PAIRS) + BLK * j, BLK)]
                    nc.vector.tensor_tensor(out, buf[:, :], out, ALU.add).then_inc(read, 1)

            def combine(hh, k, u_last):
                v.wait_ge(read, u_last + 1)
                nc.vector.tensor_tensor(mmax[:, hh, :], mx[:, hh, :, 0], mx[:, hh, :, 1], ALU.max
                                        ).then_inc(mmax_ready, 1)
                v.wait_ge(mmax_ready, 2 * k + hh + 1)
                nc.vector.tensor_scalar(negm[:, hh, :], mmax[:, hh, :], -1.0, None, ALU.mult
                                        ).then_inc(negm_ready, 1)

            def normalise(k):
                v.wait_ge(r_loaded, 32 * (k + 1))
                v.wait_ge(ut_ready, k + 1)
                nc.vector.tensor_tensor(on[:, :], ut[:, :], rb[:, :], ALU.mult).then_inc(norm_done, 1)

            def run(n, par, units, base, even, work=work):
                seen = 0
                for kind, hh, j in units:
                    k = n - 1 if kind in "lrng" else n + 1
                    if kind == "r":
                        v.wait_ge(sums_spread, 16 * (k + 1))
                        nc.vector.reciprocal(inv_c[:, :], sums_c[:, :]).then_inc(inv_ready, 1)
                        continue
                    if kind == "n":
                        normalise(k)
                        continue
                    unit(kind, hh, j, base + seen, work[(even + seen) % len(work)], 1 - par, k)
                    if kind == "s" and j == 2 * TT - 1:
                        combine(hh, k, base + seen)
                    seen += 1

            run(-1, 1, NEXT_UNITS, 0, 0, start_work)
            v.wait_ge(cleared, 2)

            def step(n, par, first, last):
                run(n, par, units_of(first, last), units_before(n), 0 if first else (1 + par) % 2)

            steps(v, step)
            run(STEPS0, 0, FINISH_ONLY, units_before(STEPS0 - 1) + 3, 1)

        @block.tensor
        def _(pe):
            def unit(kind, hh, j, u, buf, par, k, proj_end, turns):
                if not (isinstance(u, int) and u < turns):
                    pe.wait_ge(read, u - turns + 1)
                if kind in "qk":
                    src, part = (m.aq, 0) if kind == "q" else (m.ak, 2)
                    cols = ds(T * (k // PAIRS) + BLK * j, BLK)
                    nc.tensor.matmul(buf[:, :], w[par][:, hh, part, :, :].rearrange("p a d -> p (a d)"), src[:, cols],
                                     start=True, stop=False)
                    ins = nc.tensor.matmul(buf[:, :], w[par][:, hh, part + 1, :, :].rearrange("p a d -> p (a d)"), src[:, cols],
                                           start=False, stop=True)
                elif kind == "s":
                    if j == 0:
                        pe.wait_ge(read, proj_end)
                    ins = nc.tensor.matmul(buf[:, :], qq[par][hh][:, ts(j // 2, P)], kk[par][hh][:, ts(j % 2, BLK)],
                                           start=True, stop=True)
                elif kind == "m":
                    pe.wait_ge(negm_ready, 2 * k + hh + 1)
                    ins = nc.tensor.matmul(buf[0:TT, 0:P], negm[:, hh, :], m.ident[:, :], start=True, stop=True)
                elif kind == "l":
                    pe.wait_ge(summed, 14 * (k + 1))
                    for q in range(4):
                        ins = nc.tensor.matmul(buf[32 * q:32 * (q + 1), :], ones[:, :],
                                               psum_k[:, q // 2, ts(q % 2, BLK)], start=True, stop=True)
                elif kind == "g":
                    pe.wait_ge(norm_done, k + 1)
                    pe.wait_ge(g_loaded, 16 * (k + 1))
                    ins = nc.tensor.matmul(buf[:, :], g[:, :], on[:, ts(j, BLK)], start=True, stop=True)
                ins.then_inc(filled, 1)

            def run(n, par, todo, base, even, first, units, work=work):
                seen = 0
                for what, *rest in todo:
                    if what == "UNIT":
                        kind, hh, j = rest
                        if kind not in "rn":
                            unit(kind, hh, j, base + seen, work[(even + seen) % len(work)], 1 - par,
                                 n - 1 if kind in "lg" else n + 1,
                                 base + position(units, "k", hh, 1) + 1 if kind == "s" else None, len(work))
                            seen += 1
                    elif what == "ST":
                        kt, hh, j = rest
                        at = 2 * TT * n + 2 * kt + hh
                        if j == 0 and not (first and kt == 0):
                            pe.wait_ge(exp_done, at - 1)
                        if kt == 0 and j == 0:
                            pe.wait_ge(row_loaded[hh], 16 * (n + 1))
                        for part, (ka, qa) in enumerate(((kk, qq), (k2, q2))):
                            ins = nc.tensor.matmul(st[hh][:, ts(j, BLK)], ka[par][hh][:, ts(kt, P)],
                                                   qa[par][hh][:, ts(j, BLK)],
                                                   start=(part == 0), stop=(part == 1))
                        if j:
                            ins.then_inc(st_filled, 1)
                    else:
                        kt, j = rest
                        if j == 0:
                            pe.wait_ge(exp_done, 2 * TT * n + 2 * kt + 2)
                        if kt == 0 and j == 0:
                            pe.wait_ge(c_loaded[par], 16 * (n // 2 + 1))
                            if not first:
                                pe.wait_ge(ut_ready, n)
                        product(kt % TT, j, par if kt >= 0 else 1 - par)

            def product(kt, j, par):
                for hh in R2:
                    ins = nc.tensor.matmul(pv[D0 * hh:D0 * (hh + 1), ts(j, BLK)], c[par][:, kt, :],
                                           prob[kt % 4][:, hh, ts(j, BLK)],
                                           start=(kt == 0), stop=(kt == TT - 1))
                if j:
                    ins.then_inc(pv_done, 1)

            pe.wait_ge(w_loaded[0], 48)
            run(-1, 1, [("UNIT",) + u for u in NEXT_UNITS], 0, 0, True, NEXT_UNITS, start_work)
            pe.wait_ge(cleared, 2)
            pe.wait_ge(read, N_NEXT)

            def step(n, par, first, last):
                if not last:
                    pe.wait_ge(w_loaded[1 - par], 48 * ((n + 1) // 2 + 1))
                units = units_of(first, last)
                run(n, par, script(units, first), units_before(n), 0 if first else (1 + par) % 2, first, units)

            steps(pe, step)
            pe.wait_ge(exp_done, 2 * TT * STEPS0)
            for j in range(2):
                product(TT - 1, j, (STEPS0 - 1) % 2)
            run(STEPS0, 0, [("UNIT",) + u for u in FINISH_ONLY], units_before(STEPS0 - 1) + 3, 1, False, FINISH_ONLY)


def residual_out(nc, m, d):
    with ExitStack() as ctx:
        ob = ctx.enter_context(nc.sbuf_tensor("ob", [P, BLK], F32))
        tr = ctx.enter_context(nc.psum_tensor("trr", [P, TPB, P], F32))

        def sem(name):
            return m.ctx.enter_context(nc.semaphore(name))
        ob_ready, transposed, added = sem("ob_ready"), sem("tr_r"), sem("added_r")
        block = ctx.enter_context(nc.Block())

        @block.scalar
        def _(act):
            for j in range(NBLK):
                if j:
                    act.wait_ge(transposed, j)
                nc.scalar.activation(ob[:, :], m.out_t[:, ts(j, BLK)], ACT.Identity, bias=m.out_bias[:, 0:1]
                                     ).then_inc(ob_ready, 1)

        @block.tensor
        def _(pe):
            for j in range(NBLK):
                pe.wait_ge(ob_ready, j + 1)
                if j:
                    pe.wait_ge(added, j)
                for t in range(TPB):
                    ins = nc.tensor.transpose(tr[:, t, :], ob[:, ts(t, P)], m.ident[:, :])
                ins.then_inc(transposed, 1)

        @block.vector
        def _(v):
            for j in range(NBLK):
                v.wait_ge(transposed, j + 1)
                xs = m.x[:, TPB * j:TPB * (j + 1), :]
                nc.vector.tensor_tensor(xs, tr[:, :, :], xs, ALU.add).then_inc(added, 1)


def spread_gates(sp, m, gates, j):
    sp.dma_start(m.gb[:, j % 2, :, :], gates[:, ts(j, BLK)].partition_broadcast(P)).then_inc(m.spread, 16)


def spread_later_gates(sp, m, gates, added):
    for j in range(1, NBLK):
        if j >= 2:
            sp.wait_ge(added, j - 1)
        spread_gates(sp, m, gates, j)
        sp.wait_ge(m.spread, 16 * (j + 1))


def split_chunks(m):
    width = 9 * P
    out = []
    for arrays in m.split:
        flat = [a[:, :, :].rearrange("p u d -> p (u d)") for a in arrays]
        size = flat[0].shape[1]
        for at in range(0, size, width):
            out.append([a[:, at:min(at + width, size)] for a in flat])
    return out


def split_product(nc, out, w_lead, w_rest, x_lead, x_rest, start, stop):
    nc.tensor.matmul(out, w_lead, x_lead, start=start, stop=False)
    nc.tensor.matmul(out, w_lead, x_rest, start=False, stop=False)
    return nc.tensor.matmul(out, w_rest, x_lead, start=False, stop=stop)


def router(nc, m, d, layer, w_dram, w1_dram, b1_dram, b2_dram):
    L = str(layer)
    with ExitStack() as ctx:
        def sb(name, shape, dt=F32):
            return ctx.enter_context(nc.sbuf_tensor(name + "_r" + L, shape, dt))

        def sem(name):
            return m.ctx.enter_context(nc.semaphore(name + "_r" + L))

        wr = sb("wr", [P if layer == 0 else HR, NEXP])
        if layer == 1:
            wr1 = sb("wr1", [P, HR])
            br1 = sb("br1", [HR, 1])
            br2 = sb("br2", [P, NEXP])
            hr = sb("hr", [HR, N])
        iota = sb("iota", [P, NEXP])
        layernorm_buffers(m, sb)
        shape = [P, NT, NEXP]
        lg, ex, probs, top, oh, gate = (sb(n, shape) for n in ("lg", "ex", "probs", "top", "oh", "gate"))
        idx = sb("idx", shape, U32)
        idxf = sb("idxf", [P, NT, TOPK])
        col = sb("col", [P, 8, NT])
        tr = [ctx.enter_context(nc.psum_tensor(f"tr_r{L}{i}", [P, BLK], F32)) for i in range(2)]
        hp = ctx.enter_context(nc.psum_tensor("hp_r" + L, [P, BLK], F32))
        lp = ctx.enter_context(nc.psum_tensor("lp_r" + L, [P, NT, NEXP], F32))
        gp = ctx.enter_context(nc.psum_tensor("gp_r" + L, [P, N], F32))
        loaded, m.ln_step, m.std_ready = sem("loaded"), sem("ln_step"), sem("std_ready")
        xn_ready, transposed, xt_ready = sem("xn_ready"), sem("transposed"), sem("xt_ready")
        hid_filled, hid_ready, logits_done = sem("hid_filled"), sem("hid_ready"), sem("logits_done")
        step, shifted, exp_done, gate_ready = sem("step"), sem("shifted"), sem("exp_done"), sem("gate_ready")
        x_split, w_lead, experts_loaded = sem("x_split"), sem("w_lead"), sem("experts_loaded")
        sources = m.split
        m.split = [(sb(f"whole{n}", lead.shape), lead, rest) for n, (_, lead, rest) in enumerate(sources)]
        rows_filled, rows_ready, stored, m.spread = sem("rows_filled"), sem("rows_ready"), sem("stored"), sem("spread")
        block = ctx.enter_context(nc.Block())
        n_loads = 2 if layer == 0 else 5
        chunks = split_chunks(m)
        first_chunks = len(chunks) // 2

        @block.sync
        def _(sp):
            sp.dma_start(wr[:, :], w_dram).then_inc(loaded, 16)
            sp.dma_start(iota[:, :], d["iota"]).then_inc(loaded, 16)
            if layer == 1:
                for dst, src in ((wr1, w1_dram), (br1, b1_dram), (br2, b2_dram)):
                    sp.dma_start(dst[:, :], src).then_inc(loaded, 16)
            for (whole, _, _), (src, _, _) in zip(m.split, sources):
                sp.dma_start(whole[:, :, :], src).then_inc(experts_loaded, 16)
            m.load_biases(sp)
            sp.wait_ge(rows_ready, 2)
            gates = d["gates0"] if layer == 0 else d["gates1"]
            sp.dma_start(gates, m.gate_t[0:NEXP, :]).then_inc(stored, 16)
            sp.wait_ge(stored, 16)
            spread_gates(sp, m, gates, 0)
            sp.wait_ge(m.spread, 16)
            m.await_biases(sp)

        @block.gpsimd
        def _(pool):
            nc.gpsimd.memset(m.gate_t[:, :], 1.0).then_inc(rows_ready, 1)
            for j in range(NBLK):
                pool.wait_ge(xt_ready, j + 1)
                nc.gpsimd.tensor_copy(m.xt_lead[:, ts(j, BLK)], m.xt_all[:, ts(j, BLK)]).then_inc(x_split, 1)
                pool.wait_ge(x_split, 2 * j + 1)
                nc.gpsimd.tensor_tensor(m.xt_rest[:, ts(j, BLK)], m.xt_all[:, ts(j, BLK)], m.xt_lead[:, ts(j, BLK)],
                                        ALU.subtract).then_inc(x_split, 1)

        @block.vector
        def _(v):
            count = [0]

            def link(ins):
                count[0] += 1
                ins.then_inc(step, 1)
                v.wait_ge(step, count[0])

            def split_rest(start, end):
                for n in range(start, end):
                    whole, lead, rest = chunks[n]
                    v.wait_ge(w_lead, n + 1)
                    nc.vector.tensor_tensor(rest, whole, lead, ALU.subtract)

            layernorm_statistics(nc, v, m)
            for j in range(NBLK):
                normalise_block(nc, v, m, j, xn_ready, transposed)
            split_rest(0, first_chunks)
            v.wait_ge(loaded, 16 * n_loads)
            v.wait_ge(logits_done, 1)
            if layer == 0:
                link(nc.vector.tensor_copy(lg[:, :, :], lp[:, :, :]))
            else:
                link(nc.vector.tensor_tensor(lg[:, :, :], lp[:, :, :],
                                             br2[:, :].unsqueeze(1).to_broadcast(shape), ALU.add))
            link(nc.vector.reduce_max(col[:, 0, :], lg[:, :, :], AX.X))
            nc.vector.tensor_tensor(lg[:, :, :], lg[:, :, :], col[:, 0, :].unsqueeze(2).to_broadcast(shape),
                                    ALU.subtract).then_inc(shifted, 1)
            v.wait_ge(exp_done, 1)
            link(nc.vector.reduce_sum(col[:, 1, :], ex[:, :, :], AX.X))
            link(nc.vector.reciprocal(col[:, 2, :], col[:, 1, :]))
            link(nc.vector.tensor_tensor(probs[:, :, :], ex[:, :, :],
                                         col[:, 2, :].unsqueeze(2).to_broadcast(shape), ALU.mult))
            for t in range(NT):
                ins = nc.vector.max(top[:, t, :], probs[:, t, :])
            link(ins)
            for t in range(NT):
                ins = nc.vector.max_index(idx[:, t, :], top[:, t, :], probs[:, t, :])
            link(ins)
            link(nc.vector.tensor_copy(idxf[:, :, :], idx[:, :, 0:TOPK]))
            if layer == 0:
                link(nc.vector.tensor_tensor(col[:, 3, :], top[:, :, 0], top[:, :, 1], ALU.add))
                link(nc.vector.reciprocal(col[:, 4, :], col[:, 3, :]))
                nc.vector.tensor_tensor(col[:, 5, :], top[:, :, 0], col[:, 4, :], ALU.mult)
                link(nc.vector.tensor_tensor(col[:, 6, :], top[:, :, 1], col[:, 4, :], ALU.mult))
            else:
                nc.vector.tensor_tensor(col[:, 3, :], top[:, :, 1], top[:, :, 0], ALU.subtract).then_inc(shifted, 1)
                v.wait_ge(exp_done, 2)
                link(nc.vector.tensor_scalar(col[:, 4, :], col[:, 7, :], 1.0, None, ALU.add))
                link(nc.vector.reciprocal(col[:, 5, :], col[:, 4, :]))
                link(nc.vector.tensor_tensor(col[:, 6, :], col[:, 7, :], col[:, 5, :], ALU.mult))
            iota_b = iota[:, :].unsqueeze(1).to_broadcast(shape)
            link(nc.vector.tensor_tensor(oh[:, :, :], iota_b, idxf[:, :, 0:1].to_broadcast(shape), ALU.is_equal))
            link(nc.vector.tensor_tensor(gate[:, :, :], oh[:, :, :], col[:, 5, :].unsqueeze(2).to_broadcast(shape),
                                         ALU.mult))
            link(nc.vector.tensor_tensor(oh[:, :, :], iota_b, idxf[:, :, 1:2].to_broadcast(shape), ALU.is_equal))
            link(nc.vector.tensor_tensor(oh[:, :, :], oh[:, :, :], col[:, 6, :].unsqueeze(2).to_broadcast(shape),
                                         ALU.mult))
            nc.vector.tensor_tensor(gate[:, :, :], gate[:, :, :], oh[:, :, :], ALU.add).then_inc(gate_ready, 1)
            v.wait_ge(rows_ready, 1)
            v.wait_ge(rows_filled, 1)
            nc.vector.tensor_copy(m.gate_t[0:NEXP, :], gp[0:NEXP, :]).then_inc(rows_ready, 1)
            split_rest(first_chunks, len(chunks))

        @block.scalar
        def _(act):
            def split_lead(start, end):
                for whole, lead, _ in chunks[start:end]:
                    nc.scalar.copy(lead, whole).then_inc(w_lead, 1)

            if layer == 1:
                act.wait_ge(loaded, 16 * n_loads)
            deviation(nc, act, m)
            for j in range(NBLK):
                act.wait_ge(transposed, j + 1)
                nc.scalar.copy(m.xt_all[:, ts(j, BLK)], tr[j % 2][:, :]).then_inc(xt_ready, 1)
                if layer == 1:
                    act.wait_ge(hid_filled, j + 1)
                    nc.scalar.activation(hr[:, ts(j, BLK)], hp[0:HR, :], ACT.Relu, bias=br1[:, 0:1]
                                         ).then_inc(hid_ready, 1)
            act.wait_ge(experts_loaded, 16 * len(m.split))
            split_lead(0, first_chunks)
            act.wait_ge(shifted, 1)
            nc.scalar.activation(ex[:, :, :], lg[:, :, :], ACT.Exp).then_inc(exp_done, 1)
            if layer == 1:
                act.wait_ge(shifted, 2)
                nc.scalar.activation(col[:, 7, :], col[:, 3, :], ACT.Exp, scale=1.0 / TOPK).then_inc(exp_done, 1)
            split_lead(first_chunks, len(chunks))

        @block.tensor
        def _(pe):
            pe.wait_ge(loaded, 16 * n_loads)
            transpose_block(nc, pe, m, 0, tr, xn_ready, xt_ready, transposed)
            for j in range(NBLK):
                if j + 1 < NBLK:
                    transpose_block(nc, pe, m, j + 1, tr, xn_ready, xt_ready, transposed)
                pe.wait_ge(xt_ready, j + 1)
                if layer == 1:
                    if j:
                        pe.wait_ge(hid_ready, j)
                    nc.tensor.matmul(hp[0:HR, :], wr1[:, :], m.xt_all[:, ts(j, BLK)], start=True, stop=True
                                     ).then_inc(hid_filled, 1)
                    pe.wait_ge(hid_ready, j + 1)
                src = m.xt_all if layer == 0 else hr
                for t in range(TPB * j, TPB * (j + 1)):
                    ins = nc.tensor.matmul(lp[:, t, :], src[:, ts(t, P)], wr[:, :], start=True, stop=True)
            ins.then_inc(logits_done, 1)
            pe.wait_ge(gate_ready, 1)
            for t in range(NT):
                ins = nc.tensor.matmul(gp[0:NEXP, ts(t, P)], gate[:, t, :], m.ident[:, :], start=True, stop=True)
            ins.then_inc(rows_filled, 1)


HR = E // 4


def experts0(nc, m, d):
    with ExitStack() as ctx:
        def sb(name, shape, dt=F32):
            return ctx.enter_context(nc.sbuf_tensor(name, shape, dt))

        def pb(name, shape):
            return ctx.enter_context(nc.psum_tensor(name, shape, F32))

        def sem(name):
            return m.ctx.enter_context(nc.semaphore(name))

        R = 4
        s = [sb(f"silu0_{i}", [P, BLK]) for i in range(2)]
        hid = [sb(f"hid0_{i}", [P, BLK]) for i in range(R)]
        lead = [sb(f"hid0_lead{i}", [P, BLK], F32R) for i in range(R)]
        rest = [sb(f"hid0_rest{i}", [P, BLK], F32R) for i in range(R)]
        ob = sb("ob0", [P, BLK])
        h1 = [pb(f"h1_{i}", [P, BLK]) for i in range(2)]
        h2 = [pb(f"h2_{i}", [P, BLK]) for i in range(2)]
        out = pb("out0", [P, BLK])
        tr = pb("tr_e0", [P, TPB, P])
        up_done, silu_done, gated, hid_done = sem("up_done0"), sem("silu_done0"), sem("gated0"), sem("hid_done0")
        lead_done, rest_done = sem("lead_done0"), sem("rest_done0")
        down_done, ob_ready, transposed, added = sem("down_done0"), sem("ob_ready0"), sem("tr_done0"), sem("added0")
        block = ctx.enter_context(nc.Block())

        @block.sync
        def _(sp):
            spread_later_gates(sp, m, d["gates0"], added)

        @block.tensor
        def _(pe):
            with pe.Fori(0, NBLK) as j:
                cols = ds(BLK * j, BLK)

                def down(e):
                    pe.wait_ge(rest_done, NEXP * j + e + 1)
                    split_product(nc, out[:, :], m.down_lead[:, e, :], m.down_rest[:, e, :],
                                  lead[e % R][:, :], rest[e % R][:, :], e == 0, e == NEXP - 1
                                  ).then_inc(down_done, 1)

                for e in range(NEXP):
                    if e >= 2:
                        pe.wait_ge(hid_done, NEXP * j + e - 1)
                    for half, h in ((0, h1), (1, h2)):
                        part = ts(half, P)
                        ins = split_product(nc, h[e % 2][:, :], m.up_lead[:, e, part],
                                            m.up_rest[:, e, part], m.xt_lead[:, cols], m.xt_rest[:, cols],
                                            True, True)
                    ins.then_inc(up_done, 1)
                    if e >= R - 1:
                        down(e - R + 1)
                for e in range(NEXP - R + 1, NEXP):
                    down(e)
                pe.wait_ge(ob_ready, j + 1)
                for t in range(TPB):
                    ins = nc.tensor.transpose(tr[:, t, :], ob[:, ts(t, P)], m.ident[:, :])
                ins.then_inc(transposed, 1)

        @block.scalar
        def _(act):
            with act.Fori(0, NBLK) as j:
                def leading(e):
                    act.wait_ge(hid_done, NEXP * j + e + 1)
                    if e >= R:
                        act.wait_ge(down_done, NEXP * j + e - R + 1)
                    nc.scalar.copy(lead[e % R][:, :], hid[e % R][:, :]).then_inc(lead_done, 1)

                for e in range(NEXP):
                    act.wait_ge(up_done, NEXP * j + e + 1)
                    if e >= 2:
                        act.wait_ge(hid_done, NEXP * j + e - 1)
                    nc.scalar.activation(s[e % 2][:, :], h1[e % 2][:, :], ACT.Silu).then_inc(silu_done, 1)
                    if e:
                        leading(e - 1)
                leading(NEXP - 1)
                act.wait_ge(down_done, NEXP * (j + 1))
                nc.scalar.copy(ob[:, :], out[:, :]).then_inc(ob_ready, 1)

        @block.gpsimd
        def _(pool):
            with pool.Fori(0, NBLK) as j:
                for e in range(NEXP):
                    pool.wait_ge(lead_done, NEXP * j + e + 1)
                    nc.gpsimd.tensor_tensor(rest[e % R][:, :], hid[e % R][:, :], lead[e % R][:, :], ALU.subtract
                                            ).then_inc(rest_done, 1)

        @block.vector
        def _(v):
            with v.Fori(0, NBLK) as j:
                v.wait_ge(m.spread, 16 * (j + 1))
                for e in range(NEXP):
                    at = NEXP * j + e
                    v.wait_ge(up_done, at + 1)
                    if e >= R:
                        v.wait_ge(rest_done, at - R + 1)
                    nc.vector.tensor_tensor(hid[e % R][:, :], h2[e % 2][:, :], m.gb[:, j % 2, e, :], ALU.mult
                                            ).then_inc(gated, 1)
                    v.wait_ge(gated, at + 1)
                    v.wait_ge(silu_done, at + 1)
                    nc.vector.tensor_tensor(hid[e % R][:, :], hid[e % R][:, :], s[e % 2][:, :], ALU.mult
                                            ).then_inc(hid_done, 1)
                v.wait_ge(transposed, j + 1)
                xs = m.x[:, ds(TPB * j, TPB), :]
                nc.vector.tensor_tensor(xs, tr[:, :, :], xs, ALU.add).then_inc(added, 1)


def l1_prologue(nc, m, d):
    with ExitStack() as ctx:
        def sb(name, shape, dt=F32):
            return ctx.enter_context(nc.sbuf_tensor(name, shape, dt))

        def pb(name, shape):
            return ctx.enter_context(nc.psum_tensor(name, shape, F32))

        def sem(name):
            return m.ctx.enter_context(nc.semaphore(name))

        wkv = sb("wkv", [P, E])
        wv = sb("wv1", [P, E])
        wrope = sb("wrope", [P, 4, P])
        cs = sb("cs", [P, 2, T])
        masks = sb("masks", [P, 2, P])
        layernorm_buffers(m, lambda name, shape: sb(name + "1", shape))
        ca, cb, rot, low = ([sb(f"{n}{i}", [P, BLK]) for i in range(2)] for n in ("ca", "cb", "rot", "low"))
        hi = [sb(f"hi1_{i}", [P, BLK], F32R) for i in range(2)]
        tr = [pb(f"tr1_{i}", [P, BLK]) for i in range(2)]
        ckp = pb("ckp", [P, BLK])
        vp = pb("vp", [P, TPB, E])
        rp = [[pb(f"rp{i}{s}", [P, BLK]) for s in range(2)] for i in range(2)]
        rotary = ((m.xt_all, m.qr, 1), (m.ck_all, m.kr, 0))
        loaded, m.ln_step, m.std_ready = sem("loaded1"), sem("ln_step1"), sem("std_ready1")
        xn_ready, transposed, xt_ready = sem("xn_ready1"), sem("transposed1"), sem("xt_ready1")
        ck_filled, ck_ready, v_filled, v_read = sem("ck_filled"), sem("ck_ready"), sem("v_filled"), sem("v_read")
        r_filled, r_read, rot_step, hi_ready, packed = (sem("r_filled"), sem("r_read"), sem("rot_step"),
                                                        sem("hi_ready"), sem("packed"))
        cleared, m_ready = sem("v_cleared"), sem("m_ready")
        block = ctx.enter_context(nc.Block())

        @block.sync
        def _(sp):
            for dst, src in ((wkv, d["wkv"]), (wv, d["wv1"]), (m.coef, d["coef"])):
                sp.dma_start(dst[:, :], src).then_inc(loaded, 16)
            for dst, src in ((wrope, d["wrope"]), (cs, d["cs"]), (masks, d["masks"]), (m.wk_all, d["wk1"]), (m.wq_all, d["wq1"])):
                sp.dma_start(dst[:, :, :], src).then_inc(loaded, 16)
            sp.wait_ge(loaded, 16 * 8)

        v_rows = m.v_all[:, :, :, :, :, :].rearrange("p b q t g d -> p (b q t g) d")

        @block.gpsimd
        def _(pool):
            nc.gpsimd.memset(v_rows, 0.0).then_inc(cleared, 1)
            pool.wait_ge(cleared, 1)
            nc.gpsimd.memset(v_rows[:, :, D1:D1 + 1], 1.0).then_inc(cleared, 1)

        @block.vector
        def _(v):
            layernorm_statistics(nc, v, m)

            def rotate(u):
                v.wait_ge(r_filled, u + 1)
                if u >= 2:
                    v.wait_ge(hi_ready, u - 1)
                pos = ds(BLK * (u // 2 % 2), BLK)
                nc.vector.tensor_tensor(ca[u % 2][:, :], rp[u % 2][0][:, :], cs[:, 0, pos], ALU.mult)
                nc.vector.tensor_tensor(cb[u % 2][:, :], rp[u % 2][1][:, :], cs[:, 1, pos], ALU.mult).then_inc(r_read, 1)
                v.wait_ge(r_read, u + 1)
                nc.vector.tensor_tensor(rot[u % 2][:, :], ca[u % 2][:, :], cb[u % 2][:, :], ALU.add
                                        ).then_inc(rot_step, 1)

            def pack(u):
                v.wait_ge(hi_ready, u + 1)
                _, dst, n = rotary[u % 2]
                nc.vector.scalar_tensor_tensor(dst[:, ts(u // 2, BLK)], hi[u % 2][:, :].bitcast(F32),
                                               m.coef[:, 3 + 2 * n:4 + 2 * n], low[u % 2][:, :], ALU.mult, ALU.add
                                               ).then_inc(packed, 1)

            normalise_block(nc, v, m, 0, xn_ready, transposed)
            normalise_block(nc, v, m, 1, xn_ready, transposed)
            v.wait_ge(loaded, 16 * 8)
            v.wait_ge(cleared, 2)
            nc.vector.tensor_copy(m.identr[:, :], m.ident[:, :])
            nc.vector.tensor_copy(m.maskr[:, :, :], masks[:, :, :]).then_inc(m_ready, 1)
            for j in range(NBLK):
                rotate(2 * j)
                if j:
                    pack(2 * j - 1)
                if j + 2 < NBLK:
                    normalise_block(nc, v, m, j + 2, xn_ready, transposed)
                v.wait_ge(v_filled, j + 1)
                for t in range(TPB):
                    ins = nc.vector.tensor_copy(m.v_all[:, j // 2, :, TPB * (j % 2) + t, :, 0:D1],
                                                vp[:, t, :].rearrange("p (q g d) -> p q g d", q=QUADS, d=D1))
                ins.then_inc(v_read, 1)
                rotate(2 * j + 1)
                pack(2 * j)
            pack(2 * NBLK - 1)

        @block.scalar
        def _(act):
            deviation(nc, act, m)

            def copy_xt(j):
                act.wait_ge(transposed, j + 1)
                nc.scalar.copy(m.xt_all[:, ts(j, BLK)], tr[j % 2][:, :]).then_inc(xt_ready, 1)

            copy_xt(0)
            act.wait_ge(loaded, 16 * 8)
            for j in range(NBLK):
                if j + 1 < NBLK:
                    copy_xt(j + 1)
                act.wait_ge(ck_filled, j + 1)
                nc.scalar.copy(m.ck_all[:, ts(j, BLK)], ckp[:, :]).then_inc(ck_ready, 1)
                for u in (2 * j, 2 * j + 1):
                    act.wait_ge(rot_step, u + 1)
                    if u >= 2:
                        act.wait_ge(packed, u - 1)
                    c = 2 + 2 * rotary[u % 2][2]
                    nc.scalar.activation(low[u % 2][:, :], rot[u % 2][:, :], ACT.Copy, scale=m.coef[:, c:c + 1])
                    nc.scalar.copy(hi[u % 2][:, :], rot[u % 2][:, :]).then_inc(hi_ready, 1)

        @block.tensor
        def _(pe):
            transpose_block(nc, pe, m, 0, tr, xn_ready, xt_ready, transposed)
            pe.wait_ge(loaded, 16 * 8)
            for j in range(NBLK):
                if j + 1 < NBLK:
                    transpose_block(nc, pe, m, j + 1, tr, xn_ready, xt_ready, transposed)
                pe.wait_ge(xt_ready, j + 1)
                if j:
                    pe.wait_ge(ck_ready, j)
                nc.tensor.matmul(ckp[:, :], wkv[:, :], m.xt_all[:, ts(j, BLK)], start=True, stop=True
                                 ).then_inc(ck_filled, 1)
                for u in (2 * j, 2 * j + 1):
                    if u % 2:
                        pe.wait_ge(ck_ready, j + 1)
                        if j:
                            pe.wait_ge(v_read, j)
                        for t in range(TPB):
                            ins = nc.tensor.matmul(vp[:, t, :], m.ck_all[:, ts(TPB * j + t, P)], wv[:, :],
                                                   start=True, stop=True)
                        ins.then_inc(v_filled, 1)
                    if u >= 2:
                        pe.wait_ge(r_read, u - 1)
                    src, _, n = rotary[u % 2]
                    for s in range(2):
                        ins = nc.tensor.matmul(rp[u % 2][s][:, :], wrope[:, 2 * n + s, :], src[:, ts(j, BLK)],
                                               start=True, stop=True)
                    ins.then_inc(r_filled, 1)


def s_pieces():
    out = []
    for t in range(TT):
        width = (t + 1) * P
        if width <= BLK:
            out.append((t, 0, width, True))
        else:
            out += [(t, 0, BLK, False), (t, BLK, width - BLK, True)]
    return out


PIECES = s_pieces()
EARLY = [u for u in range(len(PIECES)) if PIECES[u][0] < TPB]
LATE = [u for u in range(len(PIECES)) if PIECES[u][0] >= TPB]


def s_early(first, last):
    return [("s", g, u) for g in range(4) for u in EARLY][first:last]


def s_late():
    out = [("s", g, u) for g in range(4) for u in LATE]
    for g in range(3):
        out.insert(len(LATE) * (g + 1) + 2 + g, ("m", g, 0))
    return out + [("m", 3, 0)]


PROJ1 = [("k", 0, 0), ("q", 0, 0), ("k", 0, 1), ("q", 0, 1)]
START1 = PROJ1 + s_early(0, None) + PROJ1 + s_late()
NEXT1 = (PROJ1[:1] + s_early(0, 2) + PROJ1[1:2] + s_early(2, 8) + PROJ1[2:3] + s_early(8, 10) + PROJ1[3:]
         + s_early(10, None) + s_late())
FINISH1 = [("t", 0, 0), ("t", 0, 1)]
FULL1 = FINISH1 + NEXT1
AT_TILE = [8, 8, 8, 8, 7, 7, 6, 5]


def before_last_projection(units, seen):
    same = [i for i in range(seen) if units[i][0] == units[seen][0]]
    return same[-1] if same else None


def quads_ahead(units, seen):
    kind = units[seen][0]
    return 1 + (kind in "kq" and not (units is START1 and seen < len(PROJ1)))


def script1(units):
    left, out = list(units), []
    for kt in range(TT):
        parts = [("ST", kt, g) for g in range(4)]
        if kt:
            parts += [("PV", kt - 1, n) for n in range(len(q_pieces(kt - 1)))]
        for n, part in enumerate(parts):
            out.append(part)
            for _ in range(AT_TILE[kt] * (n + 1) // len(parts) - AT_TILE[kt] * n // len(parts)):
                if left:
                    out.append(("UNIT",) + left.pop(0))
    out.append(("PV", TT - 1, 0))
    return out + [("UNIT",) + u for u in left]


def units_before1(n):
    at_0 = len(START1)
    return at_0 if isinstance(n, int) and n == 0 else at_0 + len(NEXT1) + len(FULL1) * (n - 1)


def q_pieces(kt):
    lo = P * kt
    return [(lo, BLK), (BLK, T)] if lo < BLK else [(lo, T)]


def l1_attention(nc, m, d):
    with ExitStack() as ctx:
        def sb(name, shape, dt=F32):
            return ctx.enter_context(nc.sbuf_tensor(name, shape, dt))

        def sem(name):
            return m.ctx.enter_context(nc.semaphore(name))

        R2, R4 = range(2), range(4)
        HEAD = 3 * DR
        ROW = HEAD + 3 * D1
        kk = [sb(f"l1_kk{a}", [P, 4, T], F32R) for a in R2]
        qq = [sb(f"l1_qq{a}", [P, 4, T], F32R) for a in R2]
        wk, wq = sb("l1_wk", [P, P]), sb("l1_wq", [P, P])
        val = [sb(f"l1_v{a}", [P, TT, 4, 32]) for a in R2]
        prob = [sb(f"l1_prob{s}", [P, 4, T]) for s in R2]
        low = [sb(f"l1_low{i}", [P, BLK]) for i in R2]
        hi = [sb(f"l1_hi{i}", [P, BLK], F32R) for i in R2]
        head = [sb(f"l1_head{s}", [P, T], F32R) for s in R2]
        ut = sb("l1_ut", [P, T])
        mx = sb("l1_mx", [P, 4, TT, 2])
        mmax = sb("l1_mmax", [P, 4, TT])
        negm = sb("l1_negm", [P, 4, TT])
        mrow = [sb(f"l1_mrow{g}", [TT, P], F32R) for g in R4]
        rs = sb("l1_rs", [P, 2, TPB, 4])
        st = [ctx.enter_context(nc.psum_tensor(f"l1_st{h}", [P, T], F32)) for h in R2]
        pv = ctx.enter_context(nc.psum_tensor("l1_pv", [P, T], F32))
        work = [ctx.enter_context(nc.psum_tensor(f"l1_work{h}", [P, BLK], F32)) for h in R2]

        start_work = work + [st[h][:, ts(j, BLK)] for h in R2 for j in R2]

        cleared = sem("cleared1")
        w_loaded = sem("l1_w_loaded")
        val_loaded, rope_copied = [sem(f"val_loaded{a}") for a in R2], sem("rope_copied")
        rope_loaded, k_loaded, q_loaded = ([[sem(f"{name}_loaded{a}{j}") for j in R2] for a in R2]
                                           for name in ("rope", "k", "q"))
        row_loaded = [sem(f"row_loaded1{g}") for g in R4]
        filled, read, halves = sem("work_filled1"), sem("work_read1"), sem("halves")
        negm_ready, mmax_ready, rs_ready = sem("negm_ready1"), sem("mmax_ready1"), sem("rs_ready")
        st_filled, exp_done, pv_done, ut_ready = sem("st_filled1"), sem("exp_done1"), sem("pv_done1"), sem("ut_ready1")
        block = ctx.enter_context(nc.Block())

        def steps(eng, step):
            step(0, 0, True, False)
            with eng.Fori(0, (STEPS1 - 2) // 2) as i:
                step(2 * i + 1, 1, False, False)
                step(2 * i + 2, 0, False, False)
            step(STEPS1 - 1, 1, False, True)

        def units_of(first, last):
            return NEXT1 if first else FINISH1 if last else FULL1

        def at_unit(first, last, kind, j):
            return [u[0] == kind and u[2] == j for u in units_of(first, last)].index(True)

        def even_of(first, par):
            return (len(START1) + (0 if first else len(NEXT1) + (1 + par) * len(FULL1))) % 2

        @block.sync
        def _(sp):
            v_steps = m.v_all[:, :, :, :, :, :].rearrange("p b q t g d -> p (b q t g) d")

            def load_weights(k):
                sp.dma_start(wk[:, :], m.wk_all[:, k % QUADS, :]).then_inc(w_loaded, 16)
                sp.dma_start(wq[:, :], m.wq_all[:, k % QUADS, :]).then_inc(w_loaded, 16)

            def load_values(k, par):
                sp.dma_start(val[par][:, :, :, 0:2 * D1].rearrange("p t g d -> p (t g) d"),
                             v_steps[:, ds(TT * 4 * k, TT * 4), :]
                             ).then_inc(val_loaded[par], 16)

            def load_rows(k, par, j):
                load_heads(par, j)
                load_rope(k, par, j)

            def load_heads(par, j):
                half = ts(j, BLK)
                for dst, src, loaded in ((kk, head[0], k_loaded), (qq, head[1], q_loaded)):
                    for h in R4:
                        sp.dma_start(dst[par][HEAD:P, h, half].bitcast(F32),
                                     src[32 * h:32 * (h + 1), half].bitcast(F32)).then_inc(loaded[par][j], 16)

            def load_rope(k, par, j):
                sp.dma_start(qq[par][0:HEAD, :, ts(j, BLK)].bitcast(F32),
                             m.qr[0:HEAD, ds(T * (k // QUADS % B) + BLK * j, BLK)].unsqueeze(1)
                             .to_broadcast([HEAD, 4, BLK]).bitcast(F32)).then_inc(rope_loaded[par][j], 16)

            def max_rows(par, units, base):
                seen = 0
                for kind, g, j in units:
                    if kind == "m":
                        sp.wait_ge(read, base + seen + 1)
                        sp.dma_start(qq[par][ROW:ROW + 1, g, :].bitcast(F32), mrow[g][:, :].bitcast(F32)
                                     ).then_inc(row_loaded[g], 16)
                    seen += 1

            load_weights(0)
            load_rope(0, 0, 0)
            load_rope(0, 0, 1)
            sp.wait_ge(read, len(PROJ1) // 2)
            load_heads(0, 0)
            sp.wait_ge(read, len(PROJ1))
            load_heads(0, 1)
            load_weights(1)
            sp.wait_ge(read, START1.index(("m", 0, 0)) - len(LATE) - 2)
            load_weights(2)
            load_rows(1, 1, 0)
            sp.wait_ge(cleared, 2)
            load_values(0, 0)
            max_rows(0, START1, 0)

            def step(n, par, first, last):
                if not last:
                    base, units = units_before1(n), units_of(first, last)
                    if not first:
                        sp.wait_ge(pv_done, TT * n)
                    load_rows(n + 1, 1 - par, 1)
                    load_values(n + 1, 1 - par)
                    sp.wait_ge(read, base + units.index(("q", 0, 1)) + 1)
                    sp.wait_ge(st_filled, 4 * (TT * n + TPB))
                    load_rows(n + 2, par, 0)
                    load_weights(n + 3)
                    max_rows(1 - par, units, base)

            steps(sp, step)
            sp.wait_ge(w_loaded, 32 * (STEPS1 + 2))
            sp.wait_ge(rope_loaded[0][0], 16 * (STEPS1 // 2 + 1))
            sp.wait_ge(k_loaded[0][0], 64 * (STEPS1 // 2 + 1))
            sp.wait_ge(q_loaded[0][0], 64 * (STEPS1 // 2 + 1))

        @block.scalar
        def _(act):
            def run(n, par, todo, base, even, first, units, work=work):
                seen = 0
                for what, kind, *rest in todo:
                    if what == "UNIT":
                        j = rest[1]
                        if kind in "kq":
                            act.wait_ge(filled, base + seen + 1)
                            back = before_last_projection(units, seen)
                            if back is not None:
                                act.wait_ge(read, base + back + 1)
                            elif not (isinstance(base, int) and base == 0):
                                act.wait_ge(read, base)
                            b = kind == "q"
                            buf = work[(even + seen) % len(work)]
                            c = 6 + 2 * (kind == "q")
                            one = m.coef[:, 10:11] if kind == "k" else m.coef[:, 11:12]
                            nc.scalar.activation(low[b][:, :], buf[:, :], ACT.Identity, scale=m.coef[:, c:c + 1], bias=one)
                            nc.scalar.copy(hi[b][:, :], buf[:, :]).then_inc(halves, 1)
                        seen += 1
                    elif what == "ST":
                        kt, g = kind, rest[0]
                        act.wait_ge(st_filled, 4 * (TT * n + kt) + g + 1)
                        if not (first and kt < 2):
                            act.wait_ge(pv_done, TT * n + kt - 1)
                        nc.scalar.activation(prob[kt % 2][:, g, P * kt:T], st[g % 2][:, P * kt:T], ACT.Exp,
                                             scale=SCALE1).then_inc(exp_done, 1)

            for g in R4:
                nc.scalar.copy(kk[0][0:HEAD, g, 0:BLK], m.kr[0:HEAD, 0:BLK].bitcast(F32)).then_inc(rope_copied, 1)
            run(-1, 1, [("UNIT",) + u for u in START1], 0, 0, True, START1, start_work)

            def step(n, par, first, last):
                units = units_of(first, last)
                run(n, par, script1(units), units_before1(n), even_of(first, par), first, units)
                act.wait_ge(pv_done, TT * (n + 1))
                if not first:
                    act.wait_ge(read, units_before1(n) + at_unit(first, last, "t", 1) + 1)
                nc.scalar.copy(ut[:, :], pv[:, :]).then_inc(ut_ready, 1)

            steps(act, step)

        @block.gpsimd
        def _(pool):
            nc.gpsimd.memset(mx[:, :, :, :], -3e38).then_inc(cleared, 1)

            pool.wait_ge(rope_copied, 4)

            def copy_rope(k, par, j):
                for g in R4:
                    nc.gpsimd.tensor_copy(kk[par][0:HEAD, g, ts(j, BLK)],
                                          m.kr[0:HEAD, ds(T * (k // QUADS % B) + BLK * j, BLK)].bitcast(F32)
                                          ).then_inc(rope_copied, 1)

            copy_rope(0, 0, 1)
            for a in R2:
                ins = nc.gpsimd.memset(val[a][:, :, :, 2 * D1:], 0.0)
            ins.then_inc(cleared, 1)
            copy_rope(1, 1, 0)

            def step(n, par, first, last):
                if not last:
                    if not first:
                        pool.wait_ge(st_filled, 4 * TT * n)
                    copy_rope(n + 1, 1 - par, 1)
                    pool.wait_ge(st_filled, 4 * (TT * n + TPB))
                    copy_rope(n + 2, par, 0)

            steps(pool, step)

        @block.vector
        def _(v):
            def combine(g, k, u_last):
                v.wait_ge(read, u_last + 1)
                nc.vector.tensor_tensor(mmax[:, g, :], mx[:, g, :, 0], mx[:, g, :, 1], ALU.max).then_inc(mmax_ready, 1)
                v.wait_ge(mmax_ready, 4 * k + g + 1)
                nc.vector.tensor_scalar(negm[:, g, :], mmax[:, g, :], -1.0, None, ALU.mult).then_inc(negm_ready, 1)

            def run(n, par, units, base, even, work=work):
                seen = 0
                for kind, g, j in units:
                    u, buf = base + seen, work[(even + seen) % len(work)]
                    if kind in "kq":
                        k = n + quads_ahead(units, seen)
                        c, b = 6 + 2 * (kind == "q"), kind == "q"
                        v.wait_ge(halves, 4 * k + 2 * j + (kind == "q") + 1)
                        if not (isinstance(k, int) and k == 0):
                            loaded = (k_loaded if kind == "k" else q_loaded)[1 - par]
                            v.wait_ge(loaded[j], 64 * ((k - 1) // 2 + 1))
                        nc.vector.scalar_tensor_tensor(head[kind == "q"][:, ts(j, BLK)], hi[b][:, :].bitcast(F32),
                                                       m.coef[:, c + 1:c + 2], low[b][:, :], ALU.mult, ALU.add
                                                       ).then_inc(read, 1)
                    elif kind == "s":
                        t, key, width, diagonal = PIECES[j]
                        v.wait_ge(filled, u + 1)
                        nc.vector.reduce_max(mx[:, g, t, (key > 0):(key > 0) + 1], buf[:, 0:width], AX.X
                                             ).then_inc(read, 1)
                        if j == len(PIECES) - 1:
                            combine(g, n + 1, u)
                    elif kind == "m":
                        k = n + 1
                        if not (isinstance(k, int) and k == 0):
                            v.wait_ge(row_loaded[g], 16 * k)
                        v.wait_ge(filled, u + 1)
                        nc.vector.tensor_copy(mrow[g][:, :], buf[0:TT, 0:P]).then_inc(read, 1)
                    else:
                        k = n - 1
                        v.wait_ge(filled, u + 1)
                        parts = buf[:, :].rearrange("p (t g c) -> p t g c", t=TPB, g=4)
                        nc.vector.reciprocal(rs[:, j, :, :], parts[:, :, :, D1]).then_inc(rs_ready, 1)
                        v.wait_ge(rs_ready, 2 * k + j + 1)
                        nc.vector.tensor_tensor(m.attn[:, ds(TT * (k // QUADS) + TPB * j, TPB), k % QUADS, :, :],
                                                parts[:, :, :, 0:D1],
                                                rs[:, j, :, :].unsqueeze(3).to_broadcast([P, TPB, 4, D1]),
                                                ALU.mult).then_inc(read, 1)
                    seen += 1

            v.wait_ge(cleared, 1)
            run(-1, 1, START1, 0, 0, start_work)

            def step(n, par, first, last):
                run(n, par, units_of(first, last), units_before1(n), even_of(first, par))

            steps(v, step)
            run(STEPS1, 0, FINISH1, units_before1(STEPS1 - 1) + 2, even_of(False, 1))

        @block.tensor
        def _(pe):
            def unit(kind, g, j, u, buf, par, k, turns):
                if not (isinstance(u, int) and u < turns):
                    pe.wait_ge(read, u - turns + 1)
                if kind in "kq":
                    w, src = (wk, m.ck_all) if kind == "k" else (wq, m.xt_all)
                    if kind == "k" and j == 0:
                        pe.wait_ge(w_loaded, 32 * (k + 1))
                    ins = nc.tensor.matmul(buf[:, :], w[:, :], src[:, ds(T * (k // QUADS % B) + BLK * j, BLK)],
                                           start=True, stop=True)
                elif kind == "s":
                    half = PIECES[j][0] >= TPB
                    if j in (EARLY[0], LATE[0]):
                        pe.wait_ge(rope_copied, 8 * k + 4 * half + g + 1)
                        if g == 0:
                            pe.wait_ge(rope_loaded[par][half], 16 * (k // 2 + 1))
                            pe.wait_ge(k_loaded[par][half], 64 * (k // 2 + 1))
                            pe.wait_ge(q_loaded[par][half], 64 * (k // 2 + 1))
                    t, key, width, diagonal = PIECES[j]
                    ins = nc.tensor.matmul(buf[:, 0:width], qq[par][:, g, ts(t, P)], kk[par][:, g, key:key + width],
                                           start=True, stop=not diagonal)
                    if diagonal:
                        ins = nc.tensor.matmul(buf[:, width - P:width], m.identr[:, :], m.maskr[:, 0, :],
                                               start=False, stop=True)
                elif kind == "m":
                    pe.wait_ge(negm_ready, 4 * k + g + 1)
                    ins = nc.tensor.matmul(buf[0:TT, 0:P], negm[:, g, :], m.ident[:, :], start=True, stop=True)
                else:
                    pe.wait_ge(ut_ready, k + 1)
                    for t in range(TPB):
                        ins = nc.tensor.transpose(buf[:, ts(t, P)], ut[:, ts(TPB * j + t, P)], m.ident[:, :])
                ins.then_inc(filled, 1)

            def run(n, par, todo, base, even, first, units, work=work):
                seen = 0
                for what, *rest in todo:
                    if what == "UNIT":
                        kind, g, j = rest
                        k = n - 1 if kind == "t" else n + quads_ahead(units, seen)
                        unit(kind, g, j, base + seen, work[(even + seen) % len(work)], 1 - par, k, len(work))
                        seen += 1
                    elif what == "ST":
                        kt, g = rest
                        at = 4 * (TT * n + kt) + g
                        if not (first and kt == 0 and g < 2):
                            pe.wait_ge(exp_done, at - 1)
                        if kt == 0:
                            pe.wait_ge(row_loaded[g], 16 * (n + 1))
                        buf = st[g % 2]
                        pieces = q_pieces(kt)
                        for n_piece, (lo, hi_) in enumerate(pieces):
                            ins = nc.tensor.matmul(buf[:, lo:hi_], kk[par][:, g, ts(kt, P)], qq[par][:, g, lo:hi_],
                                                   start=True, stop=(n_piece > 0))
                            if n_piece == 0:
                                ins = nc.tensor.matmul(buf[:, lo:lo + P], m.identr[:, :], m.maskr[:, 1, :],
                                                       start=False, stop=True)
                        ins.then_inc(st_filled, 1)
                    else:
                        kt, piece = rest
                        if piece == 0:
                            pe.wait_ge(exp_done, 4 * (TT * n + kt + 1))
                        if kt == 0 and piece == 0:
                            pe.wait_ge(val_loaded[par], 16 * (n // 2 + 1))
                            if not first:
                                pe.wait_ge(ut_ready, n)
                        lo, hi_ = q_pieces(kt)[piece]
                        for g in R4:
                            ins = nc.tensor.matmul(pv[32 * g:32 * (g + 1), lo:hi_], val[par][:, kt, g, :],
                                                   prob[kt % 2][:, g, lo:hi_], start=(kt == 0),
                                                   stop=(kt == TT - 1 or (kt == 3 and lo < BLK)))
                        if piece == len(q_pieces(kt)) - 1:
                            ins.then_inc(pv_done, 1)

            run(-1, 1, [("UNIT",) + u for u in START1], 0, 0, True, START1, start_work)
            pe.wait_ge(read, len(START1))

            def step(n, par, first, last):
                units = units_of(first, last)
                run(n, par, script1(units), units_before1(n), even_of(first, par), first, units)

            steps(pe, step)
            run(STEPS1, 0, [("UNIT",) + u for u in FINISH1], units_before1(STEPS1 - 1) + 2, even_of(False, 1), False,
                FINISH1)


def l1_output(nc, m, d):
    with ExitStack() as ctx:
        wo = ctx.enter_context(nc.sbuf_tensor("wo", [P, E], F32))
        at = [ctx.enter_context(nc.sbuf_tensor(f"at{i}", [P, BLK], F32)) for i in range(2)]
        tr = [ctx.enter_context(nc.psum_tensor(f"tr_o{i}", [P, BLK], F32)) for i in range(2)]
        out = [ctx.enter_context(nc.psum_tensor(f"out_o{i}", [P, TPB, E], F32)) for i in range(2)]

        def sem(name):
            return m.ctx.enter_context(nc.semaphore(name))
        loaded, transposed, at_ready, out_filled, added = (sem("wo_loaded"), sem("tr_o"), sem("at_ready"),
                                                           sem("out_filled"), sem("added_o"))
        block = ctx.enter_context(nc.Block())

        @block.sync
        def _(sp):
            sp.dma_start(wo[:, :], d["wo"]).then_inc(loaded, 16)

        @block.tensor
        def _(pe):
            pe.wait_ge(loaded, 16)
            for j in range(NBLK):
                if j >= 2:
                    pe.wait_ge(at_ready, j - 1)
                for t in range(TPB):
                    src = m.attn[:, TPB * j + t, :, :, :].rearrange("p a b c -> p (a b c)")
                    ins = nc.tensor.transpose(tr[j % 2][:, ts(t, P)], src, m.ident[:, :])
                ins.then_inc(transposed, 1)
                pe.wait_ge(at_ready, j + 1)
                if j >= 2:
                    pe.wait_ge(added, j - 1)
                for t in range(TPB):
                    ins = nc.tensor.matmul(out[j % 2][:, t, :], at[j % 2][:, ts(t, P)], wo[:, :], start=True, stop=True)
                ins.then_inc(out_filled, 1)

        @block.scalar
        def _(act):
            for j in range(NBLK):
                act.wait_ge(transposed, j + 1)
                if j >= 2:
                    act.wait_ge(out_filled, j - 1)
                nc.scalar.copy(at[j % 2][:, :], tr[j % 2][:, :]).then_inc(at_ready, 1)

        @block.vector
        def _(v):
            for j in range(NBLK):
                v.wait_ge(out_filled, j + 1)
                xs = m.x[:, TPB * j:TPB * (j + 1), :]
                nc.vector.tensor_tensor(xs, out[j % 2][:, :, :], xs, ALU.add).then_inc(added, 1)


def experts1(nc, m, d):
    with ExitStack() as ctx:
        def sb(name, shape, dt=F32):
            return ctx.enter_context(nc.sbuf_tensor(name, shape, dt))

        def pb(name, shape):
            return ctx.enter_context(nc.psum_tensor(name, shape, F32))

        def sem(name):
            return m.ctx.enter_context(nc.semaphore(name))

        UNITS = (NEXP + 1) * CH
        R = 5
        s = [sb(f"silu1_{i}", [P, BLK]) for i in range(R)]
        lead = [sb(f"silu1_lead{i}", [P, BLK], F32R) for i in range(R)]
        rest = [sb(f"silu1_rest{i}", [P, BLK], F32R) for i in range(R)]
        ob = sb("ob1", [P, BLK])
        hp = [pb(f"hid1_{i}", [P, BLK]) for i in range(R)]
        out = pb("out1", [P, BLK])
        tr = pb("tr_e1", [P, TPB, P])
        up_done, silu_done, gated, down_done = sem("up_done1"), sem("silu_done1"), sem("gated1"), sem("down_done1")
        lead_done, rest_done = sem("lead_done1"), [sem("rest_done_even"), sem("rest_done_odd")]
        ob_ready, transposed, added, stored = sem("ob_ready1"), sem("tr_done1"), sem("added1"), sem("stored")
        block = ctx.enter_context(nc.Block())

        def rests_before(j, u):
            return UNITS // 2 * j + u // 2 + 1

        def rest_of(eng, engine, j, u):
            eng.wait_ge(lead_done, UNITS * j + u + 1)
            engine.tensor_tensor(rest[u % R][:, :], s[u % R][:, :], lead[u % R][:, :], ALU.subtract
                                 ).then_inc(rest_done[u % 2], 1)

        @block.tensor
        def _(pe):
            with pe.Fori(0, NBLK) as j:
                cols = ds(BLK * j, BLK)

                def down(u):
                    pe.wait_ge(rest_done[u % 2], rests_before(j, u))
                    split_product(nc, out[:, :], m.w2_lead[:, u, :], m.w2_rest[:, u, :],
                                  lead[u % R][:, :], rest[u % R][:, :], u == 0, u == UNITS - 1).then_inc(down_done, 1)

                for u in range(UNITS):
                    if u >= R:
                        pe.wait_ge(silu_done, UNITS * j + u - R + 1)
                    split_product(nc, hp[u % R][:, :], m.w1_lead[:, u, :], m.w1_rest[:, u, :],
                                  m.xt_lead[:, cols], m.xt_rest[:, cols], True, True).then_inc(up_done, 1)
                    if u >= R - 1:
                        down(u - R + 1)
                nc.tensor.matmul(out[:, :], m.b2[0:NEXP + 1, :], m.gate_t[0:NEXP + 1, cols], start=False, stop=False)
                for u in range(UNITS - R + 1, UNITS):
                    down(u)
                pe.wait_ge(ob_ready, j + 1)
                for t in range(TPB):
                    ins = nc.tensor.transpose(tr[:, t, :], ob[:, ts(t, P)], m.ident[:, :])
                ins.then_inc(transposed, 1)

        @block.scalar
        def _(act):
            with act.Fori(0, NBLK) as j:
                def leading(u):
                    if u < NEXP * CH:
                        act.wait_ge(gated, NEXP * CH * j + u + 1)
                    else:
                        act.wait_ge(silu_done, UNITS * j + u + 1)
                    if u >= R:
                        act.wait_ge(down_done, UNITS * j + u - R + 1)
                    nc.scalar.copy(lead[u % R][:, :], s[u % R][:, :]).then_inc(lead_done, 1)

                for u in range(UNITS):
                    act.wait_ge(up_done, UNITS * j + u + 1)
                    if u >= R:
                        act.wait_ge(rest_done[(u - R) % 2], rests_before(j, u - R))
                    nc.scalar.activation(s[u % R][:, :], hp[u % R][:, :], ACT.Silu, bias=m.b1[:, u:u + 1]
                                         ).then_inc(silu_done, 1)
                    if u:
                        leading(u - 1)
                leading(UNITS - 1)
                act.wait_ge(down_done, UNITS * (j + 1))
                nc.scalar.copy(ob[:, :], out[:, :]).then_inc(ob_ready, 1)

        @block.gpsimd
        def _(pool):
            with pool.Fori(0, NBLK) as j:
                for u in range(0, UNITS, 2):
                    rest_of(pool, nc.gpsimd, j, u)

        @block.vector
        def _(v):
            with v.Fori(0, NBLK) as j:
                v.wait_ge(m.spread, 16 * (j + 1))
                for u in range(NEXP * CH):
                    v.wait_ge(silu_done, UNITS * j + u + 1)
                    nc.vector.tensor_tensor(s[u % R][:, :], s[u % R][:, :], m.gb[:, j % 2, u // CH, :],
                                            ALU.mult).then_inc(gated, 1)
                    if u % 2 == 0 and u:
                        rest_of(v, nc.vector, j, u - 1)
                for u in range(NEXP * CH - 1, UNITS, 2):
                    rest_of(v, nc.vector, j, u)
                v.wait_ge(transposed, j + 1)
                xs = m.x[:, ds(TPB * j, TPB), :]
                nc.vector.tensor_tensor(xs, tr[:, :, :], xs, ALU.add).then_inc(added, 1)

        @block.sync
        def _(sp):
            spread_later_gates(sp, m, d["gates1"], added)
            with sp.Fori(0, NBLK) as j:
                sp.wait_ge(added, j + 1)
                sp.dma_start(d["out"][ds(BLK * j, BLK), :].rearrange("(t p) e -> p t e", p=P),
                             m.x[:, ds(TPB * j, TPB), :]).then_inc(stored, 16)
            sp.wait_ge(stored, 16 * NBLK)


def build(nc, d):
    with ExitStack() as ctx:
        m = Mem()
        m.ctx = ctx

        def sb(name, shape, dt=F32):
            return ctx.enter_context(nc.sbuf_tensor(name, shape, dt))

        m.x = sb("x", [P, NT, E])
        m.ident = sb("ident", [P, P])
        m.eps = sb("eps", [P, 1])

        with ExitStack() as layer:
            def sl(name, shape, dt=F32):
                return layer.enter_context(nc.sbuf_tensor(name, shape, dt))

            m.aq = sl("aq", [P, N], F32R)
            m.ak = sl("ak", [P, N], F32R)
            m.w_all = sl("w_all", [P, H0, 4, D0], F32R)
            m.c_all = sl("c_all", [P, NT, D0])
            m.g_all = sl("g_all", [P, PAIRS, E])
            m.out_bias = sl("out_bias", [P, 1])
            m.out_t = sl("out_t", [P, N])
            m.qk_bias = sl("qk_bias", [P, 4 * PAIRS])
            l0_prologue(nc, m, d)
            l0_attention(nc, m, d)
            residual_out(nc, m, d)

        with ExitStack() as layer:
            def sl(name, shape, dt=F32):
                return layer.enter_context(nc.sbuf_tensor(name, shape, dt))

            m.xt_all = sl("xt_all0", [P, N])
            m.xt_lead, m.xt_rest = (sl(f"xt_{n}0", [P, N], F32R) for n in ("lead", "rest"))
            m.gb = sl("gb0", [P, 2, NEXP, BLK])
            m.gate_t = sl("gate_t0", [P, N])
            m.up_lead, m.up_rest = (sl(f"up_{n}", [P, NEXP, 2 * P], F32R) for n in ("lead", "rest"))
            m.down_lead, m.down_rest = (sl(f"down_{n}", [P, NEXP, E], F32R) for n in ("lead", "rest"))
            m.split = ((d["up"], m.up_lead, m.up_rest), (d["down"], m.down_lead, m.down_rest))
            m.load_biases = m.await_biases = lambda sp: None
            router(nc, m, d, 0, d["router"], None, None, None)
            experts0(nc, m, d)

        with ExitStack() as layer:
            def sl(name, shape, dt=F32):
                return layer.enter_context(nc.sbuf_tensor(name, shape, dt))

            m.xt_all = sl("xt_all1", [P, N])
            m.ck_all = sl("ck_all", [P, N])
            m.v_all = sl("v_all", [P, B, QUADS, TT, 4, 2 * D1])
            m.kr = sl("kr", [P, N], F32R)
            m.qr = sl("qr", [P, N], F32R)
            m.attn = sl("attn", [P, NT, QUADS, 4, D1])
            m.identr = sl("identr", [P, P], F32R)
            m.maskr = sl("maskr", [P, 2, P], F32R)
            m.coef = sl("coef", [P, 12])
            m.wk_all = sl("wk_all", [P, QUADS, P])
            m.wq_all = sl("wq_all", [P, QUADS, P])
            l1_prologue(nc, m, d)
            l1_attention(nc, m, d)
            l1_output(nc, m, d)

        with ExitStack() as layer:
            def sl(name, shape, dt=F32):
                return layer.enter_context(nc.sbuf_tensor(name, shape, dt))

            m.xt_all = sl("xt_all2", [P, N])
            m.xt_lead, m.xt_rest = (sl(f"xt_{n}1", [P, N], F32R) for n in ("lead", "rest"))
            m.gb = sl("gb1", [P, 2, NEXP, BLK])
            m.gate_t = sl("gate_t1", [P, N])
            m.w1_lead, m.w1_rest = (sl(f"up1_{n}", [P, (NEXP + 1) * CH, P], F32R) for n in ("lead", "rest"))
            m.w2_lead, m.w2_rest = (sl(f"down1_{n}", [P, (NEXP + 1) * CH, E], F32R) for n in ("lead", "rest"))
            m.split = ((d["w1"], m.w1_lead, m.w1_rest), (d["w2"], m.w2_lead, m.w2_rest))
            m.b1 = sl("bias_up1", [P, (NEXP + 1) * CH])
            m.b2 = sl("bias_down1", [NEXP + 1, E])
            loaded = ctx.enter_context(nc.semaphore("biases1_loaded"))

            def load_biases(sp):
                for dst, src in ((m.b1, d["b1"]), (m.b2, d["b2"])):
                    sp.dma_start(dst[:, :], src).then_inc(loaded, 16)

            def await_biases(sp):
                sp.wait_ge(loaded, 32)

            m.load_biases, m.await_biases = load_biases, await_biases
            router(nc, m, d, 1, d["wr2"], d["wr1"], d["br1"], d["br2"])
            experts1(nc, m, d)


def kernel(**inputs):
    import numpy as _np
    import concourse.bacc as _bacc
    from concourse import mybir as _mybir
    from concourse.bass_utils import run_bass_kernel_spmd as _run

    i = {k: _np.asarray(v) for k, v in inputs.items()}
    h, dk = 16, 64

    def twice(a):
        return _np.concatenate([a, a], axis=0)

    def qk_columns():
        q = i["L0_attn_fcq_b"].reshape(h, dk)
        k = i["L0_attn_fck_b"].reshape(h, dk)
        return twice(_np.stack([q, k], axis=1).reshape(2 * h, dk).T)

    def head_columns(w):
        w = w.reshape(128, 16, 8)
        return _np.concatenate([w, w, w, _np.zeros_like(w)], axis=2).reshape(128, 4, 128)

    def rotary_columns(w):
        swapped = _np.concatenate([w[:, 16:], w[:, :16]], axis=1)
        return [_np.tile(w, (1, 4)), _np.tile(swapped, (1, 4))]

    def rotary_tables():
        inv = (1.0 / _np.power(_np.float32(10000.0), _np.arange(0, 32, 2, dtype=_np.float32) / _np.float32(32))
               ).astype(_np.float32)
        angle = _np.outer(_np.arange(1024, dtype=_np.float32), inv).astype(_np.float32).T
        cos, sin = _np.cos(angle), _np.sin(angle)
        return _np.stack([_np.tile(_np.concatenate([cos, cos]), (4, 1)),
                          _np.tile(_np.concatenate([-sin, sin]), (4, 1))], axis=1).astype(_np.float32)

    def part_columns():
        c = _np.zeros((128, 12), _np.float32)
        row = _np.arange(128)
        for at, rest in ((2, row // 32 == 1), (4, row // 32 == 2),
                         (6, row % 32 // 8 == 1), (8, row % 32 // 8 == 2)):
            c[:, at] = rest
            c[:, at + 1] = _np.where(rest, -1.0, 1.0)
        c[:, 10] = row % 32 == 24
        return c

    def masks():
        later = _np.triu(_np.ones((128, 128), _np.float32), 1)
        return _np.stack([later, later.T], axis=1) * _np.float32(MASKED)

    wq, wk, wv = i["L0_attn_wq"], i["L0_attn_wk"], i["L0_attn_wv"]
    w1 = _np.concatenate([i["L1_ffn_We1"], i["L1_ffn_Ws1"][None]])
    w2 = _np.concatenate([i["L1_ffn_We2"], i["L1_ffn_Ws2"][None]])
    b1 = _np.concatenate([i["L1_ffn_be1"], i["L1_ffn_bs1"][None]])
    arrays = {
        "x": i["L0_attn_z"].reshape(2048, 128),
        "ident": _np.eye(128, dtype=_np.float32),
        "wl": _np.concatenate([wq, wq, wk, wk, wv], axis=1),
        "fq": twice(i["L0_attn_fcq_w"]).reshape(128, h, dk),
        "fk": twice(i["L0_attn_fck_w"]).reshape(128, h, dk),
        "fv_t": i["L0_attn_fcv_w"].reshape(dk, h, dk).transpose(2, 1, 0),
        "fo": i["L0_attn_fco_w"].reshape(h, dk, 128).transpose(1, 0, 2),
        "bv": i["L0_attn_fcv_b"].reshape(h, dk).T,
        "bo": i["L0_attn_fco_b"].reshape(128, 1),
        "qk_bias": qk_columns(),
        "router": i["L0_ffn_router_w"].T,
        "iota": _np.tile(_np.arange(8, dtype=_np.float32), (128, 1)),
        "up": i["L0_ffn_up_proj"].transpose(1, 0, 2),
        "down": i["L0_ffn_down_proj"].transpose(1, 0, 2),
        "wkv": i["L1_attn_W_kv_down"],
        "wv1": i["L1_attn_W_v_up"],
        "wrope": _np.stack(rotary_columns(i["L1_attn_W_k_rope"]) + rotary_columns(i["L1_attn_W_q_rope"]), axis=1),
        "cs": rotary_tables(),
        "masks": masks(),
        "coef": part_columns(),
        "wk1": head_columns(i["L1_attn_W_k_up"]),
        "wq1": head_columns(i["L1_attn_W_q"]),
        "wo": i["L1_attn_W_o"],
        "wr1": i["L1_ffn_Wr1"],
        "br1": i["L1_ffn_br1"].reshape(32, 1),
        "wr2": i["L1_ffn_Wr2"],
        "br2": _np.tile(i["L1_ffn_br2"], (128, 1)),
        "w1": w1.transpose(1, 0, 2).reshape(128, 36, 128),
        "w2": w2.reshape(36, 128, 128).transpose(1, 0, 2),
        "b1": b1.reshape(36, 128).T,
        "b2": _np.concatenate([i["L1_ffn_be2"], i["L1_ffn_bs2"][None]]),
    }
    nc = _bacc.Bacc("TRN2", target_bir_lowering=False, num_devices=1)
    ins, feed = {}, {}
    for name, a in arrays.items():
        a = _np.ascontiguousarray(a)
        feed["in_" + name] = a
        ins[name] = nc.dram_tensor("in_" + name, a.shape, _mybir.dt.float32, kind="ExternalInput").ap()
    ins["sums"] = nc.dram_tensor("scratch_sums", (4, 512), _mybir.dt.float32, kind="Internal").ap()
    for n in range(2):
        ins[f"gates{n}"] = nc.dram_tensor(f"scratch_gates{n}", (8, 2048), _mybir.dt.float32, kind="Internal").ap()
    ins["out"] = nc.dram_tensor("out_x", (2048, 128), _mybir.dt.float32, kind="ExternalOutput").ap()
    build(nc, ins)
    r = _run(nc, [feed], core_ids=[0])
    return r.results[0]["out_x"].reshape(2, 1024, 128)
```
